# Optimizing a Trainium2 kernel written in Bass

```python
import numpy as np
import jax
import jax.numpy as jnp

def _softmax(x, axis=-1):
    return jax.nn.softmax(x, axis=axis)

def _gelu(x):
    return jax.nn.gelu(x, approximate=True)

def _silu(x):
    return jax.nn.silu(x)

def _sigmoid(x):
    return jax.nn.sigmoid(x)

def _layernorm(x, axis=-1, eps=1e-05):
    m = jnp.mean(x, axis=axis, keepdims=True)
    v = jnp.var(x, axis=axis, keepdims=True)
    return (x - m) / jnp.sqrt(v + eps)

def _scatter_add(tgt, idx, src, axis=0):
    return tgt.at[idx].add(src)

def _segment_sum(src, seg, n):
    return jax.ops.segment_sum(src, seg, n)
kernel_name = 'mk_adaln_d1_jaxref_r8_2bd802'

def setup_inputs(seed: int=0):
    np.random.seed(seed)
    _w = jnp.asarray

    def _L0_attn_setup():
        import jax, jax.numpy as jnp
        import numpy as np
        NUM_HEADS = 16
        LN_EPS = 1e-05
        FEAT_EPS = 0.0001
        key = jax.random.key(seed)
        ks = jax.random.split(key, 4)
        B, L, D = (2, 256, 128)
        scale = 0.02
        return {'x': jax.random.normal(ks[0], (B, L, D), dtype=jnp.float32), 'Wqkv': jax.random.normal(ks[1], (3 * D, D), dtype=jnp.float32) * scale, 'bqkv': jnp.zeros((3 * D,), dtype=jnp.float32), 'Wout': jax.random.normal(ks[2], (D, D), dtype=jnp.float32) * scale, 'bout': jnp.zeros((D,), dtype=jnp.float32), 'gamma': jnp.ones((D,), dtype=jnp.float32), 'beta': jnp.zeros((D,), dtype=jnp.float32)}
    _L0_attn_in = _L0_attn_setup()

    def _L0_ffn_setup():
        import jax, jax.numpy as jnp
        import numpy as np
        B, N, D, H, E = (4, 128, 128, 16, 8)
        DK = D // H
        HID = 4 * D
        EPS = 1e-05

        def _layernorm(x, w, b):
            m = jnp.mean(x, axis=-1, keepdims=True)
            v = jnp.mean(jnp.square(x - m), axis=-1, keepdims=True)
            return (x - m) * jax.lax.rsqrt(v + EPS) * w + b

        def _msa(x, w_qkv, w_proj):
            b, n, d = x.shape
            qkv = (x @ w_qkv).reshape(b, n, 3, H, DK)
            q = qkv[:, :, 0].transpose(0, 2, 1, 3)
            k = qkv[:, :, 1].transpose(0, 2, 1, 3)
            v = qkv[:, :, 2].transpose(0, 2, 1, 3)
            attn = jnp.einsum('bhnd,bhmd->bhnm', q, k) * (1.0 / np.sqrt(DK))
            attn = jax.nn.softmax(attn, axis=-1)
            y = jnp.einsum('bhnm,bhmd->bhnd', attn, v)
            y = y.transpose(0, 2, 1, 3).reshape(b, n, d)
            return y @ w_proj

        def _moe_mlp(x, gate_w, gate_b, w1, w2):
            b, n, d = x.shape
            xf = x.reshape(b * n, d)
            logits = xf @ gate_w + gate_b
            one_hot = jax.nn.one_hot(jnp.argmax(logits, axis=-1), E, dtype=xf.dtype)
            h = jax.nn.gelu(jnp.einsum('td,edh->teh', xf, w1), approximate=True)
            y = jnp.einsum('teh,ehd->ted', h, w2)
            out = jnp.einsum('te,ted->td', one_hot, y)
            return out.reshape(b, n, d)
        key = jax.random.key(seed)
        ks = jax.random.split(key, 8)
        s = 0.02
        return {'x': jax.random.normal(ks[0], (B, N, D), jnp.float32), 'ln1_w': jnp.ones((D,), jnp.float32), 'ln1_b': jnp.zeros((D,), jnp.float32), 'w_qkv': jax.random.normal(ks[1], (D, 3 * D), jnp.float32) * s, 'w_proj': jax.random.normal(ks[2], (D, D), jnp.float32) * s, 'ln2_w': jnp.ones((D,), jnp.float32), 'ln2_b': jnp.zeros((D,), jnp.float32), 'gate_w': jax.random.normal(ks[3], (D, E), jnp.float32) * s, 'gate_b': jnp.zeros((E,), jnp.float32), 'w1': jax.random.normal(ks[4], (E, D, HID), jnp.float32) * s, 'w2': jax.random.normal(ks[5], (E, HID, D), jnp.float32) * s}
    _L0_ffn_in = _L0_ffn_setup()
    _L0_c = _w((lambda *s: np.random.randn(*s).astype(np.float32) * 0.05)(8, 128))
    _L0_wmod = _w((lambda *s: np.random.randn(*s).astype(np.float32) * 0.05)(128, 6 * 128) * 128 ** (-0.5))
    _d = {'L0_attn_x': _L0_attn_in['x'], 'L0_attn_Wqkv': _L0_attn_in['Wqkv'], 'L0_attn_bqkv': _L0_attn_in['bqkv'], 'L0_attn_Wout': _L0_attn_in['Wout'], 'L0_attn_bout': _L0_attn_in['bout'], 'L0_attn_gamma': _L0_attn_in['gamma'], 'L0_attn_beta': _L0_attn_in['beta'], 'L0_ffn_ln1_w': _L0_ffn_in['ln1_w'], 'L0_ffn_ln1_b': _L0_ffn_in['ln1_b'], 'L0_ffn_w_qkv': _L0_ffn_in['w_qkv'], 'L0_ffn_w_proj': _L0_ffn_in['w_proj'], 'L0_ffn_ln2_w': _L0_ffn_in['ln2_w'], 'L0_ffn_ln2_b': _L0_ffn_in['ln2_b'], 'L0_ffn_gate_w': _L0_ffn_in['gate_w'], 'L0_ffn_gate_b': _L0_ffn_in['gate_b'], 'L0_ffn_w1': _L0_ffn_in['w1'], 'L0_ffn_w2': _L0_ffn_in['w2'], 'L0_c': _L0_c, 'L0_wmod': _L0_wmod}
    _x0 = _d['L0_attn_x']
    _d['L0_attn_x'] = jax.random.normal(jax.random.fold_in(jax.random.key(seed), 1), (8, 512, 128), dtype=_x0.dtype)
    del _x0
    return _d

def reference(L0_attn_x, L0_attn_Wqkv, L0_attn_bqkv, L0_attn_Wout, L0_attn_bout, L0_attn_gamma, L0_attn_beta, L0_ffn_ln1_w, L0_ffn_ln1_b, L0_ffn_w_qkv, L0_ffn_w_proj, L0_ffn_ln2_w, L0_ffn_ln2_b, L0_ffn_gate_w, L0_ffn_gate_b, L0_ffn_w1, L0_ffn_w2, L0_c, L0_wmod):

    def _L0_attn_ref(x, Wqkv, bqkv, Wout, bout, gamma, beta):
        import jax, jax.numpy as jnp
        import numpy as np
        NUM_HEADS = 16
        LN_EPS = 1e-05
        FEAT_EPS = 0.0001
        B, L, D = x.shape
        H = NUM_HEADS
        E = D // H
        qkv = x @ Wqkv.T + bqkv
        q, k, v = jnp.split(qkv, 3, axis=-1)
        q = q.reshape(B, L, H, E)
        k = k.reshape(B, L, H, E)
        v = v.reshape(B, L, H, E)
        q = (jax.nn.elu(q) + 1.0 + FEAT_EPS) / jnp.sqrt(jnp.asarray(E, q.dtype))
        k = jax.nn.elu(k) + 1.0 + FEAT_EPS
        kv = jnp.einsum('blhe,blhf->blhef', k, v)
        kv_cumsum = jnp.cumsum(kv, axis=1)
        k_cumsum = jnp.cumsum(k, axis=1)
        num = jnp.einsum('blhe,blhef->blhf', q, kv_cumsum)
        den = jnp.einsum('blhe,blhe->blh', q, k_cumsum)[..., None] + FEAT_EPS
        out = (num / den).reshape(B, L, D)
        out = out @ Wout.T + bout
        mu = jnp.mean(out, axis=-1, keepdims=True)
        var = jnp.var(out, axis=-1, keepdims=True)
        return (out - mu) / jnp.sqrt(var + LN_EPS) * gamma + beta

    def _L0_ffn_ref(x, ln1_w, ln1_b, w_qkv, w_proj, ln2_w, ln2_b, gate_w, gate_b, w1, w2):
        import jax, jax.numpy as jnp
        import numpy as np
        B, N, D, H, E = (4, 128, 128, 16, 8)
        DK = D // H
        HID = 4 * D
        EPS = 1e-05

        def _layernorm(x, w, b):
            m = jnp.mean(x, axis=-1, keepdims=True)
            v = jnp.mean(jnp.square(x - m), axis=-1, keepdims=True)
            return (x - m) * jax.lax.rsqrt(v + EPS) * w + b

        def _msa(x, w_qkv, w_proj):
            b, n, d = x.shape
            qkv = (x @ w_qkv).reshape(b, n, 3, H, DK)
            q = qkv[:, :, 0].transpose(0, 2, 1, 3)
            k = qkv[:, :, 1].transpose(0, 2, 1, 3)
            v = qkv[:, :, 2].transpose(0, 2, 1, 3)
            attn = jnp.einsum('bhnd,bhmd->bhnm', q, k) * (1.0 / np.sqrt(DK))
            attn = jax.nn.softmax(attn, axis=-1)
            y = jnp.einsum('bhnm,bhmd->bhnd', attn, v)
            y = y.transpose(0, 2, 1, 3).reshape(b, n, d)
            return y @ w_proj

        def _moe_mlp(x, gate_w, gate_b, w1, w2):
            b, n, d = x.shape
            xf = x.reshape(b * n, d)
            logits = xf @ gate_w + gate_b
            one_hot = jax.nn.one_hot(jnp.argmax(logits, axis=-1), E, dtype=xf.dtype)
            h = jax.nn.gelu(jnp.einsum('td,edh->teh', xf, w1), approximate=True)
            y = jnp.einsum('teh,ehd->ted', h, w2)
            out = jnp.einsum('te,ted->td', one_hot, y)
            return out.reshape(b, n, d)
        x = x + _msa(_layernorm(x, ln1_w, ln1_b), w_qkv, w_proj)
        x = x + _moe_mlp(_layernorm(x, ln2_w, ln2_b), gate_w, gate_b, w1, w2)
        return x
    x = L0_attn_x
    mod = (_silu(L0_c) @ L0_wmod).reshape(L0_c.shape[0], 6, 1, -1)
    sa, ca, ga, sb, cb, gb = (mod[:, 0], mod[:, 1], mod[:, 2], mod[:, 3], mod[:, 4], mod[:, 5])
    ga = (2 * (ga >= 0) - 1) * jnp.maximum(jnp.abs(ga), 0.25)
    gb = (2 * (gb >= 0) - 1) * jnp.maximum(jnp.abs(gb), 0.25)
    h = _layernorm(x, axis=-1) * (1 + ca) + sa
    x = x + ga * _L0_attn_ref(h, L0_attn_Wqkv, L0_attn_bqkv, L0_attn_Wout, L0_attn_bout, L0_attn_gamma, L0_attn_beta)
    h = _layernorm(x, axis=-1) * (1 + cb) + sb
    x = x + gb * _L0_ffn_ref(h, L0_ffn_ln1_w, L0_ffn_ln1_b, L0_ffn_w_qkv, L0_ffn_w_proj, L0_ffn_ln2_w, L0_ffn_ln2_b, L0_ffn_gate_w, L0_ffn_gate_b, L0_ffn_w1, L0_ffn_w2)
    return x

_drawn_inputs = setup_inputs


def setup_inputs(seed=0):
    import zlib

    import numpy as np

    out = dict(_drawn_inputs(seed))
    spreads = {'L0_attn_bqkv': (0.0, 0.1),
     'L0_attn_bout': (0.0, 0.1),
     'L0_attn_gamma': (1.0, 0.2),
     'L0_attn_beta': (0.0, 0.375),
     'L0_ffn_ln1_w': (1.0, 0.6),
     'L0_ffn_ln1_b': (0.0, 0.8),
     'L0_ffn_ln2_w': (1.0, 0.6),
     'L0_ffn_ln2_b': (0.0, 0.8),
     'L0_ffn_gate_b': (0.0, 0.691)}
    factors = {'L0_attn_Wqkv': 4.199,
     'L0_ffn_w_qkv': 8.0,
     'L0_ffn_w_proj': 8.0,
     'L0_ffn_gate_w': 4.675,
     'L0_ffn_w1': 4.294,
     'L0_ffn_w2': 4.208}
    for name, (base, spread) in spreads.items():
        noise = np.random.default_rng([zlib.crc32(name.encode()), seed]).standard_normal(out[name].shape)
        drawn = base * np.exp(spread * noise) if base else spread * noise
        out[name] = jnp.asarray(drawn.astype(out[name].dtype))
    for name, factor in factors.items():
        out[name] = (out[name] * factor).astype(out[name].dtype)
    return out
```

```python
import concourse.bass as bass
from concourse import mybir
from contextlib import ExitStack

F32 = mybir.dt.float32
BF16 = mybir.dt.bfloat16
I32 = mybir.dt.int32
U32 = mybir.dt.uint32
ALU = mybir.AluOpType
ACT = mybir.ActivationFunctionType
AX = mybir.AxisListType.X

P = 128
B = 8
L = 512
D = 128
H = 16
E = D // H
C = L // P
T = B * C
NE = 8
HID = 4 * D
HC = HID // P
MT = T + NE - 1
G = 4
GH = H // G
VW = 32
S = H // 2
KR = 6 * E
LN_EPS = 1e-5
FEAT_EPS = 1e-4
NM = 6
Q_PART = (0, 0, 1, 0, 2, 1)
K_PART = (0, 1, 0, 2, 0, 1)
LIN_HALF = [(p // GH) % 2 for p in range(H)]
LIN_SLOT = [GH * (p // (2 * GH)) + p % GH for p in range(H)]
SOFT_HALF = [(p % GH) // 2 for p in range(H)]
SOFT_SLOT = [2 * (p // GH) + p % 2 for p in range(H)]
C_ID, C_CAUSAL, C_HMASK, C_BEFORE, C_ONES = 0, P, 2 * P, 2 * P + H, 3 * P + H
C_TILES = 4 * P + H
C_J = C_TILES + T
C_FIRST = C_J + MT
C_ALL = C_FIRST + NE


class Buffers:
    pass


def adaln_kernel(nc, x, wqkv, bqkv, wout, bout, gamma, beta, ln1_w, ln1_b, w_qkv, w_proj,
                 ln2_w, ln2_b, gate_w, gate_b, w1, w2, c_in, wmod, consts, out):
    k = Buffers()
    (k.x, k.wqkv, k.bqkv, k.wout, k.bout, k.gamma, k.beta,
     k.ln1_w, k.ln1_b, k.w_qkv, k.w_proj, k.ln2_w, k.ln2_b,
     k.gate_w, k.gate_b, k.w1, k.w2, k.c_in, k.wmod, k.consts, k.out) = (
        x, wqkv, bqkv, wout, bout, gamma, beta, ln1_w, ln1_b, w_qkv, w_proj, ln2_w, ln2_b,
        gate_w, gate_b, w1, w2, c_in, wmod, consts, out)
    top = ExitStack()
    with top:
        def sb(name, shape, dt=F32, ctx=top):
            return ctx.enter_context(nc.sbuf_tensor(name, shape, dt))

        k.bank = [top.enter_context(nc.psum_tensor(f"bank{i}", [P, 4 * P], F32)) for i in range(4)]
        k.pair = [top.enter_context(nc.psum_tensor(f"pair{i}", [P, 8 * P], F32)) for i in range(2)]
        k.bank += [k.pair[0][:, 0:512], k.pair[0][:, 512:1024], k.pair[1][:, 0:512], k.pair[1][:, 512:1024]]

        k.x_all = sb("x_all", [P, T * D])
        k.v_all = sb("v_all", [P, T * D])
        k.fq_all = sb("fq_all", [P, B * L])
        k.h_all = sb("h_all", [P, T * D])
        k.parts = sb("parts", [P, B * 6 * L], BF16)
        k.mod4 = sb("mod4", [P, 4 * B * D])
        k.gb_all = sb("gb_all", [P, B * D])
        k.G_OF, k.B_OF, k.CB_OF, k.SB_OF = 0, B * D, 2 * B * D, 3 * B * D
        k.cst = sb("cst", [P, C_ALL])
        k.ident = k.cst[:, C_ID:C_ID + P]
        k.causal = k.cst[:, C_CAUSAL:C_CAUSAL + P]
        k.hmask = k.cst[:, C_HMASK:C_HMASK + H]
        k.identb = sb("identb", [P, P], BF16)
        k.wlt = sb("wlt", [P, 3 * D])
        k.woutt = sb("woutt", [P, D])
        k.wsm = sb("wsm", [P, 3 * D])
        k.wproj = sb("wproj", [P, D])
        k.gatew = sb("gatew", [P, NE])
        k.bq2 = sb("bq2", [P, 4])
        k.lnw = sb("lnw", [P, 2])
        k.ca1t = sb("ca1t", [P, B])
        k.sat = sb("sat", [P, B])
        k.rows = sb("rows", [P, 4 * D])
        k.BV, k.BO, k.L2W, k.L2B = (k.rows[:, i * D:(i + 1) * D] for i in range(4))
        k.gateb = sb("gateb", [P, NE])
        k.spare = sb("spare", [P, 1])
        k.halfneg = sb("halfneg", [P, 4 * C])

        def tiles(ap, n):
            return ap.rearrange("p (c d) -> p c d", c=n)

        def rep(ap, n):
            return ap.unsqueeze(1).to_broadcast([P, n, ap.shape[1]])

        k.xs_dram = nc.dram_tensor("experts_in", [MT * P, D], F32).ap()
        k.ys_dram = nc.dram_tensor("experts_out", [MT * P, D], F32).ap()

        k.tiles, k.rep = tiles, rep
        setup_phase(nc, k)
        linear_prepare(nc, k)
        linear_attend(nc, k)
        softmax_prepare(nc, k)
        softmax_attend(nc, k)
        route_phase(nc, k)


def setup_phase(nc, k):
    with ExitStack() as ctx:
        def sb(name, shape, dt=F32):
            return ctx.enter_context(nc.sbuf_tensor(name, shape, dt))
        def sem(name):
            return ctx.enter_context(nc.semaphore(name))
        wl_raw = sb("wl_raw", [P, 3, D])
        wo_raw = sb("wo_raw", [P, D])
        wo_pos = sb("wo_pos", [P, D])
        bv_raw = sb("bv_raw", [P, D])
        ws_raw = sb("ws_raw", [P, 3 * D])
        c_raw = sb("c_raw", [B, D])
        c_exp = sb("c_exp", [B, D])
        c_rec = sb("c_rec", [B, D])
        c_silu = sb("c_silu", [B, D])
        ct = sb("ct", [P, B])
        ctb = sb("ctb", [P, B, P])
        wm = sb("wm", [P, NM * D])
        gamma_r = sb("gamma_r", [P, D])
        beta_r = sb("beta_r", [P, D])
        mraw = sb("mraw", [P, B, 4 * D])
        sgn = sb("sgn", [P, 2, B * D])
        mag = sb("mag", [P, 2, B * D])
        zero = sb("zero", [P, D])
        s_w = sem("weights_in")
        s_x = sem("x_in")
        s_v = sem("vector_step")
        s_e = sem("silu_exp")
        s_t = sem("transposed")
        s_m = sem("modulation_ready")
        s_me = sem("modulation_copied")
        s_z = sem("zero_ready")
        s_zd = sem("zeros_written")

        def row(ap, n):
            return ap.rearrange("(o d) -> o d", o=1).to_broadcast([P, n])

        loads = [
            (k.cst[:], k.consts),
            (c_raw[:], k.c_in),
            (wm[:], k.wmod),
            (wo_raw[:], k.wout),
            (ws_raw[:], k.w_qkv),
            (k.gatew[:], k.gate_w),
            (gamma_r[:], row(k.gamma, D)),
            (beta_r[:], row(k.beta, D)),
            (bv_raw[:], row(k.bqkv[2 * D:3 * D], D)),
            (k.BO, row(k.bout, D)),
            (k.L2W, row(k.ln2_w, D)),
            (k.L2B, row(k.ln2_b, D)),
            (k.gateb[:], row(k.gate_b, NE)),
            (k.lnw[:, 0:1], k.ln1_w.rearrange("(d o) -> d o", o=1)),
            (k.lnw[:, 1:2], k.ln1_b.rearrange("(d o) -> d o", o=1)),
        ]
        for z in range(2):
            for half in range(2):
                rows_of = k.wqkv[z * D:(z + 1) * D, :].rearrange("(s h e) d -> h e s d", h=2, e=E)
                bias_of = k.bqkv[z * D:(z + 1) * D].rearrange("(s h e o) -> h e s o", h=2, e=E, o=1)
                loads.append((wl_raw[64 * half:64 * half + 64, z, :], rows_of[half]))
                loads.append((k.bq2[64 * half:64 * half + 64, z:z + 1], bias_of[half]))
        for p in range(0, H, GH):
            vrows = k.wqkv[2 * D:3 * D, :].rearrange("(j h e) d -> h j e d", h=2, e=E)
            loads.append((wl_raw[E * p:E * (p + GH), 2, :], vrows[LIN_HALF[p], LIN_SLOT[p]:LIN_SLOT[p] + GH]))
            for half in range(2):
                prow = k.w_proj.rearrange("(j h e) d -> h j e d", h=2, e=E)
                q = p + 2 * half
                loads.append((k.wproj[E * q:E * (q + 2), :], prow[half, SOFT_SLOT[q]:SOFT_SLOT[q] + 2]))
        NL = len(loads)
        with nc.Block() as block:

            @block.sync
            def _(sp):
                with nc.allow_non_contiguous_dma("columns of biases"):
                    for dst, src in loads:
                        sp.dma_start(dst, src).then_inc(s_w, 16)
                xv = k.x.rearrange("b (c p) d -> p (b c) d", p=P)
                for i in range(4):
                    sp.dma_start(k.tiles(k.x_all[:], T)[:, i * C * 2:(i + 1) * C * 2, :],
                                 xv[:, i * C * 2:(i + 1) * C * 2, :]).then_inc(s_x, 16)
                sp.wait_ge(s_z, 1)
                sp.dma_start(k.xs_dram.rearrange("(j p) d -> p j d", p=P), k.rep(zero[:], MT)).then_inc(s_zd, 16)
                sp.wait_ge(s_x, 64)
                sp.wait_ge(s_zd, 16)

            @block.gpsimd
            def _(pool):
                pool.memset(zero[:], 0.0).then_inc(s_z, 1)
                pool.memset(k.halfneg[:], -0.5)

            @block.scalar
            def _(act):
                act.wait_ge(s_w, 16 * NL)
                act.activation(c_exp[:], c_raw[:], ACT.Exp, scale=-1.0).then_inc(s_e, 1)
                for b in range(B):
                    act.wait_ge(s_m, b + 2)
                    act.activation(mraw[:, b, :], k.bank[b % 2][:], ACT.Copy).then_inc(s_me, 1)

            @block.tensor
            def _(pe):
                pe.wait_ge(s_w, 16 * NL)
                for z in range(3):
                    pe.transpose(k.bank[0][:, z * P:(z + 1) * P], wl_raw[:, z, :], k.ident).then_inc(s_t, 1)
                pe.wait_ge(s_v, 7)
                pe.transpose(k.bank[0][:, 3 * P:4 * P], wo_pos[:], k.ident).then_inc(s_t, 1)
                pe.transpose(k.bank[1][:, 0:B], c_silu[:], k.ident[0:B, 0:B]).then_inc(s_t, 1)
                pe.wait_ge(s_v, 14)
                for j in range(2):
                    last = pe.matmul(k.bank[2][:, j * B:(j + 1) * B], wm[:, j * D:(j + 1) * D], ct[:],
                                     start=True, stop=True)
                last.then_inc(s_m, 1)
                for b in range(B):
                    if b >= 2:
                        pe.wait_ge(s_me, b - 1)
                    pe.matmul(k.bank[b % 2][:], ctb[:, b, :], wm[:, 2 * D:NM * D],
                              start=True, stop=True).then_inc(s_m, 1)

            @block.vector
            def _(dve):
                step = [0]

                def done(ins):
                    step[0] += 1
                    ins.then_inc(s_v, 1)

                def after(n=None):
                    dve.wait_ge(s_v, step[0] if n is None else n)

                dve.wait_ge(s_e, 1)
                done(dve.tensor_scalar(c_exp[:], c_exp[:], 1.0, None, ALU.add))
                after()
                done(dve.reciprocal(c_rec[:], c_exp[:]))
                after()
                done(dve.tensor_tensor(c_silu[:], c_raw[:], c_rec[:], ALU.mult))
                dve.wait_ge(s_w, 16 * NL)
                for half in range(2):
                    for dst, src in ((wo_pos[:], wo_raw[:]), (k.BV, bv_raw[:])):
                        done(dve.tensor_copy(
                            dst.rearrange("p (a h f) -> p a h f", a=2, h=2)[:, :, half, :].rearrange("p a (j e) -> p a j e", e=E),
                            src.rearrange("p (a j h e) -> p a j h e", a=2, h=2, e=E)[:, :, :, half, :]))
                dve.wait_ge(s_t, 5)
                done(dve.tensor_copy(k.wlt[:], k.bank[0][:, 0:3 * P]))
                done(dve.tensor_copy(k.woutt[:], k.bank[0][:, 3 * P:4 * P]))
                done(dve.tensor_copy(k.identb[:], k.ident))
                dve.wait_ge(s_w, 16 * NL)
                done(dve.tensor_scalar(k.bq2[:, 2:4], k.bq2[:, 0:2], FEAT_EPS, None, ALU.add))
                done(dve.tensor_copy(ct[:], k.bank[1][:, 0:B]))
                after()
                done(dve.tensor_copy(ctb[:, 0:4, :], ct[:, 0:4].unsqueeze(2).to_broadcast([P, 4, P])))
                done(dve.tensor_copy(ctb[:, 4:8, :], ct[:, 4:8].unsqueeze(2).to_broadcast([P, 4, P])))
                for z in range(2):
                    for half in range(2):
                        done(dve.tensor_copy(
                            k.wsm[:, z * D + 64 * half:z * D + 64 * half + 64].rearrange("p (e s) -> p s e", e=E),
                            ws_raw[:, z * D:(z + 1) * D].rearrange("p (s h e) -> p s h e", h=2, e=E)[:, :, half, :]))
                for half in range(2):
                    done(dve.tensor_copy(
                        k.wsm[:, 2 * D:3 * D].rearrange("p (g h j e) -> p g h j e", g=G, h=2, e=E)[:, :, half],
                        ws_raw[:, 2 * D:3 * D].rearrange("p (g j h e) -> p g j h e", g=G, h=2, e=E)[:, :, :, half, :]))
                dve.wait_ge(s_m, 1)
                done(dve.tensor_copy(k.sat[:], k.bank[2][:, 0:B]))
                done(dve.tensor_scalar(k.ca1t[:], k.bank[2][:, B:2 * B], 1.0, None, ALU.add))
                dve.wait_ge(s_me, B)
                for i, j in enumerate((0, 3)):
                    g = mraw[:, :, j * D:(j + 1) * D]
                    sg = sgn[:, i, :].rearrange("p (b d) -> p b d", b=B)
                    mg = mag[:, i, :].rearrange("p (b d) -> p b d", b=B)
                    done(dve.tensor_scalar(sg, g, 0.0, 2.0, ALU.is_ge, ALU.mult))
                    after()
                    done(dve.tensor_scalar(sg, sg, -1.0, None, ALU.add))
                    after()
                    done(dve.tensor_tensor(mg, g, sg, ALU.mult))
                    after()
                    done(dve.tensor_scalar(mg, mg, 0.25, None, ALU.max))
                    after()
                    if i == 0:
                        done(dve.tensor_tensor(mg, mg, sg, ALU.mult))
                        after()
                        done(dve.tensor_tensor(k.tiles(k.mod4[:, 0:B * D], B), mg, k.rep(gamma_r[:], B), ALU.mult))
                        done(dve.tensor_tensor(k.tiles(k.mod4[:, B * D:2 * B * D], B), mg, k.rep(beta_r[:], B), ALU.mult))
                    else:
                        done(dve.tensor_tensor(k.tiles(k.gb_all[:], B), mg, sg, ALU.mult))
                done(dve.tensor_scalar(k.tiles(k.mod4[:, 2 * B * D:3 * B * D], B), mraw[:, :, 2 * D:3 * D], 1.0, None, ALU.add))
                done(dve.tensor_copy(k.tiles(k.mod4[:, 3 * B * D:4 * B * D], B), mraw[:, :, D:2 * D]))
                after()


U4 = 4


def norm_stats(dve, k, st, mv, ve, src, n, s_st, s_mv, s_ve, base_st, base_mv):
    dve.memset(k.spare[:], 0.0)
    for i in range(n):
        dve.bn_stats(st[:, i, :], src(i)).then_inc(s_st, 1)
    dve.wait_ge(s_st, base_st + n)
    dve.memset(k.spare[:], 0.0)
    for i in range(n):
        dve.bn_aggr(mv[:, i, :], st[:, i, :]).then_inc(s_mv, 1)
    dve.wait_ge(s_mv, base_mv + n)
    dve.tensor_scalar(ve[:], mv[:, :, 1], LN_EPS, None, ALU.add).then_inc(s_ve, 1)


def linear_prepare(nc, k):
    N = U4 * C
    with ExitStack() as ctx:
        def sb(name, shape, dt=F32):
            return ctx.enter_context(nc.sbuf_tensor(name, shape, dt))
        def sem(name):
            return ctx.enter_context(nc.semaphore(name))
        st = sb("a_st", [P, N, 6])
        mv = sb("a_mv", [P, N, 2])
        ve = sb("a_ve", [P, N])
        rs = sb("a_rs", [P, N])
        xn = sb("a_xn", [P, N * D])
        ht = sb("a_ht", [P, U4 * L])
        ex = sb("a_ex", [P, 2, L])
        rl = sb("a_rl", [P, 2, L])
        ph = sb("a_ph", [P, 2, L])
        r1 = sb("a_r1", [P, 2, L])
        fk = sb("a_fk", [P, U4, L])
        s_st, s_mv, s_ve, s_rs = sem("a_stats"), sem("a_means"), sem("a_variances"), sem("a_rstd")
        s_xn, s_tr, s_ht = sem("a_normed"), sem("a_transposed"), sem("a_h_ready")
        s_pj, s_ex, s_rl, s_ph = sem("a_projected"), sem("a_exp"), sem("a_relu"), sem("a_features")
        s_p1, s_r1, s_p2, s_p3 = sem("a_part1"), sem("a_rest1"), sem("a_part2"), sem("a_part3")
        s_v, s_vc, s_kt, s_kc = sem("a_v"), sem("a_v_copied"), sem("a_k_transposed"), sem("a_k_copied")

        with nc.Block() as block:

            @block.vector
            def _(dve):
                with dve.Fori(0, B // U4) as it:
                    norm_stats(dve, k, st, mv, ve, lambda i: k.x_all[:, bass.ds(it * (N * D) + i * D, D)], N,
                               s_st, s_mv, s_ve, it * N, it * N)
                    dve.wait_ge(s_rs, it + 1)
                    for i in range(N):
                        if i == 0:
                            dve.wait_ge(s_tr, it * N + 1)
                        dve.tensor_scalar(xn[:, i * D:(i + 1) * D],
                                          k.x_all[:, bass.ds(it * (N * D) + i * D, D)],
                                          mv[:, i, 0:1], rs[:, i:i + 1], ALU.subtract, ALU.mult).then_inc(s_xn, 1)

                    def features(u):
                        for z in range(2):
                            n = 2 * u + z
                            dve.wait_ge(s_pj, it * 2 * U4 + n + 1)
                            dve.wait_ge(s_ex, it * 2 * U4 + n + 1)
                            dve.tensor_scalar(rl[:, z, :], k.bank[4 + 2 * (u % 2) + z][:], k.bq2[:, 2 + z:3 + z],
                                              FEAT_EPS, ALU.add, ALU.max).then_inc(s_rl, 1)
                        for z in range(2):
                            n = 2 * u + z
                            dve.wait_ge(s_rl, it * 2 * U4 + n + 1)
                            if z == 0:
                                f = k.fq_all[:, bass.ds(it * (U4 * L) + u * L, L)]
                            else:
                                f = fk[:, u, :]
                                if u == 0:
                                    dve.wait_ge(s_kt, it * U4 + 1)
                            dve.scalar_tensor_tensor(f, ex[:, z, :], 1.0, rl[:, z, :],
                                                     ALU.min, ALU.add).then_inc(s_ph, 1)
                        for z in range(2):
                            n = 2 * u + z
                            dve.wait_ge(s_ph, it * 2 * U4 + n + 1)
                            dve.wait_ge(s_p1, it * 2 * U4 + n + 1)
                            f = k.fq_all[:, bass.ds(it * (U4 * L) + u * L, L)] if z == 0 else fk[:, u, :]
                            dve.wait_ge(s_p3, it * 2 * U4 + n + 1)
                            dve.tensor_tensor(r1[:, z, :], f,
                                              k.parts[:, bass.ds(it * (U4 * 6 * L) + (6 * u + 3 * z) * L, L)],
                                              ALU.subtract).then_inc(s_r1, 1)

                    features(0)
                    features(1)
                    for u in range(U4):
                        dve.wait_ge(s_v, it * U4 + u + 1)
                        dve.tensor_tensor(k.tiles(k.v_all[:, bass.ds(it * (N * D) + u * C * D, C * D)], C),
                                          k.tiles(k.bank[u][:], C), k.rep(k.BV, C), ALU.add).then_inc(s_vc, 1)
                    features(2)
                    features(3)

            @block.gpsimd
            def _(pool):
                pool.sem_inc(s_p3, 2)
                with pool.Fori(0, B // U4) as it:
                    pool.wait_ge(s_ve, it + 1)
                    pool.tensor_tensor(rs[:], ve[:], k.halfneg[:], ALU.pow).then_inc(s_rs, 1)
                    for n in range(2 * U4):
                        u, z = n // 2, n % 2
                        pool.wait_ge(s_p2, it * 2 * U4 + n + 1)
                        pool.tensor_tensor(k.parts[:, bass.ds(it * (U4 * 6 * L) + (6 * u + 3 * z + 2) * L, L)],
                                           r1[:, z, :],
                                           k.parts[:, bass.ds(it * (U4 * 6 * L) + (6 * u + 3 * z + 1) * L, L)],
                                           ALU.subtract).then_inc(s_p3, 1)

            @block.scalar
            def _(act):
                with act.Fori(0, B // U4) as it:
                    for u in range(U4):
                        act.wait_ge(s_tr, it * N + C * (u + 1) + 1)
                        act.activation(ht[:, u * L:(u + 1) * L], k.bank[u][:], ACT.Identity,
                                       bias=k.sat[:, bass.ds(it * U4 + u, 1)],
                                       scale=k.ca1t[:, bass.ds(it * U4 + u, 1)]).then_inc(s_ht, 1)

                    def features(u):
                        for z in range(2):
                            act.wait_ge(s_pj, it * 2 * U4 + 2 * u + z + 1)
                            act.activation(ex[:, z, :], k.bank[4 + 2 * (u % 2) + z][:], ACT.Exp,
                                           bias=k.bq2[:, z:z + 1]).then_inc(s_ex, 1)
                        for z in range(2):
                            n = 2 * u + z
                            f = k.fq_all[:, bass.ds(it * (U4 * L) + u * L, L)] if z == 0 else fk[:, u, :]
                            act.wait_ge(s_ph, it * 2 * U4 + n + 1)
                            act.activation(k.parts[:, bass.ds(it * (U4 * 6 * L) + (6 * u + 3 * z) * L, L)],
                                           f, ACT.Copy).then_inc(s_p1, 1)
                        for z in range(2):
                            n = 2 * u + z
                            act.wait_ge(s_r1, it * 2 * U4 + n + 1)
                            act.activation(k.parts[:, bass.ds(it * (U4 * 6 * L) + (6 * u + 3 * z + 1) * L, L)],
                                           r1[:, z, :], ACT.Copy).then_inc(s_p2, 1)

                    for u in range(U4):
                        features(u)
                    for u in range(U4):
                        act.wait_ge(s_kt, it * U4 + u + 2)
                        act.activation(k.h_all[:, bass.ds(it * (N * D) + u * C * D, C * D)], k.bank[u][:],
                                       ACT.Copy).then_inc(s_kc, 1)

            @block.tensor
            def _(pe):
                pe.sem_inc(s_tr, 1)
                pe.sem_inc(s_kt, 1)
                with pe.Fori(0, B // U4) as it:
                    for u in range(U4):
                        for c in range(C):
                            i = u * C + c
                            pe.wait_ge(s_xn, it * N + i + 1)
                            pe.transpose(k.bank[u][:, c * P:(c + 1) * P], xn[:, i * D:(i + 1) * D],
                                         k.ident).then_inc(s_tr, 1)

                    def qk(u):
                        pe.wait_ge(s_ht, it * U4 + u + 1)
                        if u >= 2:
                            pe.wait_ge(s_rl, it * 2 * U4 + 2 * (u - 1))
                        for z in range(2):
                            pe.matmul(k.bank[4 + 2 * (u % 2) + z][:], k.wlt[:, z * D:(z + 1) * D],
                                      ht[:, u * L:(u + 1) * L], start=True, stop=True).then_inc(s_pj, 1)

                    qk(0)
                    qk(1)
                    for u in range(U4):
                        pe.wait_ge(s_ht, it * U4 + u + 1)
                        for c in range(C):
                            last = pe.matmul(k.bank[u][:, c * P:(c + 1) * P],
                                             ht[:, u * L + c * P:u * L + (c + 1) * P],
                                             k.wlt[:, 2 * D:3 * D], start=True, stop=True)
                        last.then_inc(s_v, 1)
                    qk(2)
                    qk(3)
                    for u in range(U4):
                        pe.wait_ge(s_vc, it * U4 + u + 1)
                        pe.wait_ge(s_ph, it * 2 * U4 + 2 * u + 2)
                        for c in range(C):
                            last = pe.transpose(k.bank[u][:, c * P:(c + 1) * P], fk[:, u, c * P:(c + 1) * P], k.ident)
                        last.then_inc(s_kt, 1)
                    pe.wait_ge(s_kc, it * U4 + U4)


def load_stacks(sp, k, qs, ks, b, sem):
    for side, (stack, part) in enumerate(((qs, Q_PART), (ks, K_PART))):
        for half in range(2):
            for r in range(6):
                sp.dma_start(stack[64 * half + E * r:64 * half + E * r + E, :, :],
                             k.parts[64 * half:64 * half + 64, bass.ds(b * (6 * L) + (3 * side + part[r]) * L, L)]
                             ).then_inc(sem, 16)


N_STACK = 24 * 16


def linear_attend(nc, k):
    with ExitStack() as ctx:
        def sb(name, shape, dt=F32):
            return ctx.enter_context(nc.sbuf_tensor(name, shape, dt))
        def sem(name):
            return ctx.enter_context(nc.semaphore(name))
        qs = [sb(f"b_qs{i}", [P, S, L], BF16) for i in range(2)]
        ks = [sb(f"b_ks{i}", [P, S, L], BF16) for i in range(2)]
        kt = [sb(f"b_kt{i}", [P, C * D]) for i in range(2)]
        vp = sb("b_vp", [P, C, H, VW])
        am = sb("b_am", [P, 2, GH, P])
        spad = sb("b_spad", [P, C - 1, H * VW])
        nt = sb("b_nt", [P, 2, G * P])
        den = sb("b_den", [P, 2, H])
        on = sb("b_on", [P, 2, D])
        ot = sb("b_ot", [P, 2, D])
        s_init, s_vp = sem("b_init"), sem("b_values")
        s_stk = [sem(f"b_stacks{i}") for i in range(2)]
        s_ktl = [sem(f"b_k_loaded{i}") for i in range(2)]
        s_at, s_am, s_sm, s_sp = sem("b_products"), sem("b_masked"), sem("b_state"), sem("b_state_masked")
        s_nm, s_nt, s_tr, s_de = sem("b_numerators"), sem("b_numerators_out"), sem("b_turned"), sem("b_denominators")
        s_rc, s_on, s_oT, s_oc = sem("b_reciprocals"), sem("b_normalised"), sem("b_output_turned"), sem("b_output_copied")
        s_y, s_yc, s_fin = sem("b_projected"), sem("b_projected_out"), sem("b_batch_read")
        b_at = [k.bank[0], k.bank[1]]
        b_nm = [k.bank[2], k.bank[3]]
        b_state, b_tr, b_ot, b_y = k.bank[4], k.bank[5], k.bank[6], k.bank[7]
        NU = C * G
        EPS = FEAT_EPS * E ** 0.5

        with nc.Block() as block:

            @block.gpsimd
            def _(pool):
                pool.memset(vp[:], 0.0).then_inc(s_init, 1)
                pool.memset(spad[:], 0.0).then_inc(s_init, 1)
                pool.wait_ge(s_init, 2)
                pool.memset(vp[:, :, :, E:E + 1], 1.0).then_inc(s_init, 1)
                with pool.Fori(0, B) as b:
                    pool.wait_ge(s_fin, b + 2)
                    for c in range(C):
                        pool.tensor_copy(vp[:, c, :, 0:E],
                                         k.v_all[:, bass.ds(b * (C * D) + c * D, D)].rearrange("p (h e) -> p h e", h=H)
                                         ).then_inc(s_vp, 1)

            @block.sync
            def _(sp):
                with sp.Fori(0, B // 2) as it:
                    for u in range(2):
                        sp.wait_ge(s_fin, it * 2 + u + 1)
                        sp.dma_start(kt[u][:], k.h_all[:, bass.ds(it * (2 * C * D) + u * C * D, C * D)]).then_inc(s_ktl[u], 16)
                        load_stacks(sp, k, qs[u], ks[u], it * 2 + u, s_stk[u])

            @block.tensor
            def _(pe):
                pe.sem_inc(s_fin, 2)
                with pe.Fori(0, B // 2) as it:
                    for u in range(2):
                        b = it * 2 + u
                        pe.wait_ge(s_ktl[u], it * 16 + 16)
                        for c in range(C - 1):
                            pe.wait_ge(s_vp, b * C + c + 1)
                            if c == 0:
                                pe.wait_ge(s_sp, b * (C - 1) + 1)
                            else:
                                pe.wait_ge(s_sp, b * (C - 1) + c + 1)
                            pe.matmul(b_state[:, 0:H * (E + 1)], kt[u][:, c * D:(c + 1) * D],
                                      vp[:, c, :, 0:E + 1], start=(c == 0), stop=(c == C - 2),
                                      skip_group_check=True).then_inc(s_sm, 1)
                        pe.wait_ge(s_stk[u], it * N_STACK + N_STACK)

                        def products(n):
                            c, g = n // G, n % G
                            pe.wait_ge(s_am, b * NU + n + 1)
                            for j in range(GH):
                                r, slot = 64 * LIN_HALF[GH * g + j], LIN_SLOT[GH * g + j]
                                last = pe.matmul(b_at[n % 2][:, j * P:(j + 1) * P],
                                                 ks[u][r:r + KR, slot, c * P:(c + 1) * P],
                                                 qs[u][r:r + KR, slot, c * P:(c + 1) * P],
                                                 start=True, stop=True)
                            last.then_inc(s_at, 1)

                        def numerators(n):
                            c, g = n // G, n % G
                            if g == 0:
                                pe.wait_ge(s_nt, b * C + c + 1)
                                pe.wait_ge(s_vp, b * C + c + 1)
                            if c and g == 0:
                                pe.wait_ge(s_sp, b * (C - 1) + c + 1)
                            cols = slice(g * P, (g + 1) * P)
                            if c:
                                pe.matmul(b_nm[c % 2][:, cols], spad[:, c - 1, cols],
                                          k.fq_all[:, bass.ds(b * L + c * P, P)], start=True, stop=False,
                                          skip_group_check=True)
                            pe.wait_ge(s_am, b * NU + n + 3)
                            for j in range(GH):
                                last = pe.matmul(b_nm[c % 2][VW * j:VW * (j + 1), cols], vp[:, c, GH * g + j, :],
                                                 am[:, n % 2, j, :], start=(c == 0), stop=True,
                                                 tile_position=(0, VW * j), skip_group_check=True)
                            last.then_inc(s_nm, 1)

                        def turn(c):
                            pe.wait_ge(s_nt, b * C + c + 3)
                            pe.wait_ge(s_on, b * C + c + 1)
                            for g in range(G):
                                last = pe.transpose(b_tr[:, g * P:(g + 1) * P], nt[:, c % 2, g * P:(g + 1) * P], k.ident)
                            last.then_inc(s_tr, 1)

                        def turn_back(c):
                            pe.wait_ge(s_on, b * C + c + 2)
                            pe.wait_ge(s_oc, b * C + c + 1)
                            pe.transpose(b_ot[:, 0:P], on[:, c % 2, :], k.ident).then_inc(s_oT, 1)

                        def project(c):
                            pe.wait_ge(s_oc, b * C + c + 2)
                            if c == 0:
                                pe.wait_ge(s_yc, b + 1)
                            pe.matmul(b_y[:, c * P:(c + 1) * P], ot[:, c % 2, :], k.woutt[:],
                                      start=True, stop=True).then_inc(s_y, 1)

                        products(0)
                        for n in range(NU):
                            if n + 1 < NU:
                                products(n + 1)
                            numerators(n)
                            c, g = n // G, n % G
                            if c and g == 1:
                                turn(c - 1)
                            if c and g == 3:
                                turn_back(c - 1)
                            if c >= 2 and g == 0:
                                project(c - 2)
                        project(C - 2)
                        turn(C - 1)
                        turn_back(C - 1)
                        project(C - 1)
                        pe.wait_ge(s_y, b * C + C)
                        pe.sem_inc(s_fin, 1)

            @block.vector
            def _(dve):
                dve.sem_inc(s_sp, 1)
                dve.sem_inc(s_am, 2)
                dve.sem_inc(s_on, 1)
                dve.sem_inc(s_yc, 1)
                dve.wait_ge(s_init, 3)
                with dve.Fori(0, B) as b:
                    def masked(n):
                        dve.wait_ge(s_at, b * NU + n + 1)
                        if n >= 2:
                            dve.wait_ge(s_nm, b * NU + n - 1)
                        dve.tensor_tensor(am[:, n % 2, :, :], k.tiles(b_at[n % 2][:], GH), k.rep(k.causal, GH),
                                          ALU.mult).then_inc(s_am, 1)

                    def state(c):
                        dve.wait_ge(s_sm, b * (C - 1) + c + 1)
                        dve.tensor_tensor(spad[:, c, :].rearrange("p (h w) -> p h w", h=H)[:, :, 0:E + 1],
                                          b_state[:, 0:H * (E + 1)].rearrange("p (h w) -> p h w", h=H),
                                          k.hmask.unsqueeze(2).to_broadcast([P, H, E + 1]),
                                          ALU.mult).then_inc(s_sp, 1)

                    def normalise(c):
                        dve.wait_ge(s_tr, b * C + c + 1)
                        heads = b_tr[:].rearrange("p (h w) -> p h w", h=H)
                        dve.tensor_scalar(den[:, c % 2, :], heads[:, :, E], EPS, None, ALU.add).then_inc(s_de, 1)
                        dve.wait_ge(s_de, b * C + c + 1)
                        dve.reciprocal(den[:, c % 2, :], den[:, c % 2, :]).then_inc(s_rc, 1)
                        dve.wait_ge(s_rc, b * C + c + 1)
                        dve.tensor_tensor(on[:, c % 2, :].rearrange("p (h e) -> p h e", h=H), heads[:, :, 0:E],
                                          den[:, c % 2, :].unsqueeze(2).to_broadcast([P, H, E]),
                                          ALU.mult).then_inc(s_on, 1)

                    for c in range(C - 1):
                        state(c)
                    for n in range(NU):
                        masked(n)
                        if n >= G and n % G == 2:
                            normalise(n // G - 1)
                    normalise(C - 1)
                    dve.wait_ge(s_y, b * C + C)
                    dve.tensor_tensor(k.tiles(k.v_all[:, bass.ds(b * (C * D), C * D)], C), k.tiles(b_y[:], C),
                                      k.rep(k.BO, C), ALU.add).then_inc(s_yc, 1)

            @block.scalar
            def _(act):
                act.sem_inc(s_nt, 2)
                act.sem_inc(s_oc, 1)
                with act.Fori(0, B) as b:
                    def numerators_out(c):
                        act.wait_ge(s_nm, b * NU + (c + 1) * G)
                        act.wait_ge(s_tr, b * C + c - 1) if c >= 2 else None
                        act.activation(nt[:, c % 2, :], b_nm[c % 2][:], ACT.Copy).then_inc(s_nt, 1)

                    def output_out(c):
                        act.wait_ge(s_oT, b * C + c + 1)
                        act.activation(ot[:, c % 2, :], b_ot[:, 0:P], ACT.Copy).then_inc(s_oc, 1)

                    for c in range(C):
                        numerators_out(c)
                        if c:
                            output_out(c - 1)
                    output_out(C - 1)


def softmax_prepare(nc, k):
    N = U4 * C
    with ExitStack() as ctx:
        def sb(name, shape, dt=F32):
            return ctx.enter_context(nc.sbuf_tensor(name, shape, dt))
        def sem(name):
            return ctx.enter_context(nc.semaphore(name))
        st = sb("c_st", [P, N, 6])
        mv = sb("c_mv", [P, 3, N, 2])
        ve = sb("c_ve", [P, N])
        rs = sb("c_rs", [P, 3, N])
        xn = sb("c_xn", [P, N * D])
        tmp = sb("c_tmp", [P, N * D])
        ht = sb("c_ht", [P, U4 * L])
        r1 = sb("c_r1", [P, 2, L])
        s_st, s_mv, s_ve, s_rs = sem("c_stats"), sem("c_means"), sem("c_variances"), sem("c_rstd")
        s_z, s_t1, s_ln, s_xn = sem("c_x_shifted"), sem("c_scaled"), sem("c_layernorms"), sem("c_normed")
        s_tr, s_ht, s_pj = sem("c_transposed"), sem("c_h_ready"), sem("c_projected")
        s_p1, s_r1, s_p2, s_p3 = sem("c_part1"), sem("c_rest1"), sem("c_part2"), sem("c_part3")
        s_v, s_vc = sem("c_v"), sem("c_v_copied")

        with nc.Block() as block:

            def tile_at(a, it, i):
                return a[:, bass.ds(it * (N * D) + i * D, D)]

            @block.vector
            def _(dve):
                with dve.Fori(0, B // U4) as it:
                    for m, (src, dst, gain) in enumerate(((k.v_all, k.x_all, k.G_OF), (k.x_all, k.h_all, k.CB_OF))):
                        norm_stats(dve, k, st, mv[:, m], ve, lambda i: tile_at(src, it, i), N,
                                   s_st, s_mv, s_ve, it * (3 * N) + m * N, it * (3 * N) + m * N)
                        for i in range(N):
                            row = k.mod4[:, bass.ds(it * (U4 * D) + gain + (i // C) * D, D)]
                            dve.scalar_tensor_tensor(tmp[:, i * D:(i + 1) * D], tile_at(src, it, i), mv[:, m, i, 0:1],
                                                     row, ALU.subtract, ALU.mult).then_inc(s_t1, 1)
                        dve.wait_ge(s_rs, it * 3 + m + 1)
                        dve.wait_ge(s_t1, it * (2 * N) + (m + 1) * N)
                        if m == 0:
                            dve.wait_ge(s_z, it * U4 + U4)
                        for i in range(N):
                            shift = (tile_at(k.x_all, it, i) if m == 0 else
                                     k.mod4[:, bass.ds(it * (U4 * D) + k.SB_OF + (i // C) * D, D)])
                            dve.scalar_tensor_tensor(tile_at(dst, it, i), tmp[:, i * D:(i + 1) * D], rs[:, m, i:i + 1],
                                                     shift, ALU.mult, ALU.add).then_inc(s_ln, 1)
                        dve.wait_ge(s_ln, it * (2 * N) + (m + 1) * N)
                    norm_stats(dve, k, st, mv[:, 2], ve, lambda i: tile_at(k.h_all, it, i), N,
                               s_st, s_mv, s_ve, it * (3 * N) + 2 * N, it * (3 * N) + 2 * N)
                    dve.wait_ge(s_rs, it * 3 + 3)
                    for i in range(N):
                        dve.tensor_scalar(xn[:, i * D:(i + 1) * D], tile_at(k.h_all, it, i),
                                          mv[:, 2, i, 0:1], rs[:, 2, i:i + 1], ALU.subtract, ALU.mult).then_inc(s_xn, 1)
                    for u in range(U4):
                        for z in range(2):
                            n = 2 * u + z
                            dve.wait_ge(s_p1, it * 2 * U4 + n + 1)
                            dve.wait_ge(s_p3, it * 2 * U4 + n + 1)
                            dve.tensor_tensor(r1[:, z, :], k.bank[4 + 2 * (u % 2) + z][:],
                                              k.parts[:, bass.ds(it * (U4 * 6 * L) + (6 * u + 3 * z) * L, L)],
                                              ALU.subtract).then_inc(s_r1, 1)

            @block.gpsimd
            def _(pool):
                pool.sem_inc(s_p3, 2)
                with pool.Fori(0, B // U4) as it:
                    for u in range(U4):
                        xu = k.tiles(k.x_all[:, bass.ds(it * (N * D) + u * C * D, C * D)], C)
                        pool.tensor_tensor(xu, xu, k.mod4[:, bass.ds(it * (U4 * D) + k.B_OF + u * D, D)]
                                           .unsqueeze(1).to_broadcast([P, C, D]), ALU.add).then_inc(s_z, 1)
                    for m in range(3):
                        pool.wait_ge(s_ve, it * 3 + m + 1)
                        pool.tensor_tensor(rs[:, m, :], ve[:], k.halfneg[:], ALU.pow).then_inc(s_rs, 1)
                    for n in range(2 * U4):
                        u, z = n // 2, n % 2
                        pool.wait_ge(s_p2, it * 2 * U4 + n + 1)
                        pool.tensor_tensor(k.parts[:, bass.ds(it * (U4 * 6 * L) + (6 * u + 3 * z + 2) * L, L)],
                                           r1[:, z, :],
                                           k.parts[:, bass.ds(it * (U4 * 6 * L) + (6 * u + 3 * z + 1) * L, L)],
                                           ALU.subtract).then_inc(s_p3, 1)

            @block.scalar
            def _(act):
                act.sem_inc(s_vc, 1)
                with act.Fori(0, B // U4) as it:
                    for u in range(U4):
                        act.wait_ge(s_tr, it * U4 + u + 1)
                        act.activation(ht[:, u * L:(u + 1) * L], k.bank[u][:], ACT.Identity,
                                       bias=k.lnw[:, 1:2], scale=k.lnw[:, 0:1]).then_inc(s_ht, 1)
                    for u in range(U4):
                        for z in range(2):
                            act.wait_ge(s_pj, it * 2 * U4 + 2 * u + z + 1)
                            act.activation(k.parts[:, bass.ds(it * (U4 * 6 * L) + (6 * u + 3 * z) * L, L)],
                                           k.bank[4 + 2 * (u % 2) + z][:], ACT.Copy).then_inc(s_p1, 1)
                        for z in range(2):
                            act.wait_ge(s_r1, it * 2 * U4 + 2 * u + z + 1)
                            act.activation(k.parts[:, bass.ds(it * (U4 * 6 * L) + (6 * u + 3 * z + 1) * L, L)],
                                           r1[:, z, :], ACT.Copy).then_inc(s_p2, 1)
                        act.wait_ge(s_v, it * U4 + u + 1)
                        act.activation(k.v_all[:, bass.ds(it * (N * D) + u * C * D, C * D)], k.bank[u][:],
                                       ACT.Copy).then_inc(s_vc, 1)

            @block.tensor
            def _(pe):
                with pe.Fori(0, B // U4) as it:
                    for u in range(U4):
                        if u == 0:
                            pe.wait_ge(s_vc, it * U4 + 1)
                        pe.wait_ge(s_xn, it * N + (u + 1) * C)
                        for c in range(C):
                            i = u * C + c
                            last = pe.transpose(k.bank[u][:, c * P:(c + 1) * P], xn[:, i * D:(i + 1) * D], k.ident)
                        last.then_inc(s_tr, 1)
                    for u in range(U4):
                        pe.wait_ge(s_ht, it * U4 + u + 1)
                        if u >= 2:
                            pe.wait_ge(s_r1, it * 2 * U4 + 2 * (u - 1))
                        for z in range(2):
                            pe.matmul(k.bank[4 + 2 * (u % 2) + z][:], k.wsm[:, z * D:(z + 1) * D],
                                      ht[:, u * L:(u + 1) * L], start=True, stop=True).then_inc(s_pj, 1)
                        for c in range(C):
                            last = pe.matmul(k.bank[u][:, c * P:(c + 1) * P], ht[:, u * L + c * P:u * L + (c + 1) * P],
                                             k.wsm[:, 2 * D:3 * D], start=True, stop=True)
                        last.then_inc(s_v, 1)


def wait(eng, sem, value):
    if isinstance(value, int) and value <= 0:
        return
    eng.wait_ge(sem, value)


def paired(eng, body):
    body(0, True, False)
    with eng.Fori(1, B // 2 - 1) as it:
        body(it, False, False)
    body(B // 2 - 1, False, True)


def softmax_attend(nc, k):
    with ExitStack() as ctx:
        def sb(name, shape, dt=F32):
            return ctx.enter_context(nc.sbuf_tensor(name, shape, dt))
        def sem(name):
            return ctx.enter_context(nc.semaphore(name))
        qs = [sb(f"d_qs{i}", [P, S, L], BF16) for i in range(2)]
        ks = [sb(f"d_ks{i}", [P, S, L], BF16) for i in range(2)]
        vp = [sb(f"d_vp{i}", [P, C, H, VW]) for i in range(2)]
        mx = sb("d_mx", [P, 2, 4 * C])
        mneg = sb("d_mneg", [P, 2, 4 * C], BF16)
        mt = sb("d_mt", [4 * C, 2, P], BF16)
        den = sb("d_den", [P, 2, H])
        on = sb("d_on", [P, 2, D])
        ot = sb("d_ot", [P, 2, D])
        nt = k.fq_all[:].rearrange("p (u g q) -> p u g q", u=2, g=G)
        pt = k.mod4[:].rearrange("p (r x f) -> p r x f", r=2, x=2)
        s_init, s_vp = sem("d_init"), sem("d_values")
        s_stk = [sem(f"d_stacks{i}") for i in range(2)]
        s_m, s_mr, s_mn, s_mt, s_mc = (sem("d_max_scores"), sem("d_maxima"), sem("d_negated"),
                                       sem("d_maxima_turned"), sem("d_maxima_copied"))
        s_row = [sem(f"d_maxima_rows{i}") for i in range(2)]
        s_s, s_e, s_pv, s_ne = sem("d_scores"), sem("d_probs"), sem("d_values_summed"), sem("d_numerators_out")
        s_ft, s_fd, s_fr, s_fo = sem("d_turned"), sem("d_denominators"), sem("d_reciprocals"), sem("d_normalised")
        s_fb, s_fe, s_fp, s_fh = sem("d_turned_back"), sem("d_output_copied"), sem("d_projected"), sem("d_y_ready")
        b_m, b_num, b_misc, b_s = [k.bank[0], k.bank[1]], k.bank[2], k.bank[3], k.pair
        NG = 2 * G
        SCALE = E ** -0.5

        with nc.Block() as block:

            @block.sync
            def _(sp):
                def stack_piece(u, b, piece):
                    side, half = piece // 2, piece % 2
                    stack, part = ((qs, Q_PART), (ks, K_PART))[side]
                    for r in range(6):
                        sp.dma_start(stack[u][64 * half + E * r:64 * half + E * r + E, :, :],
                                     k.parts[64 * half:64 * half + 64,
                                             bass.ds(b * (6 * L) + (3 * side + part[r]) * L, L)]).then_inc(s_stk[u], 16)

                def rows(i, n):
                    wait(sp, s_mc, n + 1)
                    u, g = (i // G) % 2, i % G
                    for half in range(2):
                        r = 64 * half + KR
                        sp.dma_start(qs[u][r:r + 1, 2 * g:2 * g + 2, :], mt[8 * half:8 * half + 8, i % 2, :]).then_inc(s_row[i % 2], 16)

                def body(it, first, last):
                    for i in range(NG):
                        n = it * NG + i
                        u, g = i // G, i % G
                        if g < 2 and not (last and u == 1):
                            if g == 0:
                                wait(sp, s_pv, n * C)
                            for piece in (2 * g, 2 * g + 1):
                                stack_piece(1 - u, it * 2 + u + 1, piece)
                        if not (last and i == NG - 1):
                            rows(i + 1, n + 1)

                wait(sp, s_init, 4)
                for piece in range(4):
                    stack_piece(0, 0, piece)
                rows(0, 0)
                paired(sp, body)

            @block.gpsimd
            def _(pool):
                for u in range(2):
                    pool.memset(ks[u][:], 1.0).then_inc(s_init, 1)
                    pool.memset(vp[u][:], 0.0).then_inc(s_init, 1)
                wait(pool, s_init, 4)
                for u in range(2):
                    pool.memset(vp[u][:, :, :, E:E + 1], 1.0).then_inc(s_init, 1)

                def body(it, first, last):
                    for u in range(2):
                        b = it * 2 + u
                        wait(pool, s_pv, (b - 1) * (G * C))
                        for c in range(C):
                            pool.tensor_copy(vp[u][:, c, :, 0:E],
                                             k.v_all[:, bass.ds(b * (C * D) + c * D, D)].rearrange("p (h e) -> p h e", h=H)
                                             ).then_inc(s_vp, 1)

                paired(pool, body)

            @block.tensor
            def _(pe):
                def max_scores(i, n, x):
                    u, g = (i // G) % 2, i % G
                    if g == 0 and x == 0:
                        wait(pe, s_stk[u], (n - i) * (N_STACK // NG) + (i // NG + 1) * N_STACK)
                    qt, jj, half = x // 4, x // 2 % 2, x % 2
                    r, slot = 64 * half, 2 * g + jj
                    wait(pe, s_mr, n * 16 + x - 1)
                    pe.matmul(b_m[x % 2][:], qs[u][r:r + KR, slot, qt * P:(qt + 1) * P], ks[u][r:r + KR, slot, :],
                              start=True, stop=True).then_inc(s_m, 1)

                def turn_maxima(i, n):
                    wait(pe, s_mn, n + 1)
                    wait(pe, s_fh, n - 1 - G)
                    pe.transpose(b_misc[0:4 * C, 0:P // 2].bitcast(BF16), mneg[:, i % 2, :], k.identb[:]).then_inc(s_mt, 1)

                def scores(i, n, kt, x):
                    u, g = i // G, i % G
                    if kt == 0 and x == 0:
                        wait(pe, s_row[i % 2], (n - i % 2) * 16 + 32)
                    wait(pe, s_e, n * 8 + 2 * kt + x - 1)
                    for half in range(2):
                        r, slot = 64 * half, 2 * g + x
                        last = pe.matmul(b_s[x][:, half * L:(half + 1) * L],
                                         ks[u][r:r + KR + 1, slot, kt * P:(kt + 1) * P],
                                         qs[u][r:r + KR + 1, slot, :], start=True, stop=True)
                    last.then_inc(s_s, 1)

                def values(i, n, kt):
                    u, g = i // G, i % G
                    wait(pe, s_e, n * 8 + 2 * kt + 2)
                    if kt == 0:
                        wait(pe, s_ne, n)
                        if g == 0:
                            wait(pe, s_vp, n * 1 + C)
                    for q in range(GH):
                        last = pe.matmul(b_num[VW * q:VW * (q + 1), :], vp[u][:, kt, GH * g + q, :],
                                         pt[:, kt % 2, q % 2, (q // 2) * L:(q // 2 + 1) * L],
                                         start=(kt == 0), stop=(kt == C - 1), tile_position=(0, VW * q),
                                         skip_group_check=True)
                    last.then_inc(s_pv, 1)

                def finish(i, n, step, turns):
                    u, c = (i // G + 1) % 2, i % G
                    f = n - G
                    if step == 0:
                        wait(pe, s_ne, n - c)
                        wait(pe, s_fh, f)
                        if turns:
                            wait(pe, s_mc, n + 2)
                        for g in range(G):
                            last = pe.transpose(b_misc[:, g * P:(g + 1) * P], nt[:, u, g, c * P:(c + 1) * P], k.ident)
                        last.then_inc(s_ft, 1)
                    elif step == 1:
                        wait(pe, s_fo, f + 1)
                        pe.transpose(b_misc[:, 0:P], on[:, c % 2, :], k.ident).then_inc(s_fb, 1)
                    else:
                        wait(pe, s_fe, f + 1)
                        pe.matmul(b_misc[:, 0:P], ot[:, c % 2, :], k.wproj[:], start=True, stop=True).then_inc(s_fp, 1)

                def body(it, first, last):
                    for i in range(NG):
                        n = it * NG + i
                        ahead = not (last and i + 2 >= NG)
                        behind = not (first and i < G)
                        for kt in range(C):
                            scores(i, n, kt, 0)
                            if ahead:
                                max_scores(i + 2, n + 2, 4 * kt)
                            scores(i, n, kt, 1)
                            if ahead:
                                max_scores(i + 2, n + 2, 4 * kt + 1)
                            if kt == 0 and not (last and i + 1 >= NG):
                                turn_maxima(i + 1, n + 1)
                            if kt and behind:
                                finish(i, n, kt - 1, not (last and i == NG - 1))
                            if ahead:
                                max_scores(i + 2, n + 2, 4 * kt + 2)
                            if kt:
                                values(i, n, kt - 1)
                            if ahead:
                                max_scores(i + 2, n + 2, 4 * kt + 3)
                        values(i, n, C - 1)

                wait(pe, s_init, 6)
                for n in range(2):
                    for x in range(16):
                        max_scores(n, n, x)
                turn_maxima(0, 0)
                paired(pe, body)
                for c in range(C):
                    for step in range(3):
                        finish(c, B * G + c, step, False)

            @block.vector
            def _(dve):
                def maximum(i, n, x):
                    qt, jj, half = x // 4, x // 2 % 2, x % 2
                    col = half * 8 + jj * 4 + qt
                    wait(dve, s_m, n * 16 + x + 1)
                    dve.reduce_max(mx[:, i % 2, col:col + 1], b_m[x % 2][:], AX).then_inc(s_mr, 1)

                def negate(i, n):
                    wait(dve, s_mr, n * 16 + 16)
                    wait(dve, s_mt, n - 1)
                    dve.tensor_scalar(mneg[:, i % 2, :], mx[:, i % 2, :], -1.0, None, ALU.mult).then_inc(s_mn, 1)

                def maxima_out(i, n):
                    wait(dve, s_mt, n + 1)
                    wait(dve, s_row[i % 2], (n - i % 2) * 16)
                    dve.tensor_copy(mt[:, i % 2, :], b_misc[0:4 * C, 0:P // 2].bitcast(BF16)).then_inc(s_mc, 1)

                def normalise(i, n):
                    c, f = i % G, n - G
                    heads = b_misc[:].rearrange("p (h w) -> p h w", h=H)
                    wait(dve, s_ft, f + 1)
                    dve.tensor_copy(den[:, c % 2, :], heads[:, :, E]).then_inc(s_fd, 1)
                    wait(dve, s_fd, f + 1)
                    dve.reciprocal(den[:, c % 2, :], den[:, c % 2, :]).then_inc(s_fr, 1)
                    wait(dve, s_fr, f + 1)
                    dve.tensor_tensor(on[:, c % 2, :].rearrange("p (h e) -> p h e", h=H), heads[:, :, 0:E],
                                      den[:, c % 2, :].unsqueeze(2).to_broadcast([P, H, E]), ALU.mult).then_inc(s_fo, 1)

                def add(i, n):
                    f = n - G
                    wait(dve, s_fp, f + 1)
                    y = k.h_all[:, bass.ds(f * D, D)]
                    dve.tensor_tensor(y, y, b_misc[:, 0:P], ALU.add).then_inc(s_fh, 1)

                def body(it, first, last):
                    for i in range(NG):
                        n = it * NG + i
                        ahead = not (last and i + 2 >= NG)
                        behind = not (first and i < G)
                        for kt in range(C):
                            if ahead:
                                maximum(i + 2, n + 2, 4 * kt)
                                maximum(i + 2, n + 2, 4 * kt + 1)
                            if kt == 0 and not (last and i + 1 >= NG):
                                maxima_out(i + 1, n + 1)
                            if kt == 1 and behind:
                                normalise(i, n)
                            if kt == 3 and behind:
                                add(i, n)
                            if ahead:
                                maximum(i + 2, n + 2, 4 * kt + 2)
                                maximum(i + 2, n + 2, 4 * kt + 3)
                        if ahead:
                            negate(i + 2, n + 2)

                for n in range(2):
                    for x in range(16):
                        maximum(n, n, x)
                    negate(n, n)
                maxima_out(0, 0)
                paired(dve, body)
                for c in range(C):
                    normalise(c, B * G + c)
                    add(c, B * G + c)

            @block.scalar
            def _(act):
                def probs(i, n, kt, x):
                    wait(act, s_s, n * 8 + 2 * kt + x + 1)
                    if x == 0:
                        wait(act, s_pv, n * C + kt - 1)
                    act.activation(pt[:, kt % 2, x, :], b_s[x][:], ACT.Exp, scale=SCALE).then_inc(s_e, 1)

                def output_out(i, n):
                    wait(act, s_fb, n - G + 1)
                    act.activation(ot[:, i % 2, :], b_misc[:, 0:P], ACT.Copy).then_inc(s_fe, 1)

                def numerators_out(i, n):
                    wait(act, s_pv, n * C + C)
                    act.activation(nt[:, i // G, i % G, :], b_num[:], ACT.Copy).then_inc(s_ne, 1)

                def body(it, first, last):
                    for i in range(NG):
                        n = it * NG + i
                        for kt in range(C):
                            probs(i, n, kt, 0)
                            if kt == 3 and not (first and i < G):
                                output_out(i, n)
                            probs(i, n, kt, 1)
                        numerators_out(i, n)

                paired(act, body)
                for c in range(C):
                    output_out(c, B * G + c)


def route_phase(nc, k):
    with ExitStack() as ctx:
        def sb(name, shape, dt=F32):
            return ctx.enter_context(nc.sbuf_tensor(name, shape, dt))
        k.logits = sb("e_logits", [P, T * NE])
        k.slot_u = sb("e_slot_u", [P, T], U32)
        k.expert_i = sb("e_expert_i", [P, MT], I32)
        k.w1_all = k.parts[:].bitcast(F32)[:, 0:NE * HID]
        k.w2_all = k.parts[:].bitcast(F32)[:, NE * HID:2 * NE * HID]
        gate(nc, k)
        sort_tokens(nc, k)
        run_experts(nc, k)
        add_experts(nc, k)


def gate(nc, k):
    N = U4 * C
    with ExitStack() as ctx:
        def sb(name, shape, dt=F32):
            return ctx.enter_context(nc.sbuf_tensor(name, shape, dt))
        def sem(name):
            return ctx.enter_context(nc.semaphore(name))
        st = sb("e_st", [P, N, 6])
        mv = sb("e_mv", [P, N, 2])
        ve = sb("e_ve", [P, N])
        rs = sb("e_rs", [P, N])
        xn = sb("e_xn", [P, N * D])
        tmp = sb("e_tmp", [P, N * D])
        ht = sb("e_ht", [P, U4 * L])
        s_w = sem("e_weights_in")
        s_st, s_mv, s_ve, s_rs = sem("e_stats"), sem("e_means"), sem("e_variances"), sem("e_rstd")
        s_t1, s_xn, s_cp = sem("e_scaled"), sem("e_normed"), sem("e_normed_copied")
        s_tr, s_ht, s_gl, s_lg = sem("e_transposed"), sem("e_transposed_out"), sem("e_gate_products"), sem("e_logits_out")

        with nc.Block() as block:

            @block.sync
            def _(sp):
                for e in range(NE):
                    sp.dma_start(k.w1_all[:, e * HID:(e + 1) * HID], k.w1[e]).then_inc(s_w, 16)
                    sp.dma_start(k.w2_all[:, e * HID:(e + 1) * HID].rearrange("p (c d) -> p c d", c=HC),
                                 k.w2[e].rearrange("(c p) d -> p c d", p=P)).then_inc(s_w, 16)
                sp.wait_ge(s_w, 16 * 2 * NE)

            @block.vector
            def _(dve):
                with dve.Fori(0, B // U4) as it:
                    norm_stats(dve, k, st, mv, ve, lambda i: k.h_all[:, bass.ds(it * (N * D) + i * D, D)], N,
                               s_st, s_mv, s_ve, it * N, it * N)
                    for i in range(N):
                        dve.scalar_tensor_tensor(tmp[:, i * D:(i + 1) * D], k.h_all[:, bass.ds(it * (N * D) + i * D, D)],
                                                 mv[:, i, 0:1], k.L2W, ALU.subtract, ALU.mult).then_inc(s_t1, 1)
                    dve.wait_ge(s_rs, it + 1)
                    dve.wait_ge(s_t1, it * N + N)
                    for i in range(N):
                        dve.scalar_tensor_tensor(xn[:, i * D:(i + 1) * D], tmp[:, i * D:(i + 1) * D],
                                                 rs[:, i:i + 1], k.L2B, ALU.mult, ALU.add).then_inc(s_xn, 1)
                    for u in range(U4):
                        dve.wait_ge(s_gl, it * U4 + u + 1)
                        dve.tensor_tensor(k.tiles(k.logits[:, bass.ds((it * N + u * C) * NE, C * NE)], C),
                                          k.tiles(k.bank[4 + u][:, 0:C * NE], C), k.rep(k.gateb[:], C),
                                          ALU.add).then_inc(s_lg, 1)
                    dve.wait_ge(s_cp, it * U4 + U4)

            @block.gpsimd
            def _(pool):
                with pool.Fori(0, B // U4) as it:
                    pool.wait_ge(s_ve, it + 1)
                    pool.tensor_tensor(rs[:], ve[:], k.halfneg[:], ALU.pow).then_inc(s_rs, 1)

            @block.scalar
            def _(act):
                with act.Fori(0, B // U4) as it:
                    for u in range(U4):
                        act.wait_ge(s_tr, it * U4 + u + 1)
                        act.activation(ht[:, u * L:(u + 1) * L], k.bank[u][:], ACT.Copy).then_inc(s_ht, 1)
                        act.activation(k.fq_all[:, bass.ds(it * (N * D) + u * C * D, C * D)],
                                       xn[:, u * C * D:(u + 1) * C * D], ACT.Copy).then_inc(s_cp, 1)

            @block.tensor
            def _(pe):
                with pe.Fori(0, B // U4) as it:
                    for u in range(U4):
                        pe.wait_ge(s_xn, it * N + (u + 1) * C)
                        for c in range(C):
                            i = u * C + c
                            last = pe.transpose(k.bank[u][:, c * P:(c + 1) * P], xn[:, i * D:(i + 1) * D], k.ident)
                        last.then_inc(s_tr, 1)
                    for u in range(U4):
                        pe.wait_ge(s_ht, it * U4 + u + 1)
                        for c in range(C):
                            last = pe.matmul(k.bank[4 + u][:, c * NE:(c + 1) * NE],
                                             ht[:, u * L + c * P:u * L + (c + 1) * P], k.gatew[:],
                                             start=True, stop=True)
                        last.then_inc(s_gl, 1)


def sort_tokens(nc, k):
    with ExitStack() as ctx:
        def sb(name, shape, dt=F32):
            return ctx.enter_context(nc.sbuf_tensor(name, shape, dt))
        def sem(name):
            return ctx.enter_context(nc.semaphore(name))
        mx = sb("f_mx", [P, T])
        eq = sb("f_eq", [P, T, NE])
        oh = sb("f_onehot", [P, T, NE])
        tot = sb("f_tot", [P, T * NE])
        cum = [sb(f"f_cum{i}", [P, T * NE]) for i in range(2)]
        over = sb("f_over", [P, NE, T])
        used = sb("f_used", [P, NE])
        ends = [sb(f"f_ends{i}", [P, NE]) for i in range(2)]
        base = sb("f_base", [P, NE])
        row = sb("f_row", [P, T, NE])
        slot = sb("f_slot", [P, T])
        past = sb("f_past", [P, MT, NE])
        expert = sb("f_expert", [P, MT])
        s_oh, s_pr, s_v, s_slot, s_out = (sem("f_onehot_ready"), sem("f_products"), sem("f_vector_step"),
                                          sem("f_slots_ready"), sem("f_rows_written"))
        FIRST = k.cst[:, C_FIRST:C_FIRST + NE]
        STARTS = k.cst[:, C_TILES:C_TILES + T]
        INDEX = k.cst[:, C_J:C_J + MT]

        def flat(ap):
            return ap.rearrange("p t e -> p (t e)")

        def over_experts(ap, n):
            return ap.unsqueeze(2).to_broadcast([P, n, NE])

        with nc.Block() as block:

            @block.vector
            def _(dve):
                step = [0]

                def done(ins):
                    step[0] += 1
                    ins.then_inc(s_v, 1)

                def after():
                    dve.wait_ge(s_v, step[0])

                def running_sums(src, bufs, n, width):
                    d, i = 1, 0
                    while d < n:
                        dst, w = bufs[i % 2], d * width
                        done(dve.tensor_tensor(dst[:, w:], src[:, w:], src[:, :(n - d) * width], ALU.add))
                        done(dve.tensor_copy(dst[:, 0:w], src[:, 0:w]))
                        after()
                        src, d, i = dst, 2 * d, i + 1
                    return src

                lg = k.tiles(k.logits[:], T)
                done(dve.reduce_max(mx[:], lg, AX))
                after()
                done(dve.tensor_tensor(eq[:], lg, over_experts(mx[:], T), ALU.is_equal))
                after()
                done(dve.tensor_tensor(eq[:], eq[:], k.rep(FIRST, T), ALU.mult))
                after()
                done(dve.reduce_max(mx[:], eq[:], AX))
                after()
                dve.tensor_tensor(oh[:], eq[:], over_experts(mx[:], T), ALU.is_equal).then_inc(s_oh, 1)
                dve.wait_ge(s_pr, 1)
                done(dve.tensor_copy(tot[:], k.bank[1][:, 0:T * NE]))
                after()
                sums = running_sums(tot[:], [c[:] for c in cum], T, NE)
                count = sums[:, (T - 1) * NE:T * NE]
                done(dve.tensor_tensor(over[:], count.unsqueeze(2).to_broadcast([P, NE, T]), k.rep(STARTS, NE), ALU.is_gt))
                after()
                done(dve.reduce_sum(used[:], over[:], AX))
                after()
                end = running_sums(used[:], [c[:] for c in ends], NE, 1)
                done(dve.tensor_tensor(base[:], end, used[:], ALU.subtract))
                after()
                done(dve.tensor_scalar(base[:], base[:], float(P), None, ALU.mult))
                done(dve.tensor_tensor(flat(row[:]), k.bank[0][:, 0:T * NE], tot[:], ALU.subtract))
                after()
                done(dve.tensor_tensor(flat(row[:]), flat(row[:]), sums, ALU.add))
                after()
                done(dve.tensor_tensor(row[:], row[:], k.rep(base[:], T), ALU.add))
                after()
                done(dve.tensor_tensor(row[:], row[:], oh[:], ALU.mult))
                after()
                done(dve.reduce_sum(slot[:], row[:], AX))
                after()
                dve.tensor_copy(k.slot_u[:], slot[:]).then_inc(s_slot, 1)
                done(dve.tensor_tensor(past[:], over_experts(INDEX, MT), k.rep(end, MT), ALU.is_ge))
                after()
                done(dve.reduce_sum(expert[:], past[:], AX))
                after()
                done(dve.tensor_scalar(expert[:], expert[:], float(NE - 1), None, ALU.min))
                after()
                done(dve.tensor_copy(k.expert_i[:], expert[:]))
                after()

            @block.tensor
            def _(pe):
                pe.wait_ge(s_oh, 1)
                pe.matmul(k.bank[0][:, 0:T * NE], k.cst[:, C_BEFORE:C_BEFORE + P], flat(oh[:]), start=True, stop=True)
                pe.matmul(k.bank[1][:, 0:T * NE], k.cst[:, C_ONES:C_ONES + P], flat(oh[:]),
                          start=True, stop=True).then_inc(s_pr, 1)

            @block.gpsimd
            def _(pool):
                pool.wait_ge(s_slot, 1)
                for t in range(T):
                    pool.indirect_dma_start(k.xs_dram, bass.IndirectOffsetOnAxis(ap=k.slot_u[:, t:t + 1], axis=0),
                                            k.fq_all[:, t * D:(t + 1) * D], None).then_inc(s_out, 16)
                pool.wait_ge(s_out, 16 * T)


R3 = 3


def run_experts(nc, k):
    with ExitStack() as ctx:
        def sb(name, shape, dt=F32):
            return ctx.enter_context(nc.sbuf_tensor(name, shape, dt))
        def sem(name):
            return ctx.enter_context(nc.semaphore(name))
        xin = [sb(f"g_in{i}", [P, D]) for i in range(R3)]
        xt = [sb(f"g_xt{i}", [P, P]) for i in range(R3)]
        w1c = [sb(f"g_w1_{i}", [P, HID]) for i in range(R3)]
        hid = [sb(f"g_hid{i}", [P, HC * P]) for i in range(R3)]
        yo = [sb(f"g_out{i}", [P, D]) for i in range(R3)]
        s_in = [sem(f"g_tile_in{i}") for i in range(R3)]
        s_st = [sem(f"g_tile_stored{i}") for i in range(R3)]
        s_t, s_xt, s_w1, s_up, s_g, s_dn, s_yo = (sem("g_transposed"), sem("g_xt_ready"), sem("g_w1_ready"),
                                                  sem("g_up_products"), sem("g_hidden_ready"),
                                                  sem("g_down_products"), sem("g_tile_out"))
        b_up = [k.bank[i] for i in range(R3)]
        b_dn = [k.bank[R3 + i] for i in range(R3)]
        b_t = k.bank[2 * R3]
        ITS = MT // R3

        def staged(eng, body):
            for u in range(R3):
                body(0, u, u, True, False)
            with eng.Fori(1, ITS - 1) as it:
                for u in range(R3):
                    body(it, it * R3 + u, u, False, False)
            for u in range(R3):
                body(ITS - 1, (ITS - 1) * R3 + u, u, False, True)

        def expert_of(eng, j):
            return eng.value_load(k.expert_i[0:1, bass.ds(j, 1)], min_val=0, max_val=NE - 1)

        with nc.Block() as block:

            @block.sync
            def _(sp):
                def load(it, j, u, first, last):
                    wait(sp, s_t, j - R3 + 1)
                    sp.dma_start(xin[u][:], k.xs_dram[bass.ds(j * P, P), :]).then_inc(s_in[u], 16)
                staged(sp, load)

            @block.tensor
            def _(pe):
                def turn(it, j, u):
                    wait(pe, s_in[u], it * 16 + 16)
                    wait(pe, s_xt, j)
                    pe.transpose(b_t[:, 0:P], xin[u][:], k.ident).then_inc(s_t, 1)

                def up(j, u):
                    wait(pe, s_xt, j + 1)
                    wait(pe, s_w1, j + 1)
                    for c in range(HC):
                        last = pe.matmul(b_up[u][:, c * P:(c + 1) * P], w1c[u][:, c * P:(c + 1) * P], xt[u][:],
                                         start=True, stop=True)
                    last.then_inc(s_up, 1)

                def down(j, u):
                    e = expert_of(pe, j)
                    wait(pe, s_g, j + 1)
                    wait(pe, s_yo, j - R3 + 1)
                    for c in range(HC):
                        last = pe.matmul(b_dn[u][:, 0:D], hid[u][:, c * P:(c + 1) * P],
                                         k.w2_all[:, bass.ds(e * HID + c * D, D)], start=(c == 0), stop=(c == HC - 1))
                    last.then_inc(s_dn, 1)

                def body(it, j, u, first, last):
                    up(j, u)
                    if not (last and u == R3 - 1):
                        turn(it + (u + 1) // R3, j + 1, (u + 1) % R3)
                    if not (first and u == 0):
                        down(j - 1, (u - 1) % R3)

                turn(0, 0, 0)
                staged(pe, body)
                down(MT - 1, R3 - 1)

            @block.vector
            def _(dve):
                def out(it, j, u):
                    wait(dve, s_dn, j + 1)
                    wait(dve, s_st[u], it * 16 + 16)
                    dve.tensor_copy(yo[u][:], b_dn[u][:, 0:D]).then_inc(s_yo, 1)

                def body(it, j, u, first, last):
                    e = expert_of(dve, j)
                    wait(dve, s_up, j - R3 + 1)
                    dve.tensor_copy(w1c[u][:], k.w1_all[:, bass.ds(e * HID, HID)]).then_inc(s_w1, 1)
                    wait(dve, s_t, j + 1)
                    dve.tensor_copy(xt[u][:], b_t[:, 0:P]).then_inc(s_xt, 1)
                    if not (first and u < 2):
                        out(it - (u < 2), j - 2, (u - 2) % R3)

                staged(dve, body)
                for j in (MT - 2, MT - 1):
                    out(j // R3, j, j % R3)

            @block.scalar
            def _(act):
                def store(j, u):
                    wait(act, s_yo, j + 1)
                    act.dma_start(k.ys_dram[bass.ds(j * P, P), :], yo[u][:]).then_inc(s_st[u], 16)

                def body(it, j, u, first, last):
                    wait(act, s_up, j + 1)
                    act.activation(hid[u][:], b_up[u][:], ACT.Gelu_apprx_tanh).then_inc(s_g, 1)
                    if not (first and u < 2):
                        store(j - 2, (u - 2) % R3)

                for u in range(R3):
                    act.sem_inc(s_st[u], 16)
                staged(act, body)
                for j in (MT - 2, MT - 1):
                    store(j, j % R3)
                for u in range(R3):
                    act.wait_ge(s_st[u], 16 * ITS + 16)


def add_experts(nc, k):
    with ExitStack() as ctx:
        def sem(name):
            return ctx.enter_context(nc.semaphore(name))
        s_g = [sem(f"h_gathered{b}") for b in range(B)]
        s_y, s_m, s_o, s_out = sem("h_summed"), sem("h_gated"), sem("h_ready"), sem("h_stored")
        with nc.Block() as block:

            @block.gpsimd
            def _(pool):
                for t in range(T):
                    pool.indirect_dma_start(k.v_all[:, t * D:(t + 1) * D], None, k.ys_dram,
                                            bass.IndirectOffsetOnAxis(ap=k.slot_u[:, t:t + 1], axis=0)
                                            ).then_inc(s_g[t // C], 16)

            @block.vector
            def _(dve):
                for b in range(B):
                    cols = slice(b * C * D, (b + 1) * C * D)
                    m = k.tiles(k.v_all[:, cols], C)
                    dve.wait_ge(s_g[b], 16 * C)
                    dve.tensor_tensor(m, m, k.tiles(k.h_all[:, cols], C), ALU.add).then_inc(s_y, 1)
                    dve.wait_ge(s_y, b + 1)
                    dve.tensor_tensor(m, m, k.rep(k.gb_all[:, b * D:(b + 1) * D], C), ALU.mult).then_inc(s_m, 1)
                    dve.wait_ge(s_m, b + 1)
                    dve.tensor_tensor(m, m, k.tiles(k.x_all[:, cols], C), ALU.add).then_inc(s_o, 1)

            @block.sync
            def _(sp):
                ov = k.out.rearrange("b (c p) d -> p b c d", p=P)
                for b in range(B):
                    sp.wait_ge(s_o, b + 1)
                    sp.dma_start(ov[:, b], k.tiles(k.v_all[:, b * C * D:(b + 1) * C * D], C)).then_inc(s_out, 16)
                sp.wait_ge(s_out, 16 * B)


_INS = ['L0_attn_x', 'L0_attn_Wqkv', 'L0_attn_bqkv', 'L0_attn_Wout', 'L0_attn_bout', 'L0_attn_gamma', 'L0_attn_beta',
        'L0_ffn_ln1_w', 'L0_ffn_ln1_b', 'L0_ffn_w_qkv', 'L0_ffn_w_proj', 'L0_ffn_ln2_w', 'L0_ffn_ln2_b',
        'L0_ffn_gate_w', 'L0_ffn_gate_b', 'L0_ffn_w1', 'L0_ffn_w2', 'L0_c', 'L0_wmod']


def constants():
    import numpy as np
    c = np.zeros((P, C_ALL), np.float32)
    p = np.arange(P)[:, None]
    m = np.arange(P)[None, :]
    pos = np.arange(H)[None, :]
    c[:, C_ID:C_ID + P] = p == m
    c[:, C_CAUSAL:C_CAUSAL + P] = p <= m
    slot_position = 2 * GH * (p % S // GH) + GH * (p // 64) + p % S % GH
    c[:, C_HMASK:C_HMASK + H] = slot_position == pos
    c[:, C_BEFORE:C_BEFORE + P] = p < m
    c[:, C_ONES:C_ONES + P] = 1.0
    c[:, C_TILES:C_TILES + T] = P * np.arange(T)
    c[:, C_J:C_J + MT] = np.arange(MT)
    c[:, C_FIRST:C_FIRST + NE] = NE - np.arange(NE)
    return c


def kernel(**inputs):
    import numpy as _np
    import concourse.bacc as _bacc
    from concourse import mybir as _mybir
    from concourse.bass_utils import run_bass_kernel_spmd as _run

    nc = _bacc.Bacc("TRN2", target_bir_lowering=False, num_devices=1)
    arrays, args = {}, []
    for name, a in [(n, inputs[n]) for n in _INS] + [("consts", constants())]:
        a = _np.ascontiguousarray(a)
        arrays[f"in_{name}_dram"] = a
        args.append(nc.dram_tensor(f"in_{name}_dram", a.shape, _mybir.dt.from_np(a.dtype), kind="ExternalInput").ap())
    out = nc.dram_tensor("out_0_dram", (B, L, D), F32, kind="ExternalOutput").ap()
    adaln_kernel(nc, *args, out)
    r = _run(nc, [arrays], core_ids=[0])
    return r.results[0]["out_0_dram"]
```

```python
import concourse.bass as bass
from concourse import mybir
from contextlib import ExitStack

F32 = mybir.dt.float32
BF16 = mybir.dt.bfloat16
I32 = mybir.dt.int32
U32 = mybir.dt.uint32
ALU = mybir.AluOpType
ACT = mybir.ActivationFunctionType
AX = mybir.AxisListType.X

P = 128
B = 8
L = 512
D = 128
H = 16
E = D // H
C = L // P
T = B * C
NE = 8
HID = 4 * D
HC = HID // P
MT = T + NE - 1
G = 4
GH = H // G
VW = 32
S = H // 2
KR = 6 * E
LN_EPS = 1e-5
FEAT_EPS = 1e-4
NM = 6
Q_PART = (0, 0, 0, 1, 1, 2)
K_PART = (0, 1, 2, 0, 1, 0)
LIN_HALF = [(p // GH) % 2 for p in range(H)]
LIN_SLOT = [GH * (p // (2 * GH)) + p % GH for p in range(H)]
SOFT_HALF = [(p % GH) // 2 for p in range(H)]
SOFT_SLOT = [2 * (p // GH) + p % 2 for p in range(H)]
C_ID, C_CAUSAL, C_HMASK, C_BEFORE, C_ONES = 0, P, 2 * P, 2 * P + H, 3 * P + H
C_TILES = 4 * P + H
C_J = C_TILES + T
C_FIRST = C_J + MT
C_ALL = C_FIRST + NE


class Buffers:
    pass


def adaln_kernel(nc, x, wqkv, bqkv, wout, bout, gamma, beta, ln1_w, ln1_b, w_qkv, w_proj,
                 ln2_w, ln2_b, gate_w, gate_b, w1, w2, c_in, wmod, consts, out):
    k = Buffers()
    (k.x, k.wqkv, k.bqkv, k.wout, k.bout, k.gamma, k.beta,
     k.ln1_w, k.ln1_b, k.w_qkv, k.w_proj, k.ln2_w, k.ln2_b,
     k.gate_w, k.gate_b, k.w1, k.w2, k.c_in, k.wmod, k.consts, k.out) = (
        x, wqkv, bqkv, wout, bout, gamma, beta, ln1_w, ln1_b, w_qkv, w_proj, ln2_w, ln2_b,
        gate_w, gate_b, w1, w2, c_in, wmod, consts, out)
    top = ExitStack()
    with top:
        def sb(name, shape, dt=F32, ctx=top):
            return ctx.enter_context(nc.sbuf_tensor(name, shape, dt))

        k.bank = [top.enter_context(nc.psum_tensor(f"bank{i}", [P, 4 * P], F32)) for i in range(4)]
        k.pair = [top.enter_context(nc.psum_tensor(f"pair{i}", [P, 8 * P], F32)) for i in range(2)]
        k.bank += [k.pair[0][:, 0:512], k.pair[0][:, 512:1024], k.pair[1][:, 0:512], k.pair[1][:, 512:1024]]

        k.x_all = sb("x_all", [P, T * D])
        k.v_all = sb("v_all", [P, T * D])
        k.fq_all = sb("fq_all", [P, B * L])
        k.h_all = sb("h_all", [P, T * D])
        k.qs = [sb(f"q_stack{i}", [P, S, L], BF16) for i in range(2)]
        k.ks = [sb(f"k_stack{i}", [P, 2, S, L], BF16) for i in range(2)]
        k.vp = [sb(f"values{i}", [P, C, H, E + 1]) for i in range(2)]
        k.s_stk = [top.enter_context(nc.semaphore(f"stacks{i}")) for i in range(2)]
        k.mod4 = sb("mod4", [P, 4 * B * D])
        k.gb_all = sb("gb_all", [P, B * D])
        k.G_OF, k.B_OF, k.CB_OF, k.SB_OF = 0, B * D, 2 * B * D, 3 * B * D
        k.cst = sb("cst", [P, C_ALL])
        k.ident = k.cst[:, C_ID:C_ID + P]
        k.causal = k.cst[:, C_CAUSAL:C_CAUSAL + P]
        k.hmask = k.cst[:, C_HMASK:C_HMASK + H]
        k.wlt = sb("wlt", [P, 3 * D])
        k.woutt = sb("woutt", [P, D])
        k.wsm = sb("wsm", [P, 3 * D])
        k.wproj = sb("wproj", [P, D])
        k.gatew = sb("gatew", [P, NE])
        k.bq2 = sb("bq2", [P, 4])
        k.lnw = sb("lnw", [P, 2])
        k.ca1t = sb("ca1t", [P, B])
        k.sat = sb("sat", [P, B])
        k.rows = sb("rows", [P, 4 * D])
        k.BV, k.BO, k.L2W, k.L2B = (k.rows[:, i * D:(i + 1) * D] for i in range(4))
        k.gateb = sb("gateb", [P, NE])
        k.spare = sb("spare", [P, 1])
        k.halfneg = sb("halfneg", [P, 4 * C])

        def tiles(ap, n):
            return ap.rearrange("p (c d) -> p c d", c=n)

        def rep(ap, n):
            return ap.unsqueeze(1).to_broadcast([P, n, ap.shape[1]])

        k.parts_dram = nc.dram_tensor("bf16_parts", [B, 6, P, L], BF16).ap()
        k.xs_dram = nc.dram_tensor("experts_in", [MT * P, D], F32).ap()
        k.ys_dram = nc.dram_tensor("experts_out", [MT * P, D], F32).ap()

        k.tiles, k.rep = tiles, rep
        setup_phase(nc, k)
        linear_prepare(nc, k)
        linear_attend(nc, k)
        softmax_prepare(nc, k)
        softmax_attend(nc, k)
        route_phase(nc, k)


def setup_phase(nc, k):
    with ExitStack() as ctx:
        def sb(name, shape, dt=F32):
            return ctx.enter_context(nc.sbuf_tensor(name, shape, dt))
        def sem(name):
            return ctx.enter_context(nc.semaphore(name))
        wl_raw = sb("wl_raw", [P, 3, D])
        wo_raw = sb("wo_raw", [P, D])
        wo_pos = sb("wo_pos", [P, D])
        bv_raw = sb("bv_raw", [P, D])
        ws_raw = sb("ws_raw", [P, 3 * D])
        c_raw = sb("c_raw", [B, D])
        c_exp = sb("c_exp", [B, D])
        c_rec = sb("c_rec", [B, D])
        c_silu = sb("c_silu", [B, D])
        ct = sb("ct", [P, B])
        ctb = sb("ctb", [P, B, P])
        wm = sb("wm", [P, NM * D])
        gamma_r = sb("gamma_r", [P, D])
        beta_r = sb("beta_r", [P, D])
        mraw = sb("mraw", [P, B, 4 * D])
        sgn = sb("sgn", [P, 2, B * D])
        mag = sb("mag", [P, 2, B * D])
        zero = sb("zero", [P, D])
        s_w = sem("weights_in")
        s_x = sem("x_in")
        s_v = sem("vector_step")
        s_e = sem("silu_exp")
        s_t = sem("transposed")
        s_m = sem("modulation_ready")
        s_me = sem("modulation_copied")
        s_z = sem("zero_ready")
        s_zd = sem("zeros_written")

        def row(ap, n):
            return ap.rearrange("(o d) -> o d", o=1).to_broadcast([P, n])

        loads = [
            (k.cst[:], k.consts),
            (c_raw[:], k.c_in),
            (wm[:], k.wmod),
            (wo_raw[:], k.wout),
            (ws_raw[:], k.w_qkv),
            (k.gatew[:], k.gate_w),
            (gamma_r[:], row(k.gamma, D)),
            (beta_r[:], row(k.beta, D)),
            (bv_raw[:], row(k.bqkv[2 * D:3 * D], D)),
            (k.BO, row(k.bout, D)),
            (k.L2W, row(k.ln2_w, D)),
            (k.L2B, row(k.ln2_b, D)),
            (k.gateb[:], row(k.gate_b, NE)),
            (k.lnw[:, 0:1], k.ln1_w.rearrange("(d o) -> d o", o=1)),
            (k.lnw[:, 1:2], k.ln1_b.rearrange("(d o) -> d o", o=1)),
        ]
        for z in range(2):
            for half in range(2):
                rows_of = k.wqkv[z * D:(z + 1) * D, :].rearrange("(s h e) d -> h e s d", h=2, e=E)
                bias_of = k.bqkv[z * D:(z + 1) * D].rearrange("(s h e o) -> h e s o", h=2, e=E, o=1)
                loads.append((wl_raw[64 * half:64 * half + 64, z, :], rows_of[half]))
                loads.append((k.bq2[64 * half:64 * half + 64, z:z + 1], bias_of[half]))
        for p in range(0, H, GH):
            vrows = k.wqkv[2 * D:3 * D, :].rearrange("(j h e) d -> h j e d", h=2, e=E)
            loads.append((wl_raw[E * p:E * (p + GH), 2, :], vrows[LIN_HALF[p], LIN_SLOT[p]:LIN_SLOT[p] + GH]))
            for half in range(2):
                prow = k.w_proj.rearrange("(j h e) d -> h j e d", h=2, e=E)
                q = p + 2 * half
                loads.append((k.wproj[E * q:E * (q + 2), :], prow[half, SOFT_SLOT[q]:SOFT_SLOT[q] + 2]))
        NL = len(loads)
        with nc.Block() as block:

            @block.sync
            def _(sp):
                with nc.allow_non_contiguous_dma("columns of biases"):
                    for dst, src in loads:
                        sp.dma_start(dst, src).then_inc(s_w, 16)
                xv = k.x.rearrange("b (c p) d -> p (b c) d", p=P)
                for i in range(4):
                    sp.dma_start(k.tiles(k.x_all[:], T)[:, i * C * 2:(i + 1) * C * 2, :],
                                 xv[:, i * C * 2:(i + 1) * C * 2, :]).then_inc(s_x, 16)
                sp.wait_ge(s_z, 1)
                sp.dma_start(k.xs_dram.rearrange("(j p) d -> p j d", p=P), k.rep(zero[:], MT)).then_inc(s_zd, 16)
                sp.wait_ge(s_x, 64)
                sp.wait_ge(s_zd, 16)

            @block.gpsimd
            def _(pool):
                pool.memset(zero[:], 0.0).then_inc(s_z, 1)
                pool.memset(k.halfneg[:], -0.5)
                for u in range(2):
                    pool.memset(k.qs[u][:], 0.0).then_inc(s_z, 1)
                for u in range(2):
                    pool.memset(k.vp[u][:], 1.0).then_inc(s_z, 1)
                pool.wait_ge(s_v, 2)
                pool.wait_ge(s_z, 5)
                pool.memset(k.ks[1][32:64, 0], 1.0)
                pool.memset(k.ks[1][96:128, 1], 1.0)

            @block.scalar
            def _(act):
                act.wait_ge(s_w, 16 * NL)
                act.activation(c_exp[:], c_raw[:], ACT.Exp, scale=-1.0).then_inc(s_e, 1)
                for b in range(B):
                    act.wait_ge(s_m, b + 2)
                    act.activation(mraw[:, b, :], k.bank[b % 2][:], ACT.Copy).then_inc(s_me, 1)

            @block.tensor
            def _(pe):
                pe.wait_ge(s_w, 16 * NL)
                for z in range(3):
                    pe.transpose(k.bank[0][:, z * P:(z + 1) * P], wl_raw[:, z, :], k.ident).then_inc(s_t, 1)
                pe.wait_ge(s_v, 11)
                pe.transpose(k.bank[0][:, 3 * P:4 * P], wo_pos[:], k.ident).then_inc(s_t, 1)
                pe.transpose(k.bank[1][:, 0:B], c_silu[:], k.ident[0:B, 0:B]).then_inc(s_t, 1)
                pe.wait_ge(s_v, 17)
                for j in range(2):
                    last = pe.matmul(k.bank[2][:, j * B:(j + 1) * B], wm[:, j * D:(j + 1) * D], ct[:],
                                     start=True, stop=True)
                last.then_inc(s_m, 1)
                for b in range(B):
                    if b >= 2:
                        pe.wait_ge(s_me, b - 1)
                    pe.matmul(k.bank[b % 2][:], ctb[:, b, :], wm[:, 2 * D:NM * D],
                              start=True, stop=True).then_inc(s_m, 1)

            @block.vector
            def _(dve):
                step = [0]

                def done(ins):
                    step[0] += 1
                    ins.then_inc(s_v, 1)

                def after(n=None):
                    dve.wait_ge(s_v, step[0] if n is None else n)

                for u in range(2):
                    done(dve.memset(k.ks[u][:], 0.0))
                after()
                done(dve.memset(k.ks[0][32:64, 0], 1.0))
                done(dve.memset(k.ks[0][96:128, 1], 1.0))
                dve.wait_ge(s_e, 1)
                done(dve.tensor_scalar(c_exp[:], c_exp[:], 1.0, None, ALU.add))
                after()
                done(dve.reciprocal(c_rec[:], c_exp[:]))
                after()
                done(dve.tensor_tensor(c_silu[:], c_raw[:], c_rec[:], ALU.mult))
                dve.wait_ge(s_w, 16 * NL)
                for half in range(2):
                    for dst, src in ((wo_pos[:], wo_raw[:]), (k.BV, bv_raw[:])):
                        done(dve.tensor_copy(
                            dst.rearrange("p (a h f) -> p a h f", a=2, h=2)[:, :, half, :].rearrange("p a (j e) -> p a j e", e=E),
                            src.rearrange("p (a j h e) -> p a j h e", a=2, h=2, e=E)[:, :, :, half, :]))
                dve.wait_ge(s_t, 5)
                done(dve.tensor_copy(k.wlt[:], k.bank[0][:, 0:3 * P]))
                done(dve.tensor_copy(k.woutt[:], k.bank[0][:, 3 * P:4 * P]))
                dve.wait_ge(s_w, 16 * NL)
                done(dve.tensor_scalar(k.bq2[:, 2:4], k.bq2[:, 0:2], FEAT_EPS, None, ALU.add))
                done(dve.tensor_copy(ct[:], k.bank[1][:, 0:B]))
                after()
                done(dve.tensor_copy(ctb[:, 0:4, :], ct[:, 0:4].unsqueeze(2).to_broadcast([P, 4, P])))
                done(dve.tensor_copy(ctb[:, 4:8, :], ct[:, 4:8].unsqueeze(2).to_broadcast([P, 4, P])))
                for z in range(2):
                    for half in range(2):
                        done(dve.tensor_copy(
                            k.wsm[:, z * D + 64 * half:z * D + 64 * half + 64].rearrange("p (e s) -> p s e", e=E),
                            ws_raw[:, z * D:(z + 1) * D].rearrange("p (s h e) -> p s h e", h=2, e=E)[:, :, half, :]))
                for half in range(2):
                    done(dve.tensor_copy(
                        k.wsm[:, 2 * D:3 * D].rearrange("p (g h j e) -> p g h j e", g=G, h=2, e=E)[:, :, half],
                        ws_raw[:, 2 * D:3 * D].rearrange("p (g j h e) -> p g j h e", g=G, h=2, e=E)[:, :, :, half, :]))
                dve.wait_ge(s_m, 1)
                done(dve.tensor_copy(k.sat[:], k.bank[2][:, 0:B]))
                done(dve.tensor_scalar(k.ca1t[:], k.bank[2][:, B:2 * B], 1.0, None, ALU.add))
                dve.wait_ge(s_me, B)
                for i, j in enumerate((0, 3)):
                    g = mraw[:, :, j * D:(j + 1) * D]
                    sg = sgn[:, i, :].rearrange("p (b d) -> p b d", b=B)
                    mg = mag[:, i, :].rearrange("p (b d) -> p b d", b=B)
                    done(dve.tensor_scalar(sg, g, 0.0, 2.0, ALU.is_ge, ALU.mult))
                    after()
                    done(dve.tensor_scalar(sg, sg, -1.0, None, ALU.add))
                    after()
                    done(dve.tensor_tensor(mg, g, sg, ALU.mult))
                    after()
                    done(dve.tensor_scalar(mg, mg, 0.25, None, ALU.max))
                    after()
                    if i == 0:
                        done(dve.tensor_tensor(mg, mg, sg, ALU.mult))
                        after()
                        done(dve.tensor_tensor(k.tiles(k.mod4[:, 0:B * D], B), mg, k.rep(gamma_r[:], B), ALU.mult))
                        done(dve.tensor_tensor(k.tiles(k.mod4[:, B * D:2 * B * D], B), mg, k.rep(beta_r[:], B), ALU.mult))
                    else:
                        done(dve.tensor_tensor(k.tiles(k.gb_all[:], B), mg, sg, ALU.mult))
                done(dve.tensor_scalar(k.tiles(k.mod4[:, 2 * B * D:3 * B * D], B), mraw[:, :, 2 * D:3 * D], 1.0, None, ALU.add))
                done(dve.tensor_copy(k.tiles(k.mod4[:, 3 * B * D:4 * B * D], B), mraw[:, :, D:2 * D]))
                after()


def wait(eng, sem, value):
    if isinstance(value, int) and value <= 0:
        return
    eng.wait_ge(sem, value)


def paired(eng, body):
    body(0, True, False)
    with eng.Fori(1, B // 2 - 1) as it:
        body(it, False, False)
    body(B // 2 - 1, False, True)


U4 = 4


def part(parts, u, z, i):
    return parts[:, (6 * u + 3 * z + i) * L:(6 * u + 3 * z + i + 1) * L]


def store_parts(sp, k, parts, it, u, s_p3, s_ps):
    sp.wait_ge(s_p3, it * 2 * U4 + 2 * u + 4)
    sp.dma_start(k.parts_dram[bass.ds(it * U4 + u, 1)].rearrange("b z p l -> p (b z) l"),
                 k.tiles(parts[:, u * 6 * L:(u + 1) * 6 * L], 6)).then_inc(s_ps[u], 16)


STACK_LOADS = [(side, half, i) for i in range(3) for side in range(2) for half in range(2)]
N_STACK = len(STACK_LOADS) * 16


def load_stack(sp, k, u, b, side, half, i):
    rows, first = 3 - i, (0, 3, 5)[i]
    r = 64 * half + E * first
    dst = (k.ks[u][r:r + E * rows, half] if side else k.qs[u][r:r + E * rows]).rearrange("p s l -> p (s l)")
    src = k.parts_dram[bass.ds(b, 1)].rearrange("b (z i) (h e s) l -> z i h (b e) (s l)", z=2, h=2, e=E)[side]
    src = src[0:rows, half] if side else src[i:i + 1, half].to_broadcast([rows, E, S * L])
    sp.dma_start(dst, src).then_inc(k.s_stk[u], 16)


def norm_stats(dve, k, st, mv, ve, src, n, s_st, s_mv, s_ve, base_st, base_mv):
    dve.memset(k.spare[:], 0.0)
    for i in range(n):
        dve.bn_stats(st[:, i, :], src(i)).then_inc(s_st, 1)
    dve.wait_ge(s_st, base_st + n)
    dve.memset(k.spare[:], 0.0)
    for i in range(n):
        dve.bn_aggr(mv[:, i, :], st[:, i, :]).then_inc(s_mv, 1)
    dve.wait_ge(s_mv, base_mv + n)
    dve.tensor_scalar(ve[:], mv[:, :, 1], LN_EPS, None, ALU.add).then_inc(s_ve, 1)


def linear_prepare(nc, k):
    N = U4 * C
    with ExitStack() as ctx:
        def sb(name, shape, dt=F32):
            return ctx.enter_context(nc.sbuf_tensor(name, shape, dt))
        def sem(name):
            return ctx.enter_context(nc.semaphore(name))
        st = sb("a_st", [P, N, 6])
        mv = sb("a_mv", [P, N, 2])
        ve = sb("a_ve", [P, N])
        rs = sb("a_rs", [P, N])
        xn = sb("a_xn", [P, N * D])
        ht = sb("a_ht", [P, U4 * L])
        ex = sb("a_ex", [P, 2, L])
        rl = sb("a_rl", [P, 2, L])
        parts = sb("a_parts", [P, U4 * 6 * L], BF16)
        r1 = sb("a_r1", [P, 2, L])
        fk = sb("a_fk", [P, U4, L])
        s_st, s_mv, s_ve, s_rs = sem("a_stats"), sem("a_means"), sem("a_variances"), sem("a_rstd")
        s_xn, s_tr, s_ht = sem("a_normed"), sem("a_transposed"), sem("a_h_ready")
        s_pj, s_ex, s_rl, s_ph = sem("a_projected"), sem("a_exp"), sem("a_relu"), sem("a_features")
        s_p1, s_r1, s_p2, s_p3 = sem("a_part1"), sem("a_rest1"), sem("a_part2"), sem("a_part3")
        s_v, s_vc, s_kt, s_kc = sem("a_v"), sem("a_v_copied"), sem("a_k_transposed"), sem("a_k_copied")

        s_ps = [sem(f"a_parts_stored{u}") for u in range(U4)]

        with nc.Block() as block:

            @block.sync
            def _(sp):
                for u in range(U4):
                    sp.sem_inc(s_ps[u], 16)
                with sp.Fori(0, B // U4) as it:
                    for u in range(U4):
                        store_parts(sp, k, parts, it, u, s_p3, s_ps)
                for b in range(2):
                    sp.wait_ge(s_ps[b], 32)
                    for load in STACK_LOADS:
                        load_stack(sp, k, b, b, *load)
                for u in range(U4):
                    sp.wait_ge(s_ps[u], 16 * (B // U4) + 16)

            @block.vector
            def _(dve):
                with dve.Fori(0, B // U4) as it:
                    norm_stats(dve, k, st, mv, ve, lambda i: k.x_all[:, bass.ds(it * (N * D) + i * D, D)], N,
                               s_st, s_mv, s_ve, it * N, it * N)
                    dve.wait_ge(s_rs, it + 1)
                    for i in range(N):
                        if i == 0:
                            dve.wait_ge(s_tr, it * N + 1)
                        dve.tensor_scalar(xn[:, i * D:(i + 1) * D],
                                          k.x_all[:, bass.ds(it * (N * D) + i * D, D)],
                                          mv[:, i, 0:1], rs[:, i:i + 1], ALU.subtract, ALU.mult).then_inc(s_xn, 1)

                    def features(u):
                        for z in range(2):
                            n = 2 * u + z
                            dve.wait_ge(s_pj, it * 2 * U4 + n + 1)
                            dve.wait_ge(s_ex, it * 2 * U4 + n + 1)
                            dve.tensor_scalar(rl[:, z, :], k.bank[4 + 2 * (u % 2) + z][:], k.bq2[:, 2 + z:3 + z],
                                              FEAT_EPS, ALU.add, ALU.max).then_inc(s_rl, 1)
                        for z in range(2):
                            n = 2 * u + z
                            dve.wait_ge(s_rl, it * 2 * U4 + n + 1)
                            if z == 0:
                                f = k.fq_all[:, bass.ds(it * (U4 * L) + u * L, L)]
                            else:
                                f = fk[:, u, :]
                                if u == 0:
                                    dve.wait_ge(s_kt, it * U4 + 1)
                            dve.scalar_tensor_tensor(f, ex[:, z, :], 1.0, rl[:, z, :],
                                                     ALU.min, ALU.add).then_inc(s_ph, 1)
                        for z in range(2):
                            n = 2 * u + z
                            dve.wait_ge(s_ph, it * 2 * U4 + n + 1)
                            dve.wait_ge(s_p1, it * 2 * U4 + n + 1)
                            f = k.fq_all[:, bass.ds(it * (U4 * L) + u * L, L)] if z == 0 else fk[:, u, :]
                            dve.wait_ge(s_p3, it * 2 * U4 + n + 1)
                            dve.tensor_tensor(r1[:, z, :], f,
                                              part(parts, u, z, 0),
                                              ALU.subtract).then_inc(s_r1, 1)

                    features(0)
                    features(1)
                    for u in range(U4):
                        dve.wait_ge(s_v, it * U4 + u + 1)
                        dve.tensor_tensor(k.tiles(k.v_all[:, bass.ds(it * (N * D) + u * C * D, C * D)], C),
                                          k.tiles(k.bank[u][:], C), k.rep(k.BV, C), ALU.add).then_inc(s_vc, 1)
                    features(2)
                    features(3)

            @block.gpsimd
            def _(pool):
                pool.sem_inc(s_p3, 2)
                with pool.Fori(0, B // U4) as it:
                    pool.wait_ge(s_ve, it + 1)
                    pool.tensor_tensor(rs[:], ve[:], k.halfneg[:], ALU.pow).then_inc(s_rs, 1)
                    for n in range(2 * U4):
                        u, z = n // 2, n % 2
                        pool.wait_ge(s_p2, it * 2 * U4 + n + 1)
                        pool.tensor_tensor(part(parts, u, z, 2),
                                           r1[:, z, :],
                                           part(parts, u, z, 1),
                                           ALU.subtract).then_inc(s_p3, 1)

            @block.scalar
            def _(act):
                with act.Fori(0, B // U4) as it:
                    for u in range(U4):
                        act.wait_ge(s_tr, it * N + C * (u + 1) + 1)
                        act.activation(ht[:, u * L:(u + 1) * L], k.bank[u][:], ACT.Identity,
                                       bias=k.sat[:, bass.ds(it * U4 + u, 1)],
                                       scale=k.ca1t[:, bass.ds(it * U4 + u, 1)]).then_inc(s_ht, 1)

                    def features(u):
                        for z in range(2):
                            act.wait_ge(s_pj, it * 2 * U4 + 2 * u + z + 1)
                            act.activation(ex[:, z, :], k.bank[4 + 2 * (u % 2) + z][:], ACT.Exp,
                                           bias=k.bq2[:, z:z + 1]).then_inc(s_ex, 1)
                        for z in range(2):
                            n = 2 * u + z
                            f = k.fq_all[:, bass.ds(it * (U4 * L) + u * L, L)] if z == 0 else fk[:, u, :]
                            act.wait_ge(s_ph, it * 2 * U4 + n + 1)
                            if z == 0:
                                act.wait_ge(s_ps[u], it * 16 + 16)
                            act.activation(part(parts, u, z, 0),
                                           f, ACT.Copy).then_inc(s_p1, 1)
                        for z in range(2):
                            n = 2 * u + z
                            act.wait_ge(s_r1, it * 2 * U4 + n + 1)
                            act.activation(part(parts, u, z, 1),
                                           r1[:, z, :], ACT.Copy).then_inc(s_p2, 1)

                    for u in range(U4):
                        features(u)
                    for u in range(U4):
                        act.wait_ge(s_kt, it * U4 + u + 2)
                        act.activation(k.h_all[:, bass.ds(it * (N * D) + u * C * D, C * D)], k.bank[u][:],
                                       ACT.Copy).then_inc(s_kc, 1)

            @block.tensor
            def _(pe):
                pe.sem_inc(s_tr, 1)
                pe.sem_inc(s_kt, 1)
                with pe.Fori(0, B // U4) as it:
                    for u in range(U4):
                        for c in range(C):
                            i = u * C + c
                            pe.wait_ge(s_xn, it * N + i + 1)
                            pe.transpose(k.bank[u][:, c * P:(c + 1) * P], xn[:, i * D:(i + 1) * D],
                                         k.ident).then_inc(s_tr, 1)

                    def qk(u):
                        pe.wait_ge(s_ht, it * U4 + u + 1)
                        if u >= 2:
                            pe.wait_ge(s_rl, it * 2 * U4 + 2 * (u - 1))
                        for z in range(2):
                            pe.matmul(k.bank[4 + 2 * (u % 2) + z][:], k.wlt[:, z * D:(z + 1) * D],
                                      ht[:, u * L:(u + 1) * L], start=True, stop=True).then_inc(s_pj, 1)

                    qk(0)
                    qk(1)
                    for u in range(U4):
                        pe.wait_ge(s_ht, it * U4 + u + 1)
                        for c in range(C):
                            last = pe.matmul(k.bank[u][:, c * P:(c + 1) * P],
                                             ht[:, u * L + c * P:u * L + (c + 1) * P],
                                             k.wlt[:, 2 * D:3 * D], start=True, stop=True)
                        last.then_inc(s_v, 1)
                    qk(2)
                    qk(3)
                    for u in range(U4):
                        pe.wait_ge(s_vc, it * U4 + u + 1)
                        pe.wait_ge(s_ph, it * 2 * U4 + 2 * u + 2)
                        for c in range(C):
                            last = pe.transpose(k.bank[u][:, c * P:(c + 1) * P], fk[:, u, c * P:(c + 1) * P], k.ident)
                        last.then_inc(s_kt, 1)
                    pe.wait_ge(s_kc, it * U4 + U4)


def linear_attend(nc, k):
    with ExitStack() as ctx:
        def sb(name, shape, dt=F32):
            return ctx.enter_context(nc.sbuf_tensor(name, shape, dt))
        def sem(name):
            return ctx.enter_context(nc.semaphore(name))
        qs, ks = k.qs, k.ks
        kt = [sb(f"b_kt{i}", [P, C * D]) for i in range(2)]
        vp = k.vp
        am = sb("b_am", [P, 2, GH, P])
        spad = [sb(f"b_spad{i}", [P, C - 1, H * VW]) for i in range(2)]
        nt = sb("b_nt", [P, 2, G * P])
        den = sb("b_den", [P, 2, H])
        on = sb("b_on", [P, 2, D])
        ot = sb("b_ot", [P, 2, D])
        s_init, s_vp = sem("b_init"), sem("b_values")
        s_ktl = [sem(f"b_k_loaded{i}") for i in range(2)]
        s_at, s_am, s_sm, s_sp = sem("b_products"), sem("b_masked"), sem("b_state"), sem("b_state_masked")
        s_nm, s_nt, s_tr, s_de = sem("b_numerators"), sem("b_numerators_out"), sem("b_turned"), sem("b_denominators")
        s_rc, s_on, s_oT, s_oc = sem("b_reciprocals"), sem("b_normalised"), sem("b_output_turned"), sem("b_output_copied")
        s_y, s_yc = sem("b_projected"), sem("b_projected_out")
        b_at = [k.bank[0], k.bank[1]]
        b_nm = [k.bank[2], k.bank[3]]
        b_state, b_tr, b_ot, b_y = k.bank[4], k.bank[5], k.bank[6], k.bank[7]
        NU = C * G
        STATE_AT = (7, 10, 13)
        EPS = FEAT_EPS * E ** 0.5

        with nc.Block() as block:

            @block.sync
            def _(sp):
                for u in range(2):
                    sp.dma_start(kt[u][:], k.h_all[:, u * C * D:(u + 1) * C * D]).then_inc(s_ktl[u], 16)
                with sp.Fori(1, B // 2) as it:
                    for u in range(2):
                        sp.wait_ge(s_nm, it * (2 * NU) + (u - 1) * NU)
                        sp.dma_start(kt[u][:], k.h_all[:, bass.ds(it * (2 * C * D) + u * C * D, C * D)]).then_inc(s_ktl[u], 16)
                        for load in STACK_LOADS:
                            load_stack(sp, k, u, it * 2 + u, *load)

            @block.tensor
            def _(pe):
                def state(it, b, u, c):
                    if c == 0:
                        wait(pe, s_ktl[u], it * 16 + 16)
                        wait(pe, s_vp, b + 1)
                    wait(pe, s_sp, b * (C - 1) + c)
                    pe.matmul(b_state[:, 0:H * (E + 1)], kt[u][:, c * D:(c + 1) * D],
                              vp[u][:, c], start=(c == 0), stop=(c == C - 2),
                              skip_group_check=True).then_inc(s_sm, 1)

                def products(it, b, u, n):
                    c, g = n // G, n % G
                    if n == 0:
                        wait(pe, k.s_stk[u], it * N_STACK + N_STACK)
                    wait(pe, s_am, b * NU + n - 1)
                    for j in range(GH):
                        half, slot = LIN_HALF[GH * g + j], LIN_SLOT[GH * g + j]
                        last = pe.matmul(b_at[n % 2][:, j * P:(j + 1) * P],
                                         ks[u][:, half, slot, c * P:(c + 1) * P],
                                         qs[u][:, slot, c * P:(c + 1) * P],
                                         start=True, stop=True)
                    last.then_inc(s_at, 1)

                def numerators(b, u, n):
                    c, g = n // G, n % G
                    cols = slice(g * P, (g + 1) * P)
                    if g == 0:
                        wait(pe, s_nt, b * C + c - 1)
                    if c:
                        if g == 0:
                            wait(pe, s_sp, b * (C - 1) + c)
                        pe.matmul(b_nm[c % 2][:, cols], spad[u][:, c - 1, cols],
                                  k.fq_all[:, bass.ds(b * L + c * P, P)], start=True, stop=False,
                                  skip_group_check=True)
                    wait(pe, s_am, b * NU + n + 1)
                    for j in range(GH):
                        last = pe.matmul(b_nm[c % 2][VW * j:VW * j + E + 1, cols], vp[u][:, c, GH * g + j, :],
                                         am[:, n % 2, j, :], start=(c == 0), stop=True,
                                         tile_position=(0, VW * j), skip_group_check=True)
                    last.then_inc(s_nm, 1)

                def turn(q, c):
                    wait(pe, s_nt, q + 1)
                    wait(pe, s_on, q)
                    for g in range(G):
                        last = pe.transpose(b_tr[:, g * P:(g + 1) * P], nt[:, c % 2, g * P:(g + 1) * P], k.ident)
                    last.then_inc(s_tr, 1)

                def turn_back(q, c):
                    wait(pe, s_on, q + 1)
                    wait(pe, s_oc, q)
                    pe.transpose(b_ot[:, 0:P], on[:, c % 2, :], k.ident).then_inc(s_oT, 1)

                def project(b, q, c):
                    wait(pe, s_oc, q + 1)
                    if c == 0:
                        wait(pe, s_yc, b)
                    pe.matmul(b_y[:, c * P:(c + 1) * P], ot[:, c % 2, :], k.woutt[:],
                              start=True, stop=True).then_inc(s_y, 1)

                def body(it, first, last):
                    for u in range(2):
                        b = it * 2 + u
                        first_b, last_b = first and u == 0, last and u == 1
                        for n in range(NU):
                            c, g = n // G, n % G
                            q = b * C + c
                            if n + 1 < NU:
                                products(it, b, u, n + 1)
                            elif not last_b:
                                products(it + u, b + 1, 1 - u, 0)
                            if g == 0 and not (first_b and c < 2):
                                turn_back(q - 2, (c - 2) % C)
                            if g == 1 and not (first_b and c == 0):
                                turn(q - 1, (c - 1) % C)
                            if g == 2 and not (first_b and c < 2):
                                project(b, q - 2, (c - 2) % C)
                            if n in STATE_AT and not last_b:
                                state(it + u, b + 1, 1 - u, STATE_AT.index(n))
                            numerators(b, u, n)

                wait(pe, s_init, 4)
                for c in range(C - 1):
                    state(0, 0, 0, c)
                products(0, 0, 0, 0)
                paired(pe, body)
                q = B * C - 1
                turn(q, C - 1)
                turn_back(q - 1, C - 2)
                project(B - 1, q - 1, C - 2)
                turn_back(q, C - 1)
                project(B - 1, q, C - 1)

            @block.vector
            def _(dve):
                def masked(b, n):
                    wait(dve, s_at, b * NU + n + 1)
                    wait(dve, s_nm, b * NU + n - 1)
                    dve.tensor_tensor(am[:, n % 2, :, :], k.tiles(b_at[n % 2][:], GH), k.rep(k.causal, GH),
                                      ALU.mult).then_inc(s_am, 1)

                def state(b, u, c):
                    wait(dve, s_sm, b * (C - 1) + c + 1)
                    dve.tensor_tensor(spad[u][:, c, :].rearrange("p (h w) -> p h w", h=H)[:, :, 0:E + 1],
                                      b_state[:, 0:H * (E + 1)].rearrange("p (h w) -> p h w", h=H),
                                      k.hmask.unsqueeze(2).to_broadcast([P, H, E + 1]),
                                      ALU.mult).then_inc(s_sp, 1)

                def normalise(q, c):
                    wait(dve, s_tr, q + 1)
                    heads = b_tr[:].rearrange("p (h w) -> p h w", h=H)
                    dve.tensor_scalar(den[:, c % 2, :], heads[:, :, E], EPS, None, ALU.add).then_inc(s_de, 1)
                    wait(dve, s_de, q + 1)
                    dve.reciprocal(den[:, c % 2, :], den[:, c % 2, :]).then_inc(s_rc, 1)
                    wait(dve, s_rc, q + 1)
                    dve.tensor_tensor(on[:, c % 2, :].rearrange("p (h e) -> p h e", h=H), heads[:, :, 0:E],
                                      den[:, c % 2, :].unsqueeze(2).to_broadcast([P, H, E]),
                                      ALU.mult).then_inc(s_on, 1)

                def output(b):
                    wait(dve, s_y, b * C + C)
                    dve.tensor_tensor(k.tiles(k.v_all[:, bass.ds(b * (C * D), C * D)], C), k.tiles(b_y[:], C),
                                      k.rep(k.BO, C), ALU.add).then_inc(s_yc, 1)

                def body(it, first, last):
                    for u in range(2):
                        b = it * 2 + u
                        first_b, last_b = first and u == 0, last and u == 1
                        for n in range(NU):
                            c, g = n // G, n % G
                            masked(b, n)
                            if g == 2 and not (first_b and c == 0):
                                normalise(b * C + c - 1, (c - 1) % C)
                            if n == 8 and not first_b:
                                output(b - 1)
                            if n - 1 in STATE_AT and not last_b:
                                state(b + 1, 1 - u, STATE_AT.index(n - 1))

                for bank in b_nm:
                    dve.memset(bank[:], 0.0).then_inc(s_init, 1)
                for u in range(2):
                    dve.memset(spad[u][:], 0.0).then_inc(s_init, 1)
                wait(dve, s_init, 4)
                for c in range(C - 1):
                    state(0, 0, c)
                paired(dve, body)
                normalise(B * C - 1, C - 1)
                output(B - 1)

            @block.scalar
            def _(act):
                def values(b, u):
                    wait(act, s_nm, (b - 1) * NU)
                    act.activation(vp[u][:, :, :, 0:E], k.v_all[:, bass.ds(b * (C * D), C * D)]
                                   .rearrange("p (c h e) -> p c h e", c=C, h=H), ACT.Copy).then_inc(s_vp, 1)

                def numerators_out(q, c):
                    wait(act, s_nm, (q + 1) * G)
                    wait(act, s_tr, q - 1)
                    act.activation(nt[:, c % 2, :], b_nm[c % 2][:], ACT.Copy).then_inc(s_nt, 1)

                def output_out(q, c):
                    wait(act, s_oT, q + 1)
                    act.activation(ot[:, c % 2, :], b_ot[:, 0:P], ACT.Copy).then_inc(s_oc, 1)

                def body(it, first, last):
                    for u in range(2):
                        b = it * 2 + u
                        for c in range(C):
                            q = b * C + c
                            if c == 0 and not (last and u == 1):
                                values(b + 1, 1 - u)
                            numerators_out(q, c)
                            if not (first and u == 0 and c == 0):
                                output_out(q - 1, (c - 1) % C)

                values(0, 0)
                paired(act, body)
                output_out(B * C - 1, C - 1)


def softmax_prepare(nc, k):
    N = U4 * C
    with ExitStack() as ctx:
        def sb(name, shape, dt=F32):
            return ctx.enter_context(nc.sbuf_tensor(name, shape, dt))
        def sem(name):
            return ctx.enter_context(nc.semaphore(name))
        st = sb("c_st", [P, N, 6])
        mv = sb("c_mv", [P, 3, N, 2])
        ve = sb("c_ve", [P, N])
        rs = sb("c_rs", [P, 3, N])
        xn = sb("c_xn", [P, N * D])
        tmp = sb("c_tmp", [P, N * D])
        ht = sb("c_ht", [P, U4 * L])
        r1 = sb("c_r1", [P, 2, L])
        parts = sb("c_parts", [P, U4 * 6 * L], BF16)
        s_st, s_mv, s_ve, s_rs = sem("c_stats"), sem("c_means"), sem("c_variances"), sem("c_rstd")
        s_z, s_t1, s_ln, s_xn = sem("c_x_shifted"), sem("c_scaled"), sem("c_layernorms"), sem("c_normed")
        s_tr, s_ht, s_pj = sem("c_transposed"), sem("c_h_ready"), sem("c_projected")
        s_p1, s_r1, s_p2, s_p3 = sem("c_part1"), sem("c_rest1"), sem("c_part2"), sem("c_part3")
        s_v, s_vc = sem("c_v"), sem("c_v_copied")

        s_ps = [sem(f"c_parts_stored{u}") for u in range(U4)]

        with nc.Block() as block:

            @block.sync
            def _(sp):
                for u in range(U4):
                    sp.sem_inc(s_ps[u], 16)
                with sp.Fori(0, B // U4) as it:
                    for u in range(U4):
                        store_parts(sp, k, parts, it, u, s_p3, s_ps)
                for b in range(1):
                    sp.wait_ge(s_ps[b], 32)
                    for load in STACK_LOADS:
                        load_stack(sp, k, b, b, *load)
                for u in range(U4):
                    sp.wait_ge(s_ps[u], 16 * (B // U4) + 16)

            def tile_at(a, it, i):
                return a[:, bass.ds(it * (N * D) + i * D, D)]

            @block.vector
            def _(dve):
                with dve.Fori(0, B // U4) as it:
                    for m, (src, dst, gain) in enumerate(((k.v_all, k.x_all, k.G_OF), (k.x_all, k.h_all, k.CB_OF))):
                        norm_stats(dve, k, st, mv[:, m], ve, lambda i: tile_at(src, it, i), N,
                                   s_st, s_mv, s_ve, it * (3 * N) + m * N, it * (3 * N) + m * N)
                        for i in range(N):
                            row = k.mod4[:, bass.ds(it * (U4 * D) + gain + (i // C) * D, D)]
                            dve.scalar_tensor_tensor(tmp[:, i * D:(i + 1) * D], tile_at(src, it, i), mv[:, m, i, 0:1],
                                                     row, ALU.subtract, ALU.mult).then_inc(s_t1, 1)
                        dve.wait_ge(s_rs, it * 3 + m + 1)
                        dve.wait_ge(s_t1, it * (2 * N) + (m + 1) * N)
                        if m == 0:
                            dve.wait_ge(s_z, it * U4 + U4)
                        for i in range(N):
                            shift = (tile_at(k.x_all, it, i) if m == 0 else
                                     k.mod4[:, bass.ds(it * (U4 * D) + k.SB_OF + (i // C) * D, D)])
                            dve.scalar_tensor_tensor(tile_at(dst, it, i), tmp[:, i * D:(i + 1) * D], rs[:, m, i:i + 1],
                                                     shift, ALU.mult, ALU.add).then_inc(s_ln, 1)
                        dve.wait_ge(s_ln, it * (2 * N) + (m + 1) * N)
                    norm_stats(dve, k, st, mv[:, 2], ve, lambda i: tile_at(k.h_all, it, i), N,
                               s_st, s_mv, s_ve, it * (3 * N) + 2 * N, it * (3 * N) + 2 * N)
                    dve.wait_ge(s_rs, it * 3 + 3)
                    for i in range(N):
                        dve.tensor_scalar(xn[:, i * D:(i + 1) * D], tile_at(k.h_all, it, i),
                                          mv[:, 2, i, 0:1], rs[:, 2, i:i + 1], ALU.subtract, ALU.mult).then_inc(s_xn, 1)
                    for u in range(U4):
                        for z in range(2):
                            n = 2 * u + z
                            dve.wait_ge(s_p1, it * 2 * U4 + n + 1)
                            dve.wait_ge(s_p3, it * 2 * U4 + n + 1)
                            dve.tensor_tensor(r1[:, z, :], k.bank[4 + 2 * (u % 2) + z][:],
                                              part(parts, u, z, 0),
                                              ALU.subtract).then_inc(s_r1, 1)

            @block.gpsimd
            def _(pool):
                pool.sem_inc(s_p3, 2)
                with pool.Fori(0, B // U4) as it:
                    for u in range(U4):
                        xu = k.tiles(k.x_all[:, bass.ds(it * (N * D) + u * C * D, C * D)], C)
                        pool.tensor_tensor(xu, xu, k.mod4[:, bass.ds(it * (U4 * D) + k.B_OF + u * D, D)]
                                           .unsqueeze(1).to_broadcast([P, C, D]), ALU.add).then_inc(s_z, 1)
                    for m in range(3):
                        pool.wait_ge(s_ve, it * 3 + m + 1)
                        pool.tensor_tensor(rs[:, m, :], ve[:], k.halfneg[:], ALU.pow).then_inc(s_rs, 1)
                    for n in range(2 * U4):
                        u, z = n // 2, n % 2
                        pool.wait_ge(s_p2, it * 2 * U4 + n + 1)
                        pool.tensor_tensor(part(parts, u, z, 2),
                                           r1[:, z, :],
                                           part(parts, u, z, 1),
                                           ALU.subtract).then_inc(s_p3, 1)

            @block.scalar
            def _(act):
                act.sem_inc(s_vc, 1)
                with act.Fori(0, B // U4) as it:
                    for u in range(U4):
                        act.wait_ge(s_tr, it * U4 + u + 1)
                        act.activation(ht[:, u * L:(u + 1) * L], k.bank[u][:], ACT.Identity,
                                       bias=k.lnw[:, 1:2], scale=k.lnw[:, 0:1]).then_inc(s_ht, 1)
                    for u in range(U4):
                        for z in range(2):
                            act.wait_ge(s_pj, it * 2 * U4 + 2 * u + z + 1)
                            if z == 0:
                                act.wait_ge(s_ps[u], it * 16 + 16)
                            act.activation(part(parts, u, z, 0),
                                           k.bank[4 + 2 * (u % 2) + z][:], ACT.Copy).then_inc(s_p1, 1)
                        for z in range(2):
                            act.wait_ge(s_r1, it * 2 * U4 + 2 * u + z + 1)
                            act.activation(part(parts, u, z, 1),
                                           r1[:, z, :], ACT.Copy).then_inc(s_p2, 1)
                        act.wait_ge(s_v, it * U4 + u + 1)
                        act.activation(k.v_all[:, bass.ds(it * (N * D) + u * C * D, C * D)], k.bank[u][:],
                                       ACT.Copy).then_inc(s_vc, 1)

            @block.tensor
            def _(pe):
                with pe.Fori(0, B // U4) as it:
                    for u in range(U4):
                        if u == 0:
                            pe.wait_ge(s_vc, it * U4 + 1)
                        pe.wait_ge(s_xn, it * N + (u + 1) * C)
                        for c in range(C):
                            i = u * C + c
                            last = pe.transpose(k.bank[u][:, c * P:(c + 1) * P], xn[:, i * D:(i + 1) * D], k.ident)
                        last.then_inc(s_tr, 1)
                    for u in range(U4):
                        pe.wait_ge(s_ht, it * U4 + u + 1)
                        if u >= 2:
                            pe.wait_ge(s_r1, it * 2 * U4 + 2 * (u - 1))
                        for z in range(2):
                            pe.matmul(k.bank[4 + 2 * (u % 2) + z][:], k.wsm[:, z * D:(z + 1) * D],
                                      ht[:, u * L:(u + 1) * L], start=True, stop=True).then_inc(s_pj, 1)
                        for c in range(C):
                            last = pe.matmul(k.bank[u][:, c * P:(c + 1) * P], ht[:, u * L + c * P:u * L + (c + 1) * P],
                                             k.wsm[:, 2 * D:3 * D], start=True, stop=True)
                        last.then_inc(s_v, 1)


def softmax_attend(nc, k):
    with ExitStack() as ctx:
        def sb(name, shape, dt=F32):
            return ctx.enter_context(nc.sbuf_tensor(name, shape, dt))
        def sem(name):
            return ctx.enter_context(nc.semaphore(name))
        qs, ks = k.qs, k.ks
        vp = k.vp
        mx = sb("d_mx", [P, 2, 4 * C])
        mt = sb("d_mt", [4 * C, 2, P], BF16)
        den = sb("d_den", [P, 2, H])
        on = sb("d_on", [P, 2, D])
        ot = sb("d_ot", [P, 2, D])
        nt = k.fq_all[:].rearrange("p (u g q) -> p u g q", u=2, g=G)
        pt = k.mod4[:].rearrange("p (r x f) -> p r x f", r=2, x=2)
        s_init, s_vp = sem("d_init"), sem("d_values")
        s_m, s_mr, s_mt, s_mc = sem("d_max_scores"), sem("d_maxima"), sem("d_maxima_turned"), sem("d_maxima_copied")
        s_row = [sem(f"d_maxima_rows{i}") for i in range(2)]
        s_zero = [sem(f"d_rows_cleared{i}") for i in range(2)]
        s_s, s_e, s_pv, s_ne = sem("d_scores"), sem("d_probs"), sem("d_values_summed"), sem("d_numerators_out")
        s_ft, s_fr, s_fo = sem("d_turned"), sem("d_reciprocals"), sem("d_normalised")
        s_fb, s_fe, s_fp, s_fh = sem("d_turned_back"), sem("d_output_copied"), sem("d_projected"), sem("d_y_ready")
        b_m, b_num, b_misc, b_s = [k.bank[0], k.bank[1]], k.bank[2], k.bank[3], k.pair
        NG = 2 * G
        SCALE = E ** -0.5

        with nc.Block() as block:

            @block.sync
            def _(sp):
                def rows(i, n):
                    wait(sp, s_mc, n + 1)
                    u, g = (i // G) % 2, i % G
                    for half in range(2):
                        r = 64 * half + KR
                        sp.dma_start(qs[u][r:r + 1, 2 * g:2 * g + 2, :], mt[8 * half:8 * half + 8, i % 2, :]).then_inc(s_row[i % 2], 16)

                def body(it, first, last):
                    for i in range(NG):
                        n = it * NG + i
                        u, g = i // G, i % G
                        if g < 2 and not (last and u == 1):
                            if g == 0:
                                wait(sp, s_pv, n * C)
                                for half in range(2):
                                    r = 64 * half + KR
                                    sp.dma_start(qs[1 - u][r:r + 1, :, :], qs[1 - u][r + 1:r + 2, :, :]).then_inc(s_zero[1 - u], 16)
                            for load in STACK_LOADS[6 * g:6 * g + 6]:
                                load_stack(sp, k, 1 - u, it * 2 + u + 1, *load)
                        if not (last and i == NG - 1):
                            rows(i + 1, n + 1)

                rows(0, 0)
                paired(sp, body)

            @block.gpsimd
            def _(pool):
                def body(it, first, last):
                    for u in range(2):
                        b = it * 2 + u
                        wait(pool, s_pv, (b - 1) * (G * C))
                        for c in range(C):
                            pool.tensor_copy(vp[u][:, c, :, 0:E],
                                             k.v_all[:, bass.ds(b * (C * D) + c * D, D)].rearrange("p (h e) -> p h e", h=H)
                                             ).then_inc(s_vp, 1)

                paired(pool, body)

            @block.tensor
            def _(pe):
                def max_scores(i, n, x):
                    u, g = (i // G) % 2, i % G
                    if g == 0 and x == 0:
                        wait(pe, k.s_stk[u], (n - i) * (N_STACK // NG) + (i // NG + 1 + B // 2) * N_STACK)
                        wait(pe, s_zero[u], (n - i) * (32 // NG) + (i // NG + u) * 32)
                    qt, jj, half = x // 4, x // 2 % 2, x % 2
                    slot = 2 * g + jj
                    wait(pe, s_mr, n * 16 + x - 1)
                    pe.matmul(b_m[x % 2][:], qs[u][:, slot, qt * P:(qt + 1) * P], ks[u][:, half, slot, :],
                              start=True, stop=True).then_inc(s_m, 1)

                def turn_maxima(i, n):
                    wait(pe, s_mr, n * 16 + 16)
                    wait(pe, s_fh, n - 1 - G)
                    pe.transpose(b_misc[0:4 * C, 0:P], mx[:, i % 2, :], k.ident).then_inc(s_mt, 1)

                def scores(i, n, kt, x):
                    u, g = i // G, i % G
                    if kt == 0 and x == 0:
                        wait(pe, s_row[i % 2], (n - i % 2) * 16 + 32)
                    wait(pe, s_e, n * 8 + 2 * kt + x - 1)
                    for half in range(2):
                        slot = 2 * g + x
                        last = pe.matmul(b_s[x][:, half * L:(half + 1) * L], ks[u][:, half, slot, kt * P:(kt + 1) * P],
                                         qs[u][:, slot, :], start=True, stop=True)
                    last.then_inc(s_s, 1)

                def values(i, n, kt):
                    u, g = (i // G) % 2, i % G
                    wait(pe, s_e, n * 8 + 2 * kt + 2)
                    if kt == 0:
                        wait(pe, s_ne, n)
                        if g == 0:
                            wait(pe, s_vp, n * 1 + C)
                    for q in range(GH):
                        last = pe.matmul(b_num[VW * q:VW * q + E + 1, :], vp[u][:, kt, GH * g + q, :],
                                         pt[:, kt % 2, q % 2, (q // 2) * L:(q // 2 + 1) * L],
                                         start=(kt == 0), stop=(kt == C - 1), tile_position=(0, VW * q),
                                         skip_group_check=True)
                    last.then_inc(s_pv, 1)

                def finish(i, n, step, turns):
                    u, c = (i // G + 1) % 2, i % G
                    f = n - G
                    if step == 0:
                        wait(pe, s_ne, n - c)
                        wait(pe, s_fh, f)
                        if turns:
                            wait(pe, s_mc, n + 2)
                        for g in range(G):
                            last = pe.transpose(b_misc[:, g * P:(g + 1) * P], nt[:, u, g, c * P:(c + 1) * P], k.ident)
                        last.then_inc(s_ft, 1)
                    elif step == 1:
                        wait(pe, s_fo, f + 1)
                        pe.transpose(b_misc[:, 0:P], on[:, c % 2, :], k.ident).then_inc(s_fb, 1)
                    else:
                        wait(pe, s_fe, f + 1)
                        pe.matmul(b_misc[:, 0:P], ot[:, c % 2, :], k.wproj[:], start=True, stop=True).then_inc(s_fp, 1)

                def body(it, first, last):
                    for i in range(NG):
                        n = it * NG + i
                        ahead = not (last and i + 2 >= NG)
                        behind = not (first and i < G)
                        for kt in range(C):
                            for x in range(2):
                                if ahead:
                                    max_scores(i + 2, n + 2, 4 * kt + x)
                                scores(i, n, kt, x)
                            if ahead:
                                max_scores(i + 2, n + 2, 4 * kt + 2)
                            if kt:
                                values(i, n, kt - 1)
                            elif not (first and i == 0):
                                values(i - 1, n - 1, C - 1)
                            if ahead:
                                max_scores(i + 2, n + 2, 4 * kt + 3)
                            if kt == 0 and not (last and i + 1 >= NG):
                                turn_maxima(i + 1, n + 1)
                            if kt and behind:
                                finish(i, n, kt - 1, not (last and i == NG - 1))

                wait(pe, s_init, 1)
                for n in range(2):
                    for x in range(16):
                        max_scores(n, n, x)
                turn_maxima(0, 0)
                paired(pe, body)
                values(NG - 1, B * G - 1, C - 1)
                for c in range(C):
                    for step in range(3):
                        finish(c, B * G + c, step, False)

            @block.vector
            def _(dve):
                def maximum(i, n, x):
                    qt, jj, half = x // 4, x // 2 % 2, x % 2
                    col = half * 8 + jj * 4 + qt
                    wait(dve, s_m, n * 16 + x + 1)
                    dve.reduce_max(mx[:, i % 2, col:col + 1], b_m[x % 2][:], AX).then_inc(s_mr, 1)

                def normalise(i, n):
                    c, f = i % G, n - G
                    heads = b_misc[:].rearrange("p (h w) -> p h w", h=H)
                    wait(dve, s_ft, f + 1)
                    dve.reciprocal(den[:, c % 2, :], heads[:, :, E]).then_inc(s_fr, 1)
                    wait(dve, s_fr, f + 1)
                    dve.tensor_tensor(on[:, c % 2, :].rearrange("p (h e) -> p h e", h=H), heads[:, :, 0:E],
                                      den[:, c % 2, :].unsqueeze(2).to_broadcast([P, H, E]), ALU.mult).then_inc(s_fo, 1)

                def add(i, n):
                    f = n - G
                    wait(dve, s_fp, f + 1)
                    y = k.h_all[:, bass.ds(f * D, D)]
                    dve.tensor_tensor(y, y, b_misc[:, 0:P], ALU.add).then_inc(s_fh, 1)

                def body(it, first, last):
                    for i in range(NG):
                        n = it * NG + i
                        ahead = not (last and i + 2 >= NG)
                        behind = not (first and i < G)
                        for kt in range(C):
                            if ahead:
                                maximum(i + 2, n + 2, 4 * kt)
                                maximum(i + 2, n + 2, 4 * kt + 1)
                            if kt == 0 and not (first and i <= G):
                                add(i - 1, n - 1)
                            if kt == 2 and behind:
                                normalise(i, n)
                            if ahead:
                                maximum(i + 2, n + 2, 4 * kt + 2)
                                maximum(i + 2, n + 2, 4 * kt + 3)

                dve.memset(b_num[:], 0.0).then_inc(s_init, 1)
                for n in range(2):
                    for x in range(16):
                        maximum(n, n, x)
                paired(dve, body)
                add(NG - 1, B * G - 1)
                for c in range(C):
                    normalise(c, B * G + c)
                    add(c, B * G + c)

            @block.scalar
            def _(act):
                def probs(i, n, kt, x):
                    wait(act, s_s, n * 8 + 2 * kt + x + 1)
                    if x == 0:
                        wait(act, s_pv, n * C + kt - 1)
                    act.activation(pt[:, kt % 2, x, :], b_s[x][:], ACT.Exp, scale=SCALE).then_inc(s_e, 1)

                def maxima_out(i, n):
                    wait(act, s_mt, n + 1)
                    wait(act, s_row[i % 2], (n - i % 2) * 16)
                    act.activation(mt[:, i % 2, :], b_misc[0:4 * C, 0:P], ACT.Copy, scale=-1.0).then_inc(s_mc, 1)

                def output_out(i, n):
                    wait(act, s_fb, n - G + 1)
                    act.activation(ot[:, i % 2, :], b_misc[:, 0:P], ACT.Copy).then_inc(s_fe, 1)

                def numerators_out(i, n):
                    wait(act, s_pv, n * C + C)
                    act.activation(nt[:, (i // G) % 2, i % G, :], b_num[:], ACT.Copy).then_inc(s_ne, 1)

                def body(it, first, last):
                    for i in range(NG):
                        n = it * NG + i
                        for kt in range(C):
                            probs(i, n, kt, 0)
                            if kt == 1 and not (last and i + 1 >= NG):
                                maxima_out(i + 1, n + 1)
                            if kt == 3 and not (first and i < G):
                                output_out(i, n)
                            probs(i, n, kt, 1)
                            if kt == 0 and not (first and i == 0):
                                numerators_out(i - 1, n - 1)

                maxima_out(0, 0)
                paired(act, body)
                numerators_out(NG - 1, B * G - 1)
                for c in range(C):
                    output_out(c, B * G + c)


def route_phase(nc, k):
    with ExitStack() as ctx:
        def sb(name, shape, dt=F32):
            return ctx.enter_context(nc.sbuf_tensor(name, shape, dt))
        k.logits = sb("e_logits", [P, T * NE])
        k.slot_u = sb("e_slot_u", [P, T], U32)
        k.expert_i = sb("e_expert_i", [P, MT], I32)
        k.w1_all = sb("e_w1", [P, NE * HID])
        k.w2_all = sb("e_w2", [P, NE * HID])
        gate(nc, k)
        sort_tokens(nc, k)
        run_experts(nc, k)
        add_experts(nc, k)


def gate(nc, k):
    N = U4 * C
    with ExitStack() as ctx:
        def sb(name, shape, dt=F32):
            return ctx.enter_context(nc.sbuf_tensor(name, shape, dt))
        def sem(name):
            return ctx.enter_context(nc.semaphore(name))
        st = sb("e_st", [P, N, 6])
        mv = sb("e_mv", [P, N, 2])
        ve = sb("e_ve", [P, N])
        rs = sb("e_rs", [P, N])
        xn = sb("e_xn", [P, N * D])
        tmp = sb("e_tmp", [P, N * D])
        ht = sb("e_ht", [P, U4 * L])
        s_w = sem("e_weights_in")
        s_st, s_mv, s_ve, s_rs = sem("e_stats"), sem("e_means"), sem("e_variances"), sem("e_rstd")
        s_t1, s_xn, s_cp = sem("e_scaled"), sem("e_normed"), sem("e_normed_copied")
        s_tr, s_ht, s_gl, s_lg = sem("e_transposed"), sem("e_transposed_out"), sem("e_gate_products"), sem("e_logits_out")

        with nc.Block() as block:

            @block.sync
            def _(sp):
                for e in range(NE):
                    sp.dma_start(k.w1_all[:, e * HID:(e + 1) * HID], k.w1[e]).then_inc(s_w, 16)
                    sp.dma_start(k.w2_all[:, e * HID:(e + 1) * HID].rearrange("p (c d) -> p c d", c=HC),
                                 k.w2[e].rearrange("(c p) d -> p c d", p=P)).then_inc(s_w, 16)
                sp.wait_ge(s_w, 16 * 2 * NE)

            @block.vector
            def _(dve):
                with dve.Fori(0, B // U4) as it:
                    norm_stats(dve, k, st, mv, ve, lambda i: k.h_all[:, bass.ds(it * (N * D) + i * D, D)], N,
                               s_st, s_mv, s_ve, it * N, it * N)
                    for i in range(N):
                        dve.scalar_tensor_tensor(tmp[:, i * D:(i + 1) * D], k.h_all[:, bass.ds(it * (N * D) + i * D, D)],
                                                 mv[:, i, 0:1], k.L2W, ALU.subtract, ALU.mult).then_inc(s_t1, 1)
                    dve.wait_ge(s_rs, it + 1)
                    dve.wait_ge(s_t1, it * N + N)
                    for i in range(N):
                        dve.scalar_tensor_tensor(xn[:, i * D:(i + 1) * D], tmp[:, i * D:(i + 1) * D],
                                                 rs[:, i:i + 1], k.L2B, ALU.mult, ALU.add).then_inc(s_xn, 1)
                    for u in range(U4):
                        dve.wait_ge(s_gl, it * U4 + u + 1)
                        dve.tensor_tensor(k.tiles(k.logits[:, bass.ds((it * N + u * C) * NE, C * NE)], C),
                                          k.tiles(k.bank[4 + u][:, 0:C * NE], C), k.rep(k.gateb[:], C),
                                          ALU.add).then_inc(s_lg, 1)
                    dve.wait_ge(s_cp, it * U4 + U4)

            @block.gpsimd
            def _(pool):
                with pool.Fori(0, B // U4) as it:
                    pool.wait_ge(s_ve, it + 1)
                    pool.tensor_tensor(rs[:], ve[:], k.halfneg[:], ALU.pow).then_inc(s_rs, 1)

            @block.scalar
            def _(act):
                with act.Fori(0, B // U4) as it:
                    for u in range(U4):
                        act.wait_ge(s_tr, it * U4 + u + 1)
                        act.activation(ht[:, u * L:(u + 1) * L], k.bank[u][:], ACT.Copy).then_inc(s_ht, 1)
                        act.activation(k.fq_all[:, bass.ds(it * (N * D) + u * C * D, C * D)],
                                       xn[:, u * C * D:(u + 1) * C * D], ACT.Copy).then_inc(s_cp, 1)

            @block.tensor
            def _(pe):
                with pe.Fori(0, B // U4) as it:
                    for u in range(U4):
                        pe.wait_ge(s_xn, it * N + (u + 1) * C)
                        for c in range(C):
                            i = u * C + c
                            last = pe.transpose(k.bank[u][:, c * P:(c + 1) * P], xn[:, i * D:(i + 1) * D], k.ident)
                        last.then_inc(s_tr, 1)
                    for u in range(U4):
                        pe.wait_ge(s_ht, it * U4 + u + 1)
                        for c in range(C):
                            last = pe.matmul(k.bank[4 + u][:, c * NE:(c + 1) * NE],
                                             ht[:, u * L + c * P:u * L + (c + 1) * P], k.gatew[:],
                                             start=True, stop=True)
                        last.then_inc(s_gl, 1)


def sort_tokens(nc, k):
    with ExitStack() as ctx:
        def sb(name, shape, dt=F32):
            return ctx.enter_context(nc.sbuf_tensor(name, shape, dt))
        def sem(name):
            return ctx.enter_context(nc.semaphore(name))
        mx = sb("f_mx", [P, T])
        eq = sb("f_eq", [P, T, NE])
        oh = sb("f_onehot", [P, T, NE])
        tot = sb("f_tot", [P, T * NE])
        cum = [sb(f"f_cum{i}", [P, T * NE]) for i in range(2)]
        over = sb("f_over", [P, NE, T])
        used = sb("f_used", [P, NE])
        ends = [sb(f"f_ends{i}", [P, NE]) for i in range(2)]
        base = sb("f_base", [P, NE])
        row = sb("f_row", [P, T, NE])
        slot = sb("f_slot", [P, T])
        past = sb("f_past", [P, MT, NE])
        expert = sb("f_expert", [P, MT])
        s_oh, s_pr, s_v, s_slot, s_out = (sem("f_onehot_ready"), sem("f_products"), sem("f_vector_step"),
                                          sem("f_slots_ready"), sem("f_rows_written"))
        FIRST = k.cst[:, C_FIRST:C_FIRST + NE]
        STARTS = k.cst[:, C_TILES:C_TILES + T]
        INDEX = k.cst[:, C_J:C_J + MT]

        def flat(ap):
            return ap.rearrange("p t e -> p (t e)")

        def over_experts(ap, n):
            return ap.unsqueeze(2).to_broadcast([P, n, NE])

        with nc.Block() as block:

            @block.vector
            def _(dve):
                step = [0]

                def done(ins):
                    step[0] += 1
                    ins.then_inc(s_v, 1)

                def after():
                    dve.wait_ge(s_v, step[0])

                def running_sums(src, bufs, n, width):
                    d, i = 1, 0
                    while d < n:
                        dst, w = bufs[i % 2], d * width
                        done(dve.tensor_tensor(dst[:, w:], src[:, w:], src[:, :(n - d) * width], ALU.add))
                        done(dve.tensor_copy(dst[:, 0:w], src[:, 0:w]))
                        after()
                        src, d, i = dst, 2 * d, i + 1
                    return src

                lg = k.tiles(k.logits[:], T)
                done(dve.reduce_max(mx[:], lg, AX))
                after()
                done(dve.tensor_tensor(eq[:], lg, over_experts(mx[:], T), ALU.is_equal))
                after()
                done(dve.tensor_tensor(eq[:], eq[:], k.rep(FIRST, T), ALU.mult))
                after()
                done(dve.reduce_max(mx[:], eq[:], AX))
                after()
                dve.tensor_tensor(oh[:], eq[:], over_experts(mx[:], T), ALU.is_equal).then_inc(s_oh, 1)
                dve.wait_ge(s_pr, 1)
                done(dve.tensor_copy(tot[:], k.bank[1][:, 0:T * NE]))
                after()
                sums = running_sums(tot[:], [c[:] for c in cum], T, NE)
                count = sums[:, (T - 1) * NE:T * NE]
                done(dve.tensor_tensor(over[:], count.unsqueeze(2).to_broadcast([P, NE, T]), k.rep(STARTS, NE), ALU.is_gt))
                after()
                done(dve.reduce_sum(used[:], over[:], AX))
                after()
                end = running_sums(used[:], [c[:] for c in ends], NE, 1)
                done(dve.tensor_tensor(base[:], end, used[:], ALU.subtract))
                after()
                done(dve.tensor_scalar(base[:], base[:], float(P), None, ALU.mult))
                done(dve.tensor_tensor(flat(row[:]), k.bank[0][:, 0:T * NE], tot[:], ALU.subtract))
                after()
                done(dve.tensor_tensor(flat(row[:]), flat(row[:]), sums, ALU.add))
                after()
                done(dve.tensor_tensor(row[:], row[:], k.rep(base[:], T), ALU.add))
                after()
                done(dve.tensor_tensor(row[:], row[:], oh[:], ALU.mult))
                after()
                done(dve.reduce_sum(slot[:], row[:], AX))
                after()
                dve.tensor_copy(k.slot_u[:], slot[:]).then_inc(s_slot, 1)
                done(dve.tensor_tensor(past[:], over_experts(INDEX, MT), k.rep(end, MT), ALU.is_ge))
                after()
                done(dve.reduce_sum(expert[:], past[:], AX))
                after()
                done(dve.tensor_scalar(expert[:], expert[:], float(NE - 1), None, ALU.min))
                after()
                done(dve.tensor_copy(k.expert_i[:], expert[:]))
                after()

            @block.tensor
            def _(pe):
                pe.wait_ge(s_oh, 1)
                pe.matmul(k.bank[0][:, 0:T * NE], k.cst[:, C_BEFORE:C_BEFORE + P], flat(oh[:]), start=True, stop=True)
                pe.matmul(k.bank[1][:, 0:T * NE], k.cst[:, C_ONES:C_ONES + P], flat(oh[:]),
                          start=True, stop=True).then_inc(s_pr, 1)

            @block.gpsimd
            def _(pool):
                pool.wait_ge(s_slot, 1)
                for t in range(T):
                    pool.indirect_dma_start(k.xs_dram, bass.IndirectOffsetOnAxis(ap=k.slot_u[:, t:t + 1], axis=0),
                                            k.fq_all[:, t * D:(t + 1) * D], None).then_inc(s_out, 16)
                pool.wait_ge(s_out, 16 * T)


R3 = 3


def run_experts(nc, k):
    with ExitStack() as ctx:
        def sb(name, shape, dt=F32):
            return ctx.enter_context(nc.sbuf_tensor(name, shape, dt))
        def sem(name):
            return ctx.enter_context(nc.semaphore(name))
        xin = [sb(f"g_in{i}", [P, D]) for i in range(R3)]
        xt = [sb(f"g_xt{i}", [P, P]) for i in range(R3)]
        w1c = [sb(f"g_w1_{i}", [P, HID]) for i in range(R3)]
        hid = [sb(f"g_hid{i}", [P, HC * P]) for i in range(R3)]
        yo = [sb(f"g_out{i}", [P, D]) for i in range(R3)]
        s_in = [sem(f"g_tile_in{i}") for i in range(R3)]
        s_st = [sem(f"g_tile_stored{i}") for i in range(R3)]
        s_t, s_xt, s_w1, s_up, s_g, s_dn, s_yo = (sem("g_transposed"), sem("g_xt_ready"), sem("g_w1_ready"),
                                                  sem("g_up_products"), sem("g_hidden_ready"),
                                                  sem("g_down_products"), sem("g_tile_out"))
        b_up = [k.bank[i] for i in range(R3)]
        b_dn = [k.bank[R3 + i] for i in range(R3)]
        b_t = k.bank[2 * R3]
        ITS = MT // R3

        def staged(eng, body):
            for u in range(R3):
                body(0, u, u, True, False)
            with eng.Fori(1, ITS - 1) as it:
                for u in range(R3):
                    body(it, it * R3 + u, u, False, False)
            for u in range(R3):
                body(ITS - 1, (ITS - 1) * R3 + u, u, False, True)

        def expert_of(eng, j):
            return eng.value_load(k.expert_i[0:1, bass.ds(j, 1)], min_val=0, max_val=NE - 1)

        with nc.Block() as block:

            @block.sync
            def _(sp):
                def load(it, j, u, first, last):
                    wait(sp, s_t, j - R3 + 1)
                    sp.dma_start(xin[u][:], k.xs_dram[bass.ds(j * P, P), :]).then_inc(s_in[u], 16)
                staged(sp, load)

            @block.tensor
            def _(pe):
                def turn(it, j, u):
                    wait(pe, s_in[u], it * 16 + 16)
                    wait(pe, s_xt, j)
                    pe.transpose(b_t[:, 0:P], xin[u][:], k.ident).then_inc(s_t, 1)

                def up(j, u):
                    wait(pe, s_xt, j + 1)
                    wait(pe, s_w1, j + 1)
                    for c in range(HC):
                        last = pe.matmul(b_up[u][:, c * P:(c + 1) * P], w1c[u][:, c * P:(c + 1) * P], xt[u][:],
                                         start=True, stop=True)
                    last.then_inc(s_up, 1)

                def down(j, u):
                    e = expert_of(pe, j)
                    wait(pe, s_g, j + 1)
                    wait(pe, s_yo, j - R3 + 1)
                    for c in range(HC):
                        last = pe.matmul(b_dn[u][:, 0:D], hid[u][:, c * P:(c + 1) * P],
                                         k.w2_all[:, bass.ds(e * HID + c * D, D)], start=(c == 0), stop=(c == HC - 1))
                    last.then_inc(s_dn, 1)

                def body(it, j, u, first, last):
                    up(j, u)
                    if not (last and u == R3 - 1):
                        turn(it + (u + 1) // R3, j + 1, (u + 1) % R3)
                    if not (first and u == 0):
                        down(j - 1, (u - 1) % R3)

                turn(0, 0, 0)
                staged(pe, body)
                down(MT - 1, R3 - 1)

            @block.vector
            def _(dve):
                def out(it, j, u):
                    wait(dve, s_dn, j + 1)
                    wait(dve, s_st[u], it * 16 + 16)
                    dve.tensor_copy(yo[u][:], b_dn[u][:, 0:D]).then_inc(s_yo, 1)

                def body(it, j, u, first, last):
                    e = expert_of(dve, j)
                    wait(dve, s_up, j - R3 + 1)
                    dve.tensor_copy(w1c[u][:], k.w1_all[:, bass.ds(e * HID, HID)]).then_inc(s_w1, 1)
                    wait(dve, s_t, j + 1)
                    dve.tensor_copy(xt[u][:], b_t[:, 0:P]).then_inc(s_xt, 1)
                    if not (first and u < 2):
                        out(it - (u < 2), j - 2, (u - 2) % R3)

                staged(dve, body)
                for j in (MT - 2, MT - 1):
                    out(j // R3, j, j % R3)

            @block.scalar
            def _(act):
                def store(j, u):
                    wait(act, s_yo, j + 1)
                    act.dma_start(k.ys_dram[bass.ds(j * P, P), :], yo[u][:]).then_inc(s_st[u], 16)

                def body(it, j, u, first, last):
                    wait(act, s_up, j + 1)
                    act.activation(hid[u][:], b_up[u][:], ACT.Gelu_apprx_tanh).then_inc(s_g, 1)
                    if not (first and u < 2):
                        store(j - 2, (u - 2) % R3)

                for u in range(R3):
                    act.sem_inc(s_st[u], 16)
                staged(act, body)
                for j in (MT - 2, MT - 1):
                    store(j, j % R3)
                for u in range(R3):
                    act.wait_ge(s_st[u], 16 * ITS + 16)


def add_experts(nc, k):
    with ExitStack() as ctx:
        def sem(name):
            return ctx.enter_context(nc.semaphore(name))
        s_g = [sem(f"h_gathered{b}") for b in range(B)]
        s_y, s_m, s_o, s_out = sem("h_summed"), sem("h_gated"), sem("h_ready"), sem("h_stored")
        with nc.Block() as block:

            @block.gpsimd
            def _(pool):
                for t in range(T):
                    pool.indirect_dma_start(k.v_all[:, t * D:(t + 1) * D], None, k.ys_dram,
                                            bass.IndirectOffsetOnAxis(ap=k.slot_u[:, t:t + 1], axis=0)
                                            ).then_inc(s_g[t // C], 16)

            @block.vector
            def _(dve):
                for b in range(B):
                    cols = slice(b * C * D, (b + 1) * C * D)
                    m = k.tiles(k.v_all[:, cols], C)
                    dve.wait_ge(s_g[b], 16 * C)
                    dve.tensor_tensor(m, m, k.tiles(k.h_all[:, cols], C), ALU.add).then_inc(s_y, 1)
                    dve.wait_ge(s_y, b + 1)
                    dve.tensor_tensor(m, m, k.rep(k.gb_all[:, b * D:(b + 1) * D], C), ALU.mult).then_inc(s_m, 1)
                    dve.wait_ge(s_m, b + 1)
                    dve.tensor_tensor(m, m, k.tiles(k.x_all[:, cols], C), ALU.add).then_inc(s_o, 1)

            @block.sync
            def _(sp):
                ov = k.out.rearrange("b (c p) d -> p b c d", p=P)
                for b in range(B):
                    sp.wait_ge(s_o, b + 1)
                    sp.dma_start(ov[:, b], k.tiles(k.v_all[:, b * C * D:(b + 1) * C * D], C)).then_inc(s_out, 16)
                sp.wait_ge(s_out, 16 * B)


_INS = ['L0_attn_x', 'L0_attn_Wqkv', 'L0_attn_bqkv', 'L0_attn_Wout', 'L0_attn_bout', 'L0_attn_gamma', 'L0_attn_beta',
        'L0_ffn_ln1_w', 'L0_ffn_ln1_b', 'L0_ffn_w_qkv', 'L0_ffn_w_proj', 'L0_ffn_ln2_w', 'L0_ffn_ln2_b',
        'L0_ffn_gate_w', 'L0_ffn_gate_b', 'L0_ffn_w1', 'L0_ffn_w2', 'L0_c', 'L0_wmod']


def constants():
    import numpy as np
    c = np.zeros((P, C_ALL), np.float32)
    p = np.arange(P)[:, None]
    m = np.arange(P)[None, :]
    pos = np.arange(H)[None, :]
    c[:, C_ID:C_ID + P] = p == m
    c[:, C_CAUSAL:C_CAUSAL + P] = p <= m
    slot_position = 2 * GH * (p % S // GH) + GH * (p // 64) + p % S % GH
    c[:, C_HMASK:C_HMASK + H] = slot_position == pos
    c[:, C_BEFORE:C_BEFORE + P] = p < m
    c[:, C_ONES:C_ONES + P] = 1.0
    c[:, C_TILES:C_TILES + T] = P * np.arange(T)
    c[:, C_J:C_J + MT] = np.arange(MT)
    c[:, C_FIRST:C_FIRST + NE] = NE - np.arange(NE)
    return c


def kernel(**inputs):
    import numpy as _np
    import concourse.bacc as _bacc
    from concourse import mybir as _mybir
    from concourse.bass_utils import run_bass_kernel_spmd as _run

    nc = _bacc.Bacc("TRN2", target_bir_lowering=False, num_devices=1)
    arrays, args = {}, []
    for name, a in [(n, inputs[n]) for n in _INS] + [("consts", constants())]:
        a = _np.ascontiguousarray(a)
        arrays[f"in_{name}_dram"] = a
        args.append(nc.dram_tensor(f"in_{name}_dram", a.shape, _mybir.dt.from_np(a.dtype), kind="ExternalInput").ap())
    out = nc.dram_tensor("out_0_dram", (B, L, D), F32, kind="ExternalOutput").ap()
    adaln_kernel(nc, *args, out)
    r = _run(nc, [arrays], core_ids=[0])
    return r.results[0]["out_0_dram"]
```

```python
import concourse.bass as bass
from concourse import mybir
from contextlib import ExitStack

F32 = mybir.dt.float32
BF16 = mybir.dt.bfloat16
I32 = mybir.dt.int32
U32 = mybir.dt.uint32
ALU = mybir.AluOpType
ACT = mybir.ActivationFunctionType
AX = mybir.AxisListType.X

P = 128
B = 8
L = 512
D = 128
H = 16
E = D // H
C = L // P
T = B * C
NE = 8
HID = 4 * D
HC = HID // P
MT = T + NE - 1
G = 4
GH = H // G
VW = 32
S = H // 2
KR = 6 * E
LN_EPS = 1e-5
FEAT_EPS = 1e-4
NM = 6
Q_PART = (0, 0, 0, 1, 1, 2)
K_PART = (0, 1, 2, 0, 1, 0)
LIN_HALF = [(p // GH) % 2 for p in range(H)]
LIN_SLOT = [GH * (p // (2 * GH)) + p % GH for p in range(H)]
SOFT_HALF = [(p % GH) // 2 for p in range(H)]
SOFT_SLOT = [2 * (p // GH) + p % 2 for p in range(H)]
C_ID = 0
C_CAUSAL = C_ID + P
C_HMASK = C_CAUSAL + P
C_BEFORE = C_HMASK + H
C_ONES = C_BEFORE + P
C_STARTS = C_ONES + P
C_INDEX = C_STARTS + MT
C_FIRST = C_INDEX + P
C_LEFT = C_FIRST + NE
C_ROW = C_LEFT + T
C_ALL = C_ROW + 1


class Buffers:
    pass


def adaln_kernel(nc, x, wqkv, bqkv, wout, bout, gamma, beta, ln1_w, ln1_b, w_qkv, w_proj,
                 ln2_w, ln2_b, gate_w, gate_b, w1, w2, c_in, wmod, consts, out):
    k = Buffers()
    (k.x, k.wqkv, k.bqkv, k.wout, k.bout, k.gamma, k.beta,
     k.ln1_w, k.ln1_b, k.w_qkv, k.w_proj, k.ln2_w, k.ln2_b,
     k.gate_w, k.gate_b, k.w1, k.w2, k.c_in, k.wmod, k.consts, k.out) = (
        x, wqkv, bqkv, wout, bout, gamma, beta, ln1_w, ln1_b, w_qkv, w_proj, ln2_w, ln2_b,
        gate_w, gate_b, w1, w2, c_in, wmod, consts, out)
    top = ExitStack()
    with top:
        def sb(name, shape, dt=F32, ctx=top):
            return ctx.enter_context(nc.sbuf_tensor(name, shape, dt))

        k.bank = [top.enter_context(nc.psum_tensor(f"bank{i}", [P, 4 * P], F32)) for i in range(4)]
        k.pair = [top.enter_context(nc.psum_tensor(f"pair{i}", [P, 8 * P], F32)) for i in range(2)]
        k.bank += [k.pair[0][:, 0:512], k.pair[0][:, 512:1024], k.pair[1][:, 0:512], k.pair[1][:, 512:1024]]

        k.x_all = sb("x_all", [P, T * D])
        k.v_all = sb("v_all", [P, T * D])
        k.fq_all = sb("fq_all", [P, B * L])
        k.h_all = sb("h_all", [P, T * D])
        k.qs = [sb(f"q_stack{i}", [P, S, L], BF16) for i in range(2)]
        k.ks = [sb(f"k_stack{i}", [P, 2, S, L], BF16) for i in range(2)]
        k.vp = [sb(f"values{i}", [P, C, H, E + 1]) for i in range(2)]
        k.s_stk = [top.enter_context(nc.semaphore(f"stacks{i}")) for i in range(2)]
        k.mod4 = sb("mod4", [P, 4 * B * D])
        k.gb_all = sb("gb_all", [P, B * D])
        k.G_OF, k.B_OF, k.CB_OF, k.SB_OF = 0, B * D, 2 * B * D, 3 * B * D
        k.cst = sb("cst", [P, C_ALL])
        k.ident = k.cst[:, C_ID:C_ID + P]
        k.causal = k.cst[:, C_CAUSAL:C_CAUSAL + P]
        k.hmask = k.cst[:, C_HMASK:C_HMASK + H]
        k.wlt = sb("wlt", [P, 3 * D])
        k.woutt = sb("woutt", [P, D])
        k.wsm = sb("wsm", [P, 3 * D])
        k.wproj = sb("wproj", [P, D])
        k.gatew = sb("gatew", [P, NE])
        k.bq2 = sb("bq2", [P, 4])
        k.lnw = sb("lnw", [P, 4])
        k.ca1t = sb("ca1t", [P, B])
        k.sat = sb("sat", [P, B])
        k.rows = sb("rows", [P, 2 * D])
        k.BV, k.BO = k.rows[:, 0:D], k.rows[:, D:2 * D]
        k.gateb = sb("gateb", [P, 1])
        k.spare = sb("spare", [P, U4 + 1])
        k.halfneg = sb("halfneg", [P, C])

        def tiles(ap, n):
            return ap.rearrange("p (c d) -> p c d", c=n)

        def rep(ap, n):
            return ap.unsqueeze(1).to_broadcast([P, n, ap.shape[1]])

        k.parts_dram = nc.dram_tensor("bf16_parts", [B, 6, P, L], BF16).ap()
        k.mod_dram = nc.dram_tensor("modulation", [5, B, D], F32).ap()
        k.rows_dram = nc.dram_tensor("token_rows", [T * P, 3 * D], F32).ap()

        k.tiles, k.rep = tiles, rep
        setup_phase(nc, k)
        with ExitStack() as stored:
            k.parts = sb("linear_parts", [P, U4 * 6 * L], BF16, ctx=stored)
            k.s_parts = [stored.enter_context(nc.semaphore(f"linear_parts_stored{u}")) for u in range(U4)]
            linear_prepare(nc, k)
            linear_attend(nc, k)
        with ExitStack() as late:
            k.parts = sb("softmax_parts", [P, U4 * 6 * L], BF16, ctx=late)
            k.s_parts = [late.enter_context(nc.semaphore(f"softmax_parts_stored{u}")) for u in range(U4)]
            softmax_prepare(nc, k)
            k.w1_all = sb("experts_w1", [P, NE * HID], ctx=late)
            k.w2_all = sb("experts_w2", [P, NE * HID], ctx=late)
            k.s_w = late.enter_context(nc.semaphore("experts_weights_in"))
            softmax_attend(nc, k)
            route_phase(nc, k)


def setup_phase(nc, k):
    with ExitStack() as ctx:
        def sb(name, shape, dt=F32):
            return ctx.enter_context(nc.sbuf_tensor(name, shape, dt))
        def sem(name):
            return ctx.enter_context(nc.semaphore(name))
        wl_raw = sb("wl_raw", [P, 3, D])
        wo_raw = sb("wo_raw", [P, D])
        wo_pos = sb("wo_pos", [P, D])
        bv_raw = sb("bv_raw", [P, D])
        ws_raw = sb("ws_raw", [P, 3 * D])
        c_raw = sb("c_raw", [B, D])
        c_exp = sb("c_exp", [B, D])
        c_rec = sb("c_rec", [B, D])
        c_silu = sb("c_silu", [B, D])
        ct = sb("ct", [P, B])
        wm = sb("wm", [P, NM * D])
        gamma_r = sb("gamma_r", [B, D])
        beta_r = sb("beta_r", [B, D])
        sgn = sb("sgn", [B, 2, D])
        mag = sb("mag", [B, 2, D])
        mrow = sb("mrow", [B, 5, D])
        s_c = sem("conditioning_in")
        s_w = sem("weights_in")
        s_x = sem("x_in")
        s_v = sem("vector_step")
        s_e = sem("silu_exp")
        s_t = sem("transposed")
        s_m = sem("modulation_ready")
        s_z = sem("pool_cleared")
        s_mr = sem("modulation_rows")
        s_md = sem("modulation_stored")

        def row(ap, p, n):
            return ap.rearrange("(o d) -> o d", o=1).to_broadcast([p, n])

        loads = [
            (ws_raw[:], k.w_qkv),
            (wo_raw[:], k.wout),
            (bv_raw[:], row(k.bqkv[2 * D:3 * D], P, D)),
            (gamma_r[:], row(k.gamma, B, D)),
            (beta_r[:], row(k.beta, B, D)),
        ]
        for z in range(2):
            for half in range(2):
                rows_of = k.wqkv[z * D:(z + 1) * D, :].rearrange("(s h e) d -> h e s d", h=2, e=E)
                bias_of = k.bqkv[z * D:(z + 1) * D].rearrange("(s h e o) -> h e s o", h=2, e=E, o=1)
                loads.append((wl_raw[64 * half:64 * half + 64, z, :], rows_of[half]))
                loads.append((k.bq2[64 * half:64 * half + 64, z:z + 1], bias_of[half]))
        for p in range(0, H, GH):
            vrows = k.wqkv[2 * D:3 * D, :].rearrange("(j h e) d -> h j e d", h=2, e=E)
            loads.append((wl_raw[E * p:E * (p + GH), 2, :], vrows[LIN_HALF[p], LIN_SLOT[p]:LIN_SLOT[p] + GH]))
        NL = len(loads)
        with nc.Block() as block:

            @block.sync
            def _(sp):
                for dst, src in ((c_raw[:], k.c_in), (k.cst[:], k.consts), (wm[:], k.wmod)):
                    sp.dma_start(dst, src).then_inc(s_c, 16)
                xv = k.x.rearrange("b (c p) d -> p (b c) d", p=P)
                for i in range(4):
                    sp.dma_start(k.tiles(k.x_all[:], T)[:, i * C * 2:(i + 1) * C * 2, :],
                                 xv[:, i * C * 2:(i + 1) * C * 2, :]).then_inc(s_x, 16)
                with nc.allow_non_contiguous_dma("columns of biases"):
                    for dst, src in loads:
                        sp.dma_start(dst, src).then_inc(s_w, 16)
                sp.wait_ge(s_mr, 5)
                sp.dma_start(k.mod_dram.rearrange("i b d -> b i d"), mrow[:]).then_inc(s_md, 16)
                sp.wait_ge(s_x, 64)
                sp.wait_ge(s_md, 16)

            @block.gpsimd
            def _(pool):
                pool.memset(k.halfneg[:], -0.5)
                for u in range(2):
                    pool.memset(k.vp[u][:], 1.0).then_inc(s_z, 1)
                for u in range(2):
                    pool.memset(k.qs[u][:], 0.0).then_inc(s_z, 1)
                pool.wait_ge(s_z, 4)
                pool.wait_ge(s_v, CLEARED)
                pool.memset(k.ks[1][32:64, 0], 1.0)
                pool.memset(k.ks[1][96:128, 1], 1.0)

            @block.scalar
            def _(act):
                act.wait_ge(s_c, 48)
                act.activation(c_exp[:], c_raw[:], ACT.Exp, scale=-1.0).then_inc(s_e, 1)
                act.wait_ge(s_v, 1)
                for half in range(2):
                    ones = k.ks[0][64 * half + 32:64 * half + 64, half]
                    act.activation(ones, ones, ACT.Copy, bias=1.0)
                act.wait_ge(s_m, 2)
                act.activation(mrow[:, 2, :], k.bank[3][0:B, 2 * D:3 * D], ACT.Copy, bias=1.0).then_inc(s_mr, 1)
                act.activation(mrow[:, 3, :], k.bank[3][0:B, D:2 * D], ACT.Copy).then_inc(s_mr, 1)

            @block.tensor
            def _(pe):
                pe.wait_ge(s_v, SILU)
                pe.transpose(k.bank[1][:, 0:B], c_silu[:], k.ident[0:B, 0:B]).then_inc(s_t, 1)
                pe.wait_ge(s_v, CT)
                for j in range(2):
                    last = pe.matmul(k.bank[2][:, j * B:(j + 1) * B], wm[:, j * D:(j + 1) * D], ct[:],
                                     start=True, stop=True)
                last.then_inc(s_m, 1)
                pe.matmul(k.bank[3][0:B, :], ct[:], wm[:, 2 * D:NM * D], start=True, stop=True).then_inc(s_m, 1)
                pe.wait_ge(s_w, 16 * NL)
                for z in range(3):
                    pe.transpose(k.bank[0][:, z * P:(z + 1) * P], wl_raw[:, z, :], k.ident).then_inc(s_t, 1)
                pe.wait_ge(s_v, WO)
                pe.transpose(k.bank[0][:, 3 * P:4 * P], wo_pos[:], k.ident).then_inc(s_t, 1)

            @block.vector
            def _(dve):
                step = [0]

                def done(ins):
                    step[0] += 1
                    ins.then_inc(s_v, 1)

                def after():
                    dve.wait_ge(s_v, step[0])

                done(dve.memset(k.ks[0][:], 0.0))
                dve.wait_ge(s_e, 1)
                done(dve.tensor_scalar(c_exp[:], c_exp[:], 1.0, None, ALU.add))
                after()
                done(dve.reciprocal(c_rec[:], c_exp[:]))
                after()
                done(dve.tensor_tensor(c_silu[:], c_raw[:], c_rec[:], ALU.mult))
                assert step[0] == SILU
                dve.wait_ge(s_t, 1)
                done(dve.tensor_copy(ct[:], k.bank[1][:, 0:B]))
                assert step[0] == CT
                done(dve.memset(k.ks[1][:], 0.0))
                assert step[0] == CLEARED
                dve.wait_ge(s_m, 1)
                done(dve.tensor_copy(k.sat[:], k.bank[2][:, 0:B]))
                done(dve.tensor_scalar(k.ca1t[:], k.bank[2][:, B:2 * B], 1.0, None, ALU.add))
                dve.wait_ge(s_m, 2)
                dve.wait_ge(s_mr, 2)
                mods = k.bank[3][0:B, :]
                gates = mods.rearrange("p (i d) -> p i d", i=4)[:, 0:4:3, :]
                done(dve.tensor_scalar(sgn[:], gates, 0.0, 2.0, ALU.is_ge, ALU.mult))
                after()
                done(dve.tensor_scalar(sgn[:], sgn[:], -1.0, None, ALU.add))
                after()
                done(dve.tensor_tensor(mag[:], gates, sgn[:], ALU.mult))
                after()
                done(dve.tensor_scalar(mag[:], mag[:], 0.25, None, ALU.max))
                after()
                dve.tensor_tensor(mrow[:, 4, :], mag[:, 1], sgn[:, 1], ALU.mult).then_inc(s_mr, 1)
                done(dve.tensor_tensor(mag[:, 0], mag[:, 0], sgn[:, 0], ALU.mult))
                after()
                dve.wait_ge(s_w, 16 * NL)
                for half in range(2):
                    for dst, src in ((wo_pos[:], wo_raw[:]), (k.BV, bv_raw[:])):
                        done(dve.tensor_copy(
                            dst.rearrange("p (a h f) -> p a h f", a=2, h=2)[:, :, half, :].rearrange("p a (j e) -> p a j e", e=E),
                            src.rearrange("p (a j h e) -> p a j h e", a=2, h=2, e=E)[:, :, :, half, :]))
                assert step[0] == WO
                dve.tensor_tensor(mrow[:, 0, :], mag[:, 0], gamma_r[:], ALU.mult).then_inc(s_mr, 1)
                dve.tensor_tensor(mrow[:, 1, :], mag[:, 0], beta_r[:], ALU.mult).then_inc(s_mr, 1)
                for z in range(2):
                    for half in range(2):
                        done(dve.tensor_copy(
                            k.wsm[:, z * D + 64 * half:z * D + 64 * half + 64].rearrange("p (e s) -> p s e", e=E),
                            ws_raw[:, z * D:(z + 1) * D].rearrange("p (s h e) -> p s h e", h=2, e=E)[:, :, half, :]))
                for half in range(2):
                    done(dve.tensor_copy(
                        k.wsm[:, 2 * D:3 * D].rearrange("p (g h j e) -> p g h j e", g=G, h=2, e=E)[:, :, half],
                        ws_raw[:, 2 * D:3 * D].rearrange("p (g j h e) -> p g j h e", g=G, h=2, e=E)[:, :, :, half, :]))
                done(dve.tensor_scalar(k.bq2[:, 2:4], k.bq2[:, 0:2], FEAT_EPS, None, ALU.add))
                dve.wait_ge(s_t, 5)
                done(dve.tensor_copy(k.wlt[:], k.bank[0][:, 0:3 * P]))
                done(dve.tensor_copy(k.woutt[:], k.bank[0][:, 3 * P:4 * P]))
                after()


SILU, CT, CLEARED, WO = 4, 5, 6, 17


def late_loads(nc, sp, k, sem):
    def row(ap, n):
        return ap.rearrange("(o d) -> o d", o=1).to_broadcast([P, n])

    loads = [
        (k.BO, row(k.bout, D)),
        (k.gatew[:], k.gate_w),
        (k.gateb[0:NE, :], k.gate_b.rearrange("(e o) -> e o", o=1)),
        (k.mod4[:].rearrange("p (o f) -> p o f", o=1),
         k.mod_dram[0:4].rearrange("(o i) b d -> o (i b d)", o=1).unsqueeze(0).to_broadcast([P, 1, 4 * B * D])),
        (k.gb_all[:].rearrange("p (o f) -> p o f", o=1),
         k.mod_dram[4:5].rearrange("o b d -> o (b d)").unsqueeze(0).to_broadcast([P, 1, B * D])),
    ]
    for i, v in enumerate((k.ln1_w, k.ln1_b, k.ln2_w, k.ln2_b)):
        loads.append((k.lnw[:, i:i + 1], v.rearrange("(d o) -> d o", o=1)))
    prow = k.w_proj.rearrange("(j h e) d -> h j e d", h=2, e=E)
    for q in range(0, H, 2):
        loads.append((k.wproj[E * q:E * (q + 2), :], prow[SOFT_HALF[q], SOFT_SLOT[q]:SOFT_SLOT[q] + 2]))
    with nc.allow_non_contiguous_dma("columns of gains and shifts"):
        for dst, src in loads:
            sp.dma_start(dst, src).then_inc(sem, 16)
    return len(loads)


def wait(eng, sem, value):
    if isinstance(value, int) and value <= 0:
        return
    eng.wait_ge(sem, value)


def paired(eng, body):
    body(0, True, False)
    with eng.Fori(1, B // 2 - 1) as it:
        body(it, False, False)
    body(B // 2 - 1, False, True)


U4 = 4


ROUNDS = B // U4


def part(parts, u, z, i):
    return parts[:, (6 * u + 3 * z + i) * L:(6 * u + 3 * z + i + 1) * L]


def store_parts(sp, k, parts, it, u, s_p3, s_ps):
    sp.wait_ge(s_p3, it * 2 * U4 + 2 * u + 2)
    sp.dma_start(k.parts_dram[it * U4 + u:it * U4 + u + 1].rearrange("b z p l -> p (b z) l"),
                 k.tiles(parts[:, u * 6 * L:(u + 1) * 6 * L], 6)).then_inc(s_ps[u], 16)


def all_parts_stored(sp, k):
    for u in range(U4):
        sp.wait_ge(k.s_parts[u], 16 * ROUNDS + 16)


STACK_LOADS = [(side, half, i) for i in range(3) for side in range(2) for half in range(2)]
N_STACK = len(STACK_LOADS) * 16


def load_stack(sp, k, u, b, side, half, i):
    rows, first = 3 - i, (0, 3, 5)[i]
    r = 64 * half + E * first
    dst = (k.ks[u][r:r + E * rows, half] if side else k.qs[u][r:r + E * rows]).rearrange("p s l -> p (s l)")
    src = k.parts_dram[bass.ds(b, 1)].rearrange("b (z i) (h e s) l -> z i h (b e) (s l)", z=2, h=2, e=E)[side]
    src = src[0:rows, half] if side else src[i:i + 1, half].to_broadcast([rows, E, S * L])
    sp.dma_start(dst, src).then_inc(k.s_stk[u], 16)


STAT_STEPS = U4 + 2


def norm_stats(dve, k, st, mv, ve, src, s_st, s_mv, s_ve, rounds, steps=range(STAT_STEPS)):
    N = U4 * C
    if 0 in steps:
        dve.memset(k.spare[:, 0:1], 0.0)
    for u in steps:
        if u < U4:
            for i in range(u * C, u * C + C):
                dve.bn_stats(st[:, i, :], src(i)).then_inc(s_st, 1)
        if 1 <= u <= U4:
            dve.wait_ge(s_st, rounds * N + u * C)
            dve.memset(k.spare[:, u:u + 1], 0.0)
            for i in range((u - 1) * C, u * C):
                dve.bn_aggr(mv[:, i, :], st[:, i, :]).then_inc(s_mv, 1)
        if u >= 2:
            dve.wait_ge(s_mv, rounds * N + (u - 1) * C)
            dve.tensor_scalar(ve[:, (u - 2) * C:(u - 1) * C], mv[:, (u - 2) * C:(u - 1) * C, 1], LN_EPS, None,
                              ALU.add).then_inc(s_ve, 1)


def rstd(pool, k, rs, ve, u, s_ve, s_rs, rounds):
    pool.wait_ge(s_ve, rounds * U4 + u + 1)
    pool.tensor_tensor(rs[:, u * C:(u + 1) * C], ve[:, u * C:(u + 1) * C], k.halfneg[:], ALU.pow).then_inc(s_rs, 1)


def linear_prepare(nc, k):
    N = U4 * C
    with ExitStack() as ctx:
        def sb(name, shape, dt=F32):
            return ctx.enter_context(nc.sbuf_tensor(name, shape, dt))
        def sem(name):
            return ctx.enter_context(nc.semaphore(name))
        st = sb("a_st", [P, N, 6])
        mv = sb("a_mv", [P, N, 2])
        ve = sb("a_ve", [P, N])
        rs = sb("a_rs", [P, N])
        xn = sb("a_xn", [P, N * D])
        ht = sb("a_ht", [P, U4 * L])
        ex = sb("a_ex", [P, 2, 2, L])
        parts = k.parts
        r1 = sb("a_r1", [P, 2, L])
        fk = sb("a_fk", [P, U4, L])
        s_st, s_mv, s_ve, s_rs = sem("a_stats"), sem("a_means"), sem("a_variances"), sem("a_rstd")
        s_xn, s_tr, s_ht = sem("a_normed"), sem("a_transposed"), sem("a_h_ready")
        s_pj, s_ex, s_rl, s_ph = sem("a_projected"), sem("a_exp"), sem("a_relu"), sem("a_features")
        s_p1, s_r1, s_p2, s_p3 = sem("a_part1"), sem("a_rest1"), sem("a_part2"), sem("a_part3")
        s_v, s_vc, s_kt, s_kc = sem("a_v"), sem("a_v_copied"), sem("a_k_transposed"), sem("a_k_copied")

        s_ps = k.s_parts
        s_late = sem("a_late_loads")

        with nc.Block() as block:

            @block.sync
            def _(sp):
                late = late_loads(nc, sp, k, s_late)
                for u in range(U4):
                    sp.sem_inc(s_ps[u], 16)
                for it in range(ROUNDS):
                    for u in range(U4):
                        store_parts(sp, k, parts, it, u, s_p3, s_ps)
                        if it == 0 and 1 <= u <= 2:
                            sp.wait_ge(s_ps[u - 1], 32)
                            for load in STACK_LOADS:
                                load_stack(sp, k, u - 1, u - 1, *load)
                sp.wait_ge(s_late, 16 * late)

            @block.vector
            def _(dve):
                def stats(it, steps):
                    norm_stats(dve, k, st, mv, ve, lambda i: k.x_all[:, (it * N + i) * D:(it * N + i + 1) * D],
                               s_st, s_mv, s_ve, it, steps)

                def normalise(it):
                    for i in range(N):
                        if i % C == 0:
                            dve.wait_ge(s_rs, it * U4 + i // C + 1)
                        if i == 0:
                            wait(dve, s_tr, it * N)
                        dve.tensor_scalar(xn[:, i * D:(i + 1) * D], k.x_all[:, (it * N + i) * D:(it * N + i + 1) * D],
                                          mv[:, i, 0:1], rs[:, i:i + 1], ALU.subtract, ALU.mult).then_inc(s_xn, 1)

                def feature(it, u, z):
                    return k.fq_all[:, (it * U4 + u) * L:(it * U4 + u + 1) * L] if z == 0 else fk[:, u, :]

                def features(it, u):
                    for z in range(2):
                        n = it * 2 * U4 + 2 * u + z
                        dve.wait_ge(s_pj, n + 1)
                        dve.wait_ge(s_ex, n + 1)
                        if z and u == 0:
                            wait(dve, s_kt, it * U4)
                        dve.tensor_scalar(feature(it, u, z), k.bank[4 + 2 * (u % 2) + z][:], k.bq2[:, 2 + z:3 + z],
                                          FEAT_EPS, ALU.add, ALU.max).then_inc(s_rl, 1)
                    for z in range(2):
                        dve.wait_ge(s_rl, it * 2 * U4 + 2 * u + z + 1)
                        dve.scalar_tensor_tensor(feature(it, u, z), ex[:, u % 2, z, :], 1.0, feature(it, u, z),
                                                 ALU.min, ALU.add).then_inc(s_ph, 1)

                def rests(it, u):
                    for z in range(2):
                        n = it * 2 * U4 + 2 * u + z
                        dve.wait_ge(s_ph, n + 1)
                        dve.wait_ge(s_p1, n + 1)
                        wait(dve, s_p3, n - 1)
                        dve.tensor_tensor(r1[:, z, :], feature(it, u, z), part(parts, u, z, 0),
                                          ALU.subtract).then_inc(s_r1, 1)

                def values(it):
                    for u in range(U4):
                        dve.wait_ge(s_v, it * U4 + u + 1)
                        cols = slice((it * U4 + u) * C * D, (it * U4 + u + 1) * C * D)
                        dve.tensor_tensor(k.tiles(k.v_all[:, cols], C), k.tiles(k.bank[u][:], C), k.rep(k.BV, C),
                                          ALU.add).then_inc(s_vc, 1)

                stats(0, range(STAT_STEPS))
                normalise(0)
                for it in range(ROUNDS):
                    ahead = it + 1 < ROUNDS
                    if ahead:
                        stats(it + 1, (0,))
                    for u in range(U4):
                        features(it, u)
                        if ahead and u + 1 < STAT_STEPS:
                            stats(it + 1, (u + 1,))
                        rests(it, u)
                        if u == 1:
                            values(it)
                    if ahead:
                        stats(it + 1, range(U4 + 1, STAT_STEPS))
                        normalise(it + 1)

            @block.gpsimd
            def _(pool):
                def last_part(it, u):
                    for z in range(2):
                        pool.wait_ge(s_p2, it * 2 * U4 + 2 * u + z + 1)
                        pool.tensor_tensor(part(parts, u, z, 2), r1[:, z, :], part(parts, u, z, 1),
                                           ALU.subtract).then_inc(s_p3, 1)

                for u in range(U4):
                    rstd(pool, k, rs, ve, u, s_ve, s_rs, 0)
                for it in range(ROUNDS):
                    for u in range(U4):
                        if u == U4 - 1 and it + 1 < ROUNDS:
                            for ahead in range(U4):
                                rstd(pool, k, rs, ve, ahead, s_ve, s_rs, it + 1)
                        last_part(it, u)

            @block.scalar
            def _(act):
                act.sem_inc(s_kc, U4)
                with act.Fori(0, B // U4) as it:
                    def h_out(u):
                        act.wait_ge(s_tr, it * N + C * (u + 1))
                        act.activation(ht[:, u * L:(u + 1) * L], k.bank[u][:], ACT.Identity,
                                       bias=k.sat[:, bass.ds(it * U4 + u, 1)],
                                       scale=k.ca1t[:, bass.ds(it * U4 + u, 1)]).then_inc(s_ht, 1)

                    def exponentials(u):
                        for z in range(2):
                            act.wait_ge(s_pj, it * 2 * U4 + 2 * u + z + 1)
                            act.activation(ex[:, u % 2, z, :], k.bank[4 + 2 * (u % 2) + z][:], ACT.Exp,
                                           bias=k.bq2[:, z:z + 1]).then_inc(s_ex, 1)

                    def first_parts(u):
                        for z in range(2):
                            n = 2 * u + z
                            f = k.fq_all[:, bass.ds(it * (U4 * L) + u * L, L)] if z == 0 else fk[:, u, :]
                            act.wait_ge(s_ph, it * 2 * U4 + n + 1)
                            if z == 0:
                                act.wait_ge(s_ps[u], it * 16 + 16)
                            act.activation(part(parts, u, z, 0),
                                           f, ACT.Copy).then_inc(s_p1, 1)

                    def second_parts(u):
                        for z in range(2):
                            n = 2 * u + z
                            act.wait_ge(s_r1, it * 2 * U4 + n + 1)
                            act.activation(part(parts, u, z, 1),
                                           r1[:, z, :], ACT.Copy).then_inc(s_p2, 1)

                    h_out(0)
                    h_out(1)
                    exponentials(0)
                    h_out(2)
                    h_out(3)
                    for u in range(U4):
                        first_parts(u)
                        if u + 1 < U4:
                            exponentials(u + 1)
                        second_parts(u)
                    for u in range(U4):
                        act.wait_ge(s_kt, it * U4 + u + 1)
                        act.activation(k.h_all[:, bass.ds(it * (N * D) + u * C * D, C * D)], k.bank[u][:],
                                       ACT.Copy).then_inc(s_kc, 1)

            @block.tensor
            def _(pe):
                with pe.Fori(0, B // U4) as it:
                    def turn(u):
                        pe.wait_ge(s_kc, it * U4 + u + 1)
                        for c in range(C):
                            i = u * C + c
                            pe.wait_ge(s_xn, it * N + i + 1)
                            pe.transpose(k.bank[u][:, c * P:(c + 1) * P], xn[:, i * D:(i + 1) * D],
                                         k.ident).then_inc(s_tr, 1)

                    def qk(u):
                        pe.wait_ge(s_ht, it * U4 + u + 1)
                        if u >= 2:
                            pe.wait_ge(s_rl, it * 2 * U4 + 2 * (u - 1))
                        for z in range(2):
                            pe.matmul(k.bank[4 + 2 * (u % 2) + z][:], k.wlt[:, z * D:(z + 1) * D],
                                      ht[:, u * L:(u + 1) * L], start=True, stop=True).then_inc(s_pj, 1)

                    turn(0)
                    turn(1)
                    qk(0)
                    turn(2)
                    turn(3)
                    qk(1)
                    for u in range(U4):
                        pe.wait_ge(s_ht, it * U4 + u + 1)
                        for c in range(C):
                            last = pe.matmul(k.bank[u][:, c * P:(c + 1) * P],
                                             ht[:, u * L + c * P:u * L + (c + 1) * P],
                                             k.wlt[:, 2 * D:3 * D], start=True, stop=True)
                        last.then_inc(s_v, 1)
                    qk(2)
                    qk(3)
                    for u in range(U4):
                        pe.wait_ge(s_vc, it * U4 + u + 1)
                        pe.wait_ge(s_ph, it * 2 * U4 + 2 * u + 2)
                        for c in range(C):
                            last = pe.transpose(k.bank[u][:, c * P:(c + 1) * P], fk[:, u, c * P:(c + 1) * P], k.ident)
                        last.then_inc(s_kt, 1)


R4 = 4


def linear_attend(nc, k):
    with ExitStack() as ctx:
        def sb(name, shape, dt=F32):
            return ctx.enter_context(nc.sbuf_tensor(name, shape, dt))
        def sem(name):
            return ctx.enter_context(nc.semaphore(name))
        qs, ks = k.qs, k.ks
        kt = [sb(f"b_kt{i}", [P, C * D]) for i in range(2)]
        vp = k.vp
        am = sb("b_am", [P, R4, GH, P])
        spad = [sb(f"b_spad{i}", [P, C - 1, H * VW]) for i in range(2)]
        nt = sb("b_nt", [P, 2, G * P])
        den = sb("b_den", [P, 2, H])
        on = sb("b_on", [P, 2, D])
        ot = sb("b_ot", [P, 2, D])
        s_init, s_pad, s_vp = sem("b_init"), sem("b_states_cleared"), sem("b_values")
        s_ktl = [sem(f"b_k_loaded{i}") for i in range(2)]
        s_at, s_am, s_sm, s_sp = sem("b_products"), sem("b_masked"), sem("b_state"), sem("b_state_masked")
        s_nm, s_nt, s_tr, s_de = sem("b_numerators"), sem("b_numerators_out"), sem("b_turned"), sem("b_denominators")
        s_rc, s_on, s_oT, s_oc = sem("b_reciprocals"), sem("b_normalised"), sem("b_output_turned"), sem("b_output_copied")
        s_y, s_yc = sem("b_projected"), sem("b_projected_out")
        b_at = [k.bank[0], k.bank[1]]
        b_nm = [k.bank[2], k.bank[3]]
        b_state, b_tr, b_ot, b_y = k.bank[4], k.bank[5], k.bank[6], k.bank[7]
        NU = C * G
        STATE_AT = (7, 10, 13)
        EPS = FEAT_EPS * E ** 0.5

        with nc.Block() as block:

            @block.sync
            def _(sp):
                all_parts_stored(sp, k)
                with sp.Fori(1, B // 2) as it:
                    for u in range(2):
                        sp.wait_ge(s_nm, it * (2 * NU) + (u - 1) * NU)
                        sp.dma_start(kt[u][:], k.h_all[:, bass.ds(it * (2 * C * D) + u * C * D, C * D)]).then_inc(s_ktl[u], 16)
                        for load in STACK_LOADS:
                            load_stack(sp, k, u, it * 2 + u, *load)

            @block.tensor
            def _(pe):
                def state(it, b, u, c):
                    if c == 0:
                        wait(pe, s_ktl[u], it * 16)
                        wait(pe, s_vp, b + 1)
                    wait(pe, s_sp, b * (C - 1) + c)
                    at_once = isinstance(b, int) and b < 2
                    pe.matmul(b_state[:, 0:H * (E + 1)],
                              k.h_all[:, (b * C + c) * D:(b * C + c + 1) * D] if at_once else kt[u][:, c * D:(c + 1) * D],
                              vp[u][:, c], start=(c == 0), stop=(c == C - 2),
                              skip_group_check=True).then_inc(s_sm, 1)

                def products(it, b, u, n):
                    c, g = n // G, n % G
                    if n == 0:
                        wait(pe, k.s_stk[u], it * N_STACK + N_STACK)
                    wait(pe, s_am, b * NU + n - 1)
                    for j in range(GH):
                        half, slot = LIN_HALF[GH * g + j], LIN_SLOT[GH * g + j]
                        last = pe.matmul(b_at[n % 2][:, j * P:(j + 1) * P],
                                         ks[u][:, half, slot, c * P:(c + 1) * P],
                                         qs[u][:, slot, c * P:(c + 1) * P],
                                         start=True, stop=True)
                    last.then_inc(s_at, 1)

                def numerators(b, u, n):
                    c, g = n // G, n % G
                    cols = slice(g * P, (g + 1) * P)
                    if g == 0:
                        wait(pe, s_nt, b * C + c - 1)
                    if c:
                        if g == 0:
                            wait(pe, s_sp, b * (C - 1) + c)
                        pe.matmul(b_nm[c % 2][:, cols], spad[u][:, c - 1, cols],
                                  k.fq_all[:, bass.ds(b * L + c * P, P)], start=True, stop=False,
                                  skip_group_check=True)
                    wait(pe, s_am, b * NU + n + 1)
                    for j in range(GH):
                        last = pe.matmul(b_nm[c % 2][VW * j:VW * j + E + 1, cols], vp[u][:, c, GH * g + j, :],
                                         am[:, n % R4, j, :], start=(c == 0), stop=True,
                                         tile_position=(0, VW * j), skip_group_check=True)
                    last.then_inc(s_nm, 1)

                def turn(q, c):
                    wait(pe, s_nt, q + 1)
                    wait(pe, s_on, q)
                    for g in range(G):
                        last = pe.transpose(b_tr[:, g * P:(g + 1) * P], nt[:, c % 2, g * P:(g + 1) * P], k.ident)
                    last.then_inc(s_tr, 1)

                def turn_back(q, c):
                    wait(pe, s_on, q + 1)
                    wait(pe, s_oc, q)
                    pe.transpose(b_ot[:, 0:P], on[:, c % 2, :], k.ident).then_inc(s_oT, 1)

                def project(b, q, c):
                    wait(pe, s_oc, q + 1)
                    if c == 0:
                        wait(pe, s_yc, b)
                    pe.matmul(b_y[:, c * P:(c + 1) * P], ot[:, c % 2, :], k.woutt[:],
                              start=True, stop=True).then_inc(s_y, 1)

                def body(it, first, last):
                    for u in range(2):
                        b = it * 2 + u
                        first_b, last_b = first and u == 0, last and u == 1
                        for n in range(NU):
                            c, g = n // G, n % G
                            q = b * C + c
                            if n + 2 < NU:
                                products(it, b, u, n + 2)
                            elif not last_b:
                                products(it + u, b + 1, 1 - u, n + 2 - NU)
                            if g == 1 and not (first_b and c < 2):
                                turn_back(q - 2, (c - 2) % C)
                            if g == 2 and not (first_b and c == 0):
                                turn(q - 1, (c - 1) % C)
                            if g == 3 and not (first_b and c < 2):
                                project(b, q - 2, (c - 2) % C)
                            if n in STATE_AT and not last_b:
                                state(it + u, b + 1, 1 - u, STATE_AT.index(n))
                            numerators(b, u, n)

                for n in range(2):
                    products(0, 0, 0, n)
                for c in range(C - 1):
                    state(0, 0, 0, c)
                pe.wait_ge(s_init, 2)
                pe.wait_ge(s_pad, 2)
                paired(pe, body)
                q = B * C - 1
                turn(q, C - 1)
                turn_back(q - 1, C - 2)
                project(B - 1, q - 1, C - 2)
                turn_back(q, C - 1)
                project(B - 1, q, C - 1)

            @block.gpsimd
            def _(pool):
                for u in range(2):
                    pool.memset(spad[u][:], 0.0).then_inc(s_pad, 1)

            @block.vector
            def _(dve):
                def masked(b, n):
                    wait(dve, s_at, b * NU + n + 1)
                    wait(dve, s_nm, b * NU + n - R4 + 1)
                    dve.tensor_tensor(am[:, n % R4, :, :], k.tiles(b_at[n % 2][:], GH), k.rep(k.causal, GH),
                                      ALU.mult).then_inc(s_am, 1)

                def state(b, u, c):
                    wait(dve, s_sm, b * (C - 1) + c + 1)
                    dve.tensor_tensor(spad[u][:, c, :].rearrange("p (h w) -> p h w", h=H)[:, :, 0:E + 1],
                                      b_state[:, 0:H * (E + 1)].rearrange("p (h w) -> p h w", h=H),
                                      k.hmask.unsqueeze(2).to_broadcast([P, H, E + 1]),
                                      ALU.mult).then_inc(s_sp, 1)

                def normalise(q, c):
                    wait(dve, s_tr, q + 1)
                    heads = b_tr[:].rearrange("p (h w) -> p h w", h=H)
                    dve.tensor_scalar(den[:, c % 2, :], heads[:, :, E], EPS, None, ALU.add).then_inc(s_de, 1)
                    wait(dve, s_de, q + 1)
                    dve.reciprocal(den[:, c % 2, :], den[:, c % 2, :]).then_inc(s_rc, 1)
                    wait(dve, s_rc, q + 1)
                    dve.tensor_tensor(on[:, c % 2, :].rearrange("p (h e) -> p h e", h=H), heads[:, :, 0:E],
                                      den[:, c % 2, :].unsqueeze(2).to_broadcast([P, H, E]),
                                      ALU.mult).then_inc(s_on, 1)

                def output(b):
                    wait(dve, s_y, b * C + C)
                    dve.tensor_tensor(k.tiles(k.v_all[:, bass.ds(b * (C * D), C * D)], C), k.tiles(b_y[:], C),
                                      k.rep(k.BO, C), ALU.add).then_inc(s_yc, 1)

                def body(it, first, last):
                    for u in range(2):
                        b = it * 2 + u
                        first_b, last_b = first and u == 0, last and u == 1
                        for n in range(NU):
                            c, g = n // G, n % G
                            masked(b, n)
                            if g == 0 and not (first_b and c < 2):
                                normalise(b * C + c - 2, (c - 2) % C)
                            if n == 10 and not first_b:
                                output(b - 1)
                            if n - 2 in STATE_AT and not last_b:
                                state(b + 1, 1 - u, STATE_AT.index(n - 2))

                for bank in b_nm:
                    dve.memset(bank[:], 0.0).then_inc(s_init, 1)
                dve.wait_ge(s_pad, 1)
                for c in range(C - 1):
                    state(0, 0, c)
                dve.wait_ge(s_pad, 2)
                paired(dve, body)
                for c in (C - 2, C - 1):
                    normalise((B - 1) * C + c, c)
                output(B - 1)

            @block.scalar
            def _(act):
                def values(b, u):
                    wait(act, s_nm, (b - 1) * NU)
                    act.activation(vp[u][:, :, :, 0:E], k.v_all[:, bass.ds(b * (C * D), C * D)]
                                   .rearrange("p (c h e) -> p c h e", c=C, h=H), ACT.Copy).then_inc(s_vp, 1)

                def numerators_out(q, c):
                    wait(act, s_nm, (q + 1) * G)
                    wait(act, s_tr, q - 1)
                    act.activation(nt[:, c % 2, :], b_nm[c % 2][:], ACT.Copy).then_inc(s_nt, 1)

                def output_out(q, c):
                    wait(act, s_oT, q + 1)
                    act.activation(ot[:, c % 2, :], b_ot[:, 0:P], ACT.Copy).then_inc(s_oc, 1)

                def body(it, first, last):
                    for u in range(2):
                        b = it * 2 + u
                        for c in range(C):
                            q = b * C + c
                            if c == 0 and not (last and u == 1):
                                values(b + 1, 1 - u)
                            numerators_out(q, c)
                            if not (first and u == 0 and c == 0):
                                output_out(q - 1, (c - 1) % C)

                values(0, 0)
                paired(act, body)
                output_out(B * C - 1, C - 1)


def softmax_prepare(nc, k):
    N = U4 * C
    with ExitStack() as ctx:
        def sb(name, shape, dt=F32):
            return ctx.enter_context(nc.sbuf_tensor(name, shape, dt))
        def sem(name):
            return ctx.enter_context(nc.semaphore(name))
        st = sb("c_st", [P, N, 6])
        mv = sb("c_mv", [P, 3, N, 2])
        ve = sb("c_ve", [P, N])
        rs = sb("c_rs", [P, 3, N])
        xn = sb("c_xn", [P, N * D])
        tmp = sb("c_tmp", [P, N * D])
        ht = sb("c_ht", [P, U4 * L])
        r1 = sb("c_r1", [P, 2, L])
        parts = k.parts
        s_st, s_mv, s_ve, s_rs = sem("c_stats"), sem("c_means"), sem("c_variances"), sem("c_rstd")
        s_z, s_t1, s_ln, s_xn = sem("c_x_shifted"), sem("c_scaled"), sem("c_layernorms"), sem("c_normed")
        s_tr, s_ht, s_pj = sem("c_transposed"), sem("c_h_ready"), sem("c_projected")
        s_p1, s_r1, s_p2, s_p3 = sem("c_part1"), sem("c_rest1"), sem("c_part2"), sem("c_part3")
        s_v, s_vc = sem("c_v"), sem("c_v_copied")

        s_ps = k.s_parts

        with nc.Block() as block:

            @block.sync
            def _(sp):
                for u in range(U4):
                    sp.sem_inc(s_ps[u], 16)
                for it in range(ROUNDS):
                    for u in range(U4):
                        store_parts(sp, k, parts, it, u, s_p3, s_ps)
                        if it == 0 and 1 <= u <= 1:
                            sp.wait_ge(s_ps[u - 1], 32)
                            for load in STACK_LOADS:
                                load_stack(sp, k, u - 1, u - 1, *load)

            @block.vector
            def _(dve):
                LAYERS = ((k.v_all, k.x_all, k.G_OF), (k.x_all, k.h_all, k.CB_OF))

                def tile(a, it, i):
                    return a[:, (it * N + i) * D:(it * N + i + 1) * D]

                def row(it, i, vector):
                    b = it * U4 + i // C
                    return k.mod4[:, vector + b * D:vector + (b + 1) * D]

                def scaled(it, m):
                    src, _, gain = LAYERS[m]
                    norm_stats(dve, k, st, mv[:, m], ve, lambda i: tile(src, it, i), s_st, s_mv, s_ve, it * 3 + m)
                    for i in range(N):
                        dve.scalar_tensor_tensor(tmp[:, i * D:(i + 1) * D], tile(src, it, i), mv[:, m, i, 0:1],
                                                 row(it, i, gain), ALU.subtract, ALU.mult).then_inc(s_t1, 1)

                def shifted(it, m):
                    dst = LAYERS[m][1]
                    for i in range(N):
                        if i % C == 0:
                            dve.wait_ge(s_rs, (it * 3 + m) * U4 + i // C + 1)
                            dve.wait_ge(s_t1, (it * 2 + m) * N + i + C)
                            if m == 0:
                                dve.wait_ge(s_z, it * U4 + i // C + 1)
                        dve.scalar_tensor_tensor(tile(dst, it, i), tmp[:, i * D:(i + 1) * D], rs[:, m, i:i + 1],
                                                 tile(k.x_all, it, i) if m == 0 else row(it, i, k.SB_OF),
                                                 ALU.mult, ALU.add).then_inc(s_ln, 1)
                    dve.wait_ge(s_ln, (it * 2 + m + 1) * N)

                def normalised(it):
                    norm_stats(dve, k, st, mv[:, 2], ve, lambda i: tile(k.h_all, it, i), s_st, s_mv, s_ve, it * 3 + 2)
                    for i in range(N):
                        if i % C == 0:
                            dve.wait_ge(s_rs, (it * 3 + 2) * U4 + i // C + 1)
                            if i == 0:
                                wait(dve, s_tr, it * U4)
                        dve.tensor_scalar(xn[:, i * D:(i + 1) * D], tile(k.h_all, it, i),
                                          mv[:, 2, i, 0:1], rs[:, 2, i:i + 1], ALU.subtract, ALU.mult).then_inc(s_xn, 1)

                def rests(it, u):
                    for z in range(2):
                        n = it * 2 * U4 + 2 * u + z
                        dve.wait_ge(s_p1, n + 1)
                        wait(dve, s_p3, n - 1)
                        dve.tensor_tensor(r1[:, z, :], k.bank[4 + 2 * (u % 2) + z][:], part(parts, u, z, 0),
                                          ALU.subtract).then_inc(s_r1, 1)

                scaled(0, 0)
                for it in range(ROUNDS):
                    if it == 0:
                        shifted(it, 0)
                    scaled(it, 1)
                    shifted(it, 1)
                    normalised(it)
                    ahead = it + 1 < ROUNDS
                    if ahead:
                        scaled(it + 1, 0)
                    for u in range(U4):
                        rests(it, u)
                        if ahead and u == 1:
                            shifted(it + 1, 0)

            @block.gpsimd
            def _(pool):
                def first(it):
                    for u in range(U4):
                        b = it * U4 + u
                        xu = k.tiles(k.x_all[:, b * C * D:(b + 1) * C * D], C)
                        pool.tensor_tensor(xu, xu, k.rep(k.mod4[:, k.B_OF + b * D:k.B_OF + (b + 1) * D], C),
                                           ALU.add).then_inc(s_z, 1)
                        rstd(pool, k, rs[:, 0], ve, u, s_ve, s_rs, it * 3)

                first(0)
                for it in range(ROUNDS):
                    for m in range(1, 3):
                        for u in range(U4):
                            rstd(pool, k, rs[:, m], ve, u, s_ve, s_rs, it * 3 + m)
                    if it + 1 < ROUNDS:
                        first(it + 1)
                    for n in range(2 * U4):
                        u, z = n // 2, n % 2
                        pool.wait_ge(s_p2, it * 2 * U4 + n + 1)
                        pool.tensor_tensor(part(parts, u, z, 2), r1[:, z, :], part(parts, u, z, 1),
                                           ALU.subtract).then_inc(s_p3, 1)

            @block.scalar
            def _(act):
                act.sem_inc(s_vc, 1)
                with act.Fori(0, B // U4) as it:
                    def v_out(u):
                        act.wait_ge(s_v, it * U4 + u + 1)
                        act.activation(k.v_all[:, bass.ds(it * (N * D) + u * C * D, C * D)], k.bank[u][:],
                                       ACT.Copy).then_inc(s_vc, 1)

                    for u in range(U4):
                        act.wait_ge(s_tr, it * U4 + u + 1)
                        act.activation(ht[:, u * L:(u + 1) * L], k.bank[u][:], ACT.Identity,
                                       bias=k.lnw[:, 1:2], scale=k.lnw[:, 0:1]).then_inc(s_ht, 1)
                    for u in range(U4):
                        for z in range(2):
                            act.wait_ge(s_pj, it * 2 * U4 + 2 * u + z + 1)
                            if z == 0:
                                act.wait_ge(s_ps[u], it * 16 + 16)
                            act.activation(part(parts, u, z, 0),
                                           k.bank[4 + 2 * (u % 2) + z][:], ACT.Copy).then_inc(s_p1, 1)
                        if u:
                            v_out(u - 1)
                        for z in range(2):
                            act.wait_ge(s_r1, it * 2 * U4 + 2 * u + z + 1)
                            act.activation(part(parts, u, z, 1),
                                           r1[:, z, :], ACT.Copy).then_inc(s_p2, 1)
                    v_out(U4 - 1)

            @block.tensor
            def _(pe):
                with pe.Fori(0, B // U4) as it:
                    for u in range(U4):
                        if u == 0:
                            pe.wait_ge(s_vc, it * U4 + 1)
                        pe.wait_ge(s_xn, it * N + (u + 1) * C)
                        for c in range(C):
                            i = u * C + c
                            last = pe.transpose(k.bank[u][:, c * P:(c + 1) * P], xn[:, i * D:(i + 1) * D], k.ident)
                        last.then_inc(s_tr, 1)
                    for u in range(U4):
                        pe.wait_ge(s_ht, it * U4 + u + 1)
                        if u >= 2:
                            pe.wait_ge(s_r1, it * 2 * U4 + 2 * (u - 1))
                        for z in range(2):
                            pe.matmul(k.bank[4 + 2 * (u % 2) + z][:], k.wsm[:, z * D:(z + 1) * D],
                                      ht[:, u * L:(u + 1) * L], start=True, stop=True).then_inc(s_pj, 1)
                        for c in range(C):
                            last = pe.matmul(k.bank[u][:, c * P:(c + 1) * P], ht[:, u * L + c * P:u * L + (c + 1) * P],
                                             k.wsm[:, 2 * D:3 * D], start=True, stop=True)
                        last.then_inc(s_v, 1)


def softmax_attend(nc, k):
    with ExitStack() as ctx:
        def sb(name, shape, dt=F32):
            return ctx.enter_context(nc.sbuf_tensor(name, shape, dt))
        def sem(name):
            return ctx.enter_context(nc.semaphore(name))
        qs, ks = k.qs, k.ks
        vp = k.vp
        mx = sb("d_mx", [P, 2, 4 * C])
        mt = sb("d_mt", [4 * C, 2, P], BF16)
        den = sb("d_den", [P, 2, H])
        on = sb("d_on", [P, 2, D])
        ot = sb("d_ot", [P, 2, D])
        nt = k.fq_all[:].rearrange("p (u g q) -> p u g q", u=2, g=G)
        pt = k.mod4[:].rearrange("p (r x f) -> p r x f", r=2, x=2)
        s_init, s_vp = sem("d_init"), sem("d_values")
        s_m, s_mr, s_mt, s_mc = sem("d_max_scores"), sem("d_maxima"), sem("d_maxima_turned"), sem("d_maxima_copied")
        s_row = [sem(f"d_maxima_rows{i}") for i in range(2)]
        s_zero = [sem(f"d_rows_cleared{i}") for i in range(2)]
        s_s, s_e, s_pv, s_ne = sem("d_scores"), sem("d_probs"), sem("d_values_summed"), sem("d_numerators_out")
        s_ft, s_fr, s_fo = sem("d_turned"), sem("d_reciprocals"), sem("d_normalised")
        s_fb, s_fe, s_fp, s_fh = sem("d_turned_back"), sem("d_output_copied"), sem("d_projected"), sem("d_y_ready")
        b_m, b_num, b_misc, b_s = [k.bank[0], k.bank[1]], k.bank[2], k.bank[3], k.pair
        NG = 2 * G
        SCALE = E ** -0.5
        AT_FIRST = 6

        def max_bank(n, x, banks):
            m = x % 2 if banks == 2 else (n * 16 + x) % banks
            return b_m[m][:] if m < 2 else b_s[m // 2 - 1][:, m % 2 * L:(m % 2 + 1) * L]

        with nc.Block() as block:

            @block.sync
            def _(sp):
                def rows(i, n):
                    wait(sp, s_mc, n + 1)
                    u, g = (i // G) % 2, i % G
                    for half in range(2):
                        r = 64 * half + KR
                        sp.dma_start(qs[u][r:r + 1, 2 * g:2 * g + 2, :], mt[8 * half:8 * half + 8, i % 2, :]).then_inc(s_row[i % 2], 16)

                def body(it, first, last):
                    for i in range(NG):
                        n = it * NG + i
                        u, g = i // G, i % G
                        if g < 2 and not (last and u == 1):
                            if g == 0:
                                wait(sp, s_pv, n * C)
                                for half in range(2):
                                    r = 64 * half + KR
                                    sp.dma_start(qs[1 - u][r:r + 1, :, :], qs[1 - u][r + 1:r + 2, :, :]).then_inc(s_zero[1 - u], 16)
                            for load in STACK_LOADS[6 * g:6 * g + 6]:
                                load_stack(sp, k, 1 - u, it * 2 + u + 1, *load)
                        if not (last and i == NG - 1):
                            rows(i + 1, n + 1)

                for e in range(NE):
                    sp.dma_start(k.w1_all[:, e * HID:(e + 1) * HID], k.w1[e]).then_inc(k.s_w, 16)
                    sp.dma_start(k.w2_all[:, e * HID:(e + 1) * HID].rearrange("p (c d) -> p c d", c=HC),
                                 k.w2[e].rearrange("(c p) d -> p c d", p=P)).then_inc(k.s_w, 16)
                rows(0, 0)
                all_parts_stored(sp, k)
                paired(sp, body)

            @block.gpsimd
            def _(pool):
                def body(it, first, last):
                    for u in range(2):
                        b = it * 2 + u
                        wait(pool, s_pv, (b - 1) * (G * C))
                        for c in range(C):
                            pool.tensor_copy(vp[u][:, c, :, 0:E],
                                             k.v_all[:, bass.ds(b * (C * D) + c * D, D)].rearrange("p (h e) -> p h e", h=H)
                                             ).then_inc(s_vp, 1)

                paired(pool, body)

            @block.tensor
            def _(pe):
                def max_scores(i, n, x, banks=2):
                    u, g = (i // G) % 2, i % G
                    if g == 0 and x == 0:
                        wait(pe, k.s_stk[u], (n - i) * (N_STACK // NG) + (i // NG + 1 + B // 2) * N_STACK)
                        wait(pe, s_zero[u], (n - i) * (32 // NG) + (i // NG + u) * 32)
                    qt, jj, half = x // 4, x // 2 % 2, x % 2
                    slot = 2 * g + jj
                    wait(pe, s_mr, n * 16 + x + 1 - banks)
                    pe.matmul(max_bank(n, x, banks), qs[u][:, slot, qt * P:(qt + 1) * P], ks[u][:, half, slot, :],
                              start=True, stop=True).then_inc(s_m, 1)

                def turn_maxima(i, n):
                    wait(pe, s_mr, n * 16 + 16)
                    wait(pe, s_fh, n - 1 - G)
                    pe.transpose(b_misc[0:4 * C, 0:P], mx[:, i % 2, :], k.ident).then_inc(s_mt, 1)

                def scores(i, n, kt, x):
                    u, g = i // G, i % G
                    if kt == 0 and x == 0:
                        wait(pe, s_row[i % 2], (n - i % 2) * 16 + 32)
                    wait(pe, s_e, n * 8 + 2 * kt + x - 1)
                    for half in range(2):
                        slot = 2 * g + x
                        last = pe.matmul(b_s[x][:, half * L:(half + 1) * L], ks[u][:, half, slot, kt * P:(kt + 1) * P],
                                         qs[u][:, slot, :], start=True, stop=True)
                    last.then_inc(s_s, 1)

                def values(i, n, kt):
                    u, g = (i // G) % 2, i % G
                    wait(pe, s_e, n * 8 + 2 * kt + 2)
                    if kt == 0:
                        wait(pe, s_ne, n)
                        if g == 0:
                            wait(pe, s_vp, n * 1 + C)
                    for q in range(GH):
                        last = pe.matmul(b_num[VW * q:VW * q + E + 1, :], vp[u][:, kt, GH * g + q, :],
                                         pt[:, kt % 2, q % 2, (q // 2) * L:(q // 2 + 1) * L],
                                         start=(kt == 0), stop=(kt == C - 1), tile_position=(0, VW * q),
                                         skip_group_check=True)
                    last.then_inc(s_pv, 1)

                def finish(i, n, step, turns):
                    u, c = (i // G + 1) % 2, i % G
                    f = n - G
                    if step == 0:
                        wait(pe, s_ne, n - c)
                        wait(pe, s_fh, f)
                        if turns:
                            wait(pe, s_mc, n + 2)
                        for g in range(G):
                            last = pe.transpose(b_misc[:, g * P:(g + 1) * P], nt[:, u, g, c * P:(c + 1) * P], k.ident)
                        last.then_inc(s_ft, 1)
                    elif step == 1:
                        wait(pe, s_fo, f + 1)
                        pe.transpose(b_misc[:, 0:P], on[:, c % 2, :], k.ident).then_inc(s_fb, 1)
                    else:
                        wait(pe, s_fe, f + 1)
                        pe.matmul(b_misc[:, 0:P], ot[:, c % 2, :], k.wproj[:], start=True, stop=True).then_inc(s_fp, 1)

                def body(it, first, last):
                    for i in range(NG):
                        n = it * NG + i
                        ahead = not (last and i + 2 >= NG)
                        behind = not (first and i < G)
                        for kt in range(C):
                            for x in range(2):
                                if ahead:
                                    max_scores(i + 2, n + 2, 4 * kt + x)
                                scores(i, n, kt, x)
                            if ahead:
                                max_scores(i + 2, n + 2, 4 * kt + 2)
                            if kt:
                                values(i, n, kt - 1)
                            elif not (first and i == 0):
                                values(i - 1, n - 1, C - 1)
                            if ahead:
                                max_scores(i + 2, n + 2, 4 * kt + 3)
                            if kt == 0 and not (last and i + 1 >= NG):
                                turn_maxima(i + 1, n + 1)
                            if kt and behind:
                                finish(i, n, kt - 1, not (last and i == NG - 1))

                wait(pe, s_init, 1)
                for n in range(2):
                    for x in range(16):
                        max_scores(n, n, x, AT_FIRST)
                        if n == 1 and x == AT_FIRST - 1:
                            turn_maxima(0, 0)
                pe.wait_ge(s_mr, 2 * 16 - 2)
                paired(pe, body)
                values(NG - 1, B * G - 1, C - 1)
                for c in range(C):
                    for step in range(3):
                        finish(c, B * G + c, step, False)

            @block.vector
            def _(dve):
                def maximum(i, n, x, banks=2):
                    qt, jj, half = x // 4, x // 2 % 2, x % 2
                    col = half * 8 + jj * 4 + qt
                    wait(dve, s_m, n * 16 + x + 1)
                    dve.reduce_max(mx[:, i % 2, col:col + 1], max_bank(n, x, banks), AX).then_inc(s_mr, 1)

                def normalise(i, n):
                    c, f = i % G, n - G
                    heads = b_misc[:].rearrange("p (h w) -> p h w", h=H)
                    wait(dve, s_ft, f + 1)
                    dve.reciprocal(den[:, c % 2, :], heads[:, :, E]).then_inc(s_fr, 1)
                    wait(dve, s_fr, f + 1)
                    dve.tensor_tensor(on[:, c % 2, :].rearrange("p (h e) -> p h e", h=H), heads[:, :, 0:E],
                                      den[:, c % 2, :].unsqueeze(2).to_broadcast([P, H, E]), ALU.mult).then_inc(s_fo, 1)

                def add(i, n):
                    f = n - G
                    wait(dve, s_fp, f + 1)
                    y = k.h_all[:, bass.ds(f * D, D)]
                    dve.tensor_tensor(y, y, b_misc[:, 0:P], ALU.add).then_inc(s_fh, 1)

                def body(it, first, last):
                    for i in range(NG):
                        n = it * NG + i
                        ahead = not (last and i + 2 >= NG)
                        behind = not (first and i < G)
                        for kt in range(C):
                            if ahead:
                                maximum(i + 2, n + 2, 4 * kt)
                                maximum(i + 2, n + 2, 4 * kt + 1)
                            if kt == 0 and not (first and i <= G):
                                add(i - 1, n - 1)
                            if kt == 2 and behind:
                                normalise(i, n)
                            if ahead:
                                maximum(i + 2, n + 2, 4 * kt + 2)
                                maximum(i + 2, n + 2, 4 * kt + 3)

                dve.memset(b_num[:], 0.0).then_inc(s_init, 1)
                for n in range(2):
                    for x in range(16):
                        maximum(n, n, x, AT_FIRST)
                paired(dve, body)
                add(NG - 1, B * G - 1)
                for c in range(C):
                    normalise(c, B * G + c)
                    add(c, B * G + c)

            @block.scalar
            def _(act):
                def probs(i, n, kt, x):
                    wait(act, s_s, n * 8 + 2 * kt + x + 1)
                    if x == 0:
                        wait(act, s_pv, n * C + kt - 1)
                    act.activation(pt[:, kt % 2, x, :], b_s[x][:], ACT.Exp, scale=SCALE).then_inc(s_e, 1)

                def maxima_out(i, n):
                    wait(act, s_mt, n + 1)
                    wait(act, s_row[i % 2], (n - i % 2) * 16)
                    act.activation(mt[:, i % 2, :], b_misc[0:4 * C, 0:P], ACT.Copy, scale=-1.0).then_inc(s_mc, 1)

                def output_out(i, n):
                    wait(act, s_fb, n - G + 1)
                    act.activation(ot[:, i % 2, :], b_misc[:, 0:P], ACT.Copy).then_inc(s_fe, 1)

                def numerators_out(i, n):
                    wait(act, s_pv, n * C + C)
                    act.activation(nt[:, (i // G) % 2, i % G, :], b_num[:], ACT.Copy).then_inc(s_ne, 1)

                def body(it, first, last):
                    for i in range(NG):
                        n = it * NG + i
                        for kt in range(C):
                            probs(i, n, kt, 0)
                            if kt == 1 and not (last and i + 1 >= NG):
                                maxima_out(i + 1, n + 1)
                            if kt == 3 and not (first and i < G):
                                output_out(i, n)
                            probs(i, n, kt, 1)
                            if kt == 0 and not (first and i == 0):
                                numerators_out(i - 1, n - 1)

                maxima_out(0, 0)
                paired(act, body)
                numerators_out(NG - 1, B * G - 1)
                for c in range(C):
                    output_out(c, B * G + c)


def route_phase(nc, k):
    with ExitStack() as ctx:
        def sb(name, shape, dt=F32):
            return ctx.enter_context(nc.sbuf_tensor(name, shape, dt))
        k.logits_t = k.v_all[0:NE, :]
        k.token_u = sb("e_token_u", [P, MT], U32)
        k.fetch_u = sb("e_fetch_u", [P, MT], U32)
        k.expert_i = sb("e_expert_i", [P, MT], I32)
        gate(nc, k)
        sort_tokens(nc, k)
        run_experts(nc, k)


def token_rows(k, first, tiles, column):
    return (k.rows_dram[bass.ds(first * P, tiles * P), column * D:(column + 1) * D]
            .rearrange("(c p) d -> p c d", p=P))


def gate(nc, k):
    N = U4 * C
    with ExitStack() as ctx:
        def sb(name, shape, dt=F32):
            return ctx.enter_context(nc.sbuf_tensor(name, shape, dt))
        def sem(name):
            return ctx.enter_context(nc.semaphore(name))
        st = sb("e_st", [P, N, 6])
        mv = sb("e_mv", [P, N, 2])
        ve = sb("e_ve", [P, N])
        rs = sb("e_rs", [P, N])
        xn, ht = k.fq_all[:, 0:N * D], k.fq_all[:, N * D:2 * N * D]
        s_st, s_mv, s_ve, s_rs = sem("e_stats"), sem("e_means"), sem("e_variances"), sem("e_rstd")
        s_xn = sem("e_normed")
        s_cp = [sem(f"e_normed_stored{u}") for u in range(U4)]
        s_tr, s_ht = sem("e_transposed"), sem("e_transposed_out")
        s_gr = sem("e_gates_stored")
        s_gl, s_lt = sem("e_gate_products"), sem("e_logits_out")

        with nc.Block() as block:

            @block.sync
            def _(sp):
                for u in range(U4):
                    sp.sem_inc(s_cp[u], 16)
                for b in range(B):
                    sp.dma_start(token_rows(k, b * C, C, 1), k.rep(k.gb_all[:, b * D:(b + 1) * D], C)).then_inc(s_gr, 16)
                with sp.Fori(0, B // U4) as it:
                    for u in range(U4):
                        sp.wait_ge(s_xn, it * N + (u + 1) * C)
                        sp.dma_start(token_rows(k, it * N + u * C, C, 0),
                                     k.tiles(xn[:, u * C * D:(u + 1) * C * D], C)).then_inc(s_cp[u], 16)
                for u in range(U4):
                    sp.wait_ge(s_cp[u], 16 * (B // U4) + 16)
                sp.wait_ge(s_gr, 16 * B)

            @block.vector
            def _(dve):
                with dve.Fori(0, B // U4) as it:
                    norm_stats(dve, k, st, mv, ve, lambda i: k.h_all[:, bass.ds(it * (N * D) + i * D, D)],
                               s_st, s_mv, s_ve, it)
                    dve.wait_ge(s_tr, it * U4 + 1)
                    for i in range(N):
                        if i % C == 0:
                            dve.wait_ge(s_rs, it * U4 + i // C + 1)
                            dve.wait_ge(s_cp[i // C], it * 16 + 16)
                        dve.tensor_scalar(xn[:, i * D:(i + 1) * D], k.h_all[:, bass.ds(it * (N * D) + i * D, D)],
                                          mv[:, i, 0:1], rs[:, i:i + 1], ALU.subtract, ALU.mult).then_inc(s_xn, 1)

            @block.gpsimd
            def _(pool):
                with pool.Fori(0, B // U4) as it:
                    for u in range(U4):
                        rstd(pool, k, rs, ve, u, s_ve, s_rs, it)

            @block.scalar
            def _(act):
                with act.Fori(0, B // U4) as it:
                    for u in range(U4):
                        act.wait_ge(s_tr, it * U4 + u + 2)
                        act.activation(ht[:, u * L:(u + 1) * L], k.bank[u][:], ACT.Identity,
                                       bias=k.lnw[:, 3:4], scale=k.lnw[:, 2:3]).then_inc(s_ht, 1)
                    for u in range(U4):
                        act.wait_ge(s_gl, it * U4 + u + 1)
                        act.activation(k.logits_t[:, bass.ds((it * U4 + u) * L, L)], k.bank[4 + u][0:NE, :],
                                       ACT.Identity, bias=k.gateb[0:NE, :]).then_inc(s_lt, 1)

            @block.tensor
            def _(pe):
                pe.sem_inc(s_tr, 1)
                with pe.Fori(0, B // U4) as it:
                    def turn(u):
                        pe.wait_ge(s_xn, it * N + (u + 1) * C)
                        for c in range(C):
                            i = u * C + c
                            last = pe.transpose(k.bank[u][:, c * P:(c + 1) * P], xn[:, i * D:(i + 1) * D], k.ident)
                        last.then_inc(s_tr, 1)

                    turn(0)
                    for u in range(U4):
                        if u + 1 < U4:
                            turn(u + 1)
                        pe.wait_ge(s_ht, it * U4 + u + 1)
                        pe.matmul(k.bank[4 + u][0:NE, :], k.gatew[:], ht[:, u * L:(u + 1) * L],
                                  start=True, stop=True).then_inc(s_gl, 1)
                    pe.wait_ge(s_lt, it * U4 + U4)


def sort_tokens(nc, k):
    with ExitStack() as ctx:
        def sb(name, shape, dt=F32):
            return ctx.enter_context(nc.sbuf_tensor(name, shape, dt))
        def sem(name):
            return ctx.enter_context(nc.semaphore(name))
        mx = sb("f_mx", [P, T])
        eq = sb("f_eq", [P, T, NE])
        oh = sb("f_onehot", [P, T, NE])
        tot, *cum = (k.mod4[:, i * T * NE:(i + 1) * T * NE] for i in range(3))
        over = sb("f_over", [P, NE, T])
        used = sb("f_used", [P, NE])
        ends = [sb(f"f_ends{i}", [P, NE]) for i in range(2)]
        base = sb("f_base", [P, NE])
        row = sb("f_row", [P, T, NE])
        place = sb("f_place", [P, T])
        past = sb("f_past", [P, MT, NE])
        expert = sb("f_expert", [P, MT])
        inside, ids, perm = (
            k.parts[:, first * T:(first + n) * T] for first, n in ((0, MT), (MT + 1, 2 * MT), (3 * MT + 1, P)))
        inside = inside.rearrange("p (t m) -> p t m", t=T)
        ids = ids.rearrange("p (t i m) -> p t i m", t=T, i=2)
        perm = perm.rearrange("p (t m) -> p t m", t=T)
        begin = sb("f_begin", [P, T])
        at = sb("f_at", [P, T])
        token = sb("f_token", [P, MT])
        s_oh, s_pr, s_v, s_id = sem("f_onehot_ready"), sem("f_products"), sem("f_vector_step"), sem("f_ids_ready")
        s_in = sem("f_inside_ready")
        s_pm, s_tk = sem("f_permutations"), sem("f_tokens")
        s_lg, s_xs = sem("f_logits"), sem("f_sums_stored")
        s_gy, s_xy = sem("f_gated"), sem("f_summed")
        FIRST = k.cst[:, C_FIRST:C_FIRST + NE]
        COARSE = 1.5 * 2.0 ** 23 * P
        PT = 8
        STARTS = k.cst[:, C_STARTS:C_STARTS + MT]
        INDEX = k.cst[:, C_INDEX:C_INDEX + P]
        LEFT = k.cst[:, C_LEFT:C_LEFT + T]
        ROW = k.cst[:, C_ROW:C_ROW + 1]

        def flat(ap):
            return ap.rearrange("p t e -> p (t e)")

        def across(ap, n):
            return ap.unsqueeze(2).to_broadcast([P, ap.shape[1], n])

        with nc.Block() as block:

            @block.vector
            def _(dve):
                step = [0]

                def done(ins):
                    step[0] += 1
                    ins.then_inc(s_v, 1)

                def after():
                    dve.wait_ge(s_v, step[0])

                def running_sums(src, bufs, n, width):
                    d, i = 1, 0
                    while d < n:
                        dst, w = bufs[i % 2], d * width
                        done(dve.tensor_tensor(dst[:, w:], src[:, w:], src[:, :(n - d) * width], ALU.add))
                        done(dve.tensor_copy(dst[:, 0:w], src[:, 0:w]))
                        after()
                        src, d, i = dst, 2 * d, i + 1
                    return src

                lg = k.tiles(k.bank[4][:, 0:T * NE], T)
                dve.wait_ge(s_lg, 1)
                done(dve.reduce_max(mx[:], lg, AX))
                after()
                done(dve.tensor_tensor(eq[:], lg, across(mx[:], NE), ALU.is_equal))
                after()
                done(dve.tensor_tensor(eq[:], eq[:], k.rep(FIRST, T), ALU.mult))
                after()
                done(dve.reduce_max(mx[:], eq[:], AX))
                after()
                dve.tensor_tensor(oh[:], eq[:], across(mx[:], NE), ALU.is_equal).then_inc(s_oh, 1)
                dve.wait_ge(s_pr, 1)
                done(dve.tensor_copy(tot, k.bank[1][:, 0:T * NE]))
                after()
                sums = running_sums(tot, cum, T, NE)
                count = sums[:, (T - 1) * NE:T * NE]
                done(dve.tensor_tensor(over[:], across(count, T), k.rep(STARTS[:, 0:T], NE), ALU.is_gt))
                after()
                done(dve.reduce_sum(used[:], over[:], AX))
                after()
                end = running_sums(used[:], [c[:] for c in ends], NE, 1)
                done(dve.tensor_tensor(base[:], end, used[:], ALU.subtract))
                after()
                done(dve.tensor_scalar(base[:], base[:], float(P), None, ALU.mult))
                done(dve.tensor_tensor(flat(row[:]), k.bank[0][:, 0:T * NE], tot, ALU.subtract))
                after()
                done(dve.tensor_tensor(flat(row[:]), flat(row[:]), sums, ALU.add))
                after()
                done(dve.tensor_tensor(row[:], row[:], k.rep(base[:], T), ALU.add))
                after()
                done(dve.tensor_tensor(row[:], row[:], oh[:], ALU.mult))
                after()
                done(dve.reduce_sum(place[:], row[:], AX))
                after()
                done(dve.tensor_scalar(begin[:], place[:], -(P - 1) / 2, COARSE, ALU.add, ALU.add))
                after()
                done(dve.tensor_scalar(begin[:], begin[:], -COARSE, None, ALU.add))
                after()
                done(dve.tensor_tensor(at[:], place[:], begin[:], ALU.subtract))
                dve.tensor_tensor(inside, across(begin[:], MT), k.rep(STARTS, T), ALU.is_equal).then_inc(s_in, 1)
                dve.wait_ge(s_in, 1)
                dve.tensor_tensor(ids[:, :, 1, :], inside, across(LEFT, MT), ALU.mult).then_inc(s_id, 1)
                for t in range(0, T, PT):
                    dve.tensor_tensor(perm[:, t:t + PT, :], k.rep(INDEX, PT), across(at[:, t:t + PT], P), ALU.is_equal
                                      ).then_inc(s_pm, 1)
                done(dve.tensor_tensor(past[:], across(INDEX[:, 0:MT], NE), k.rep(end, MT), ALU.is_ge))
                after()
                done(dve.reduce_sum(expert[:], past[:], AX))
                after()
                done(dve.tensor_scalar(expert[:], expert[:], float(NE - 1), None, ALU.min))
                after()
                done(dve.tensor_copy(k.expert_i[:], expert[:]))
                dve.wait_ge(s_tk, 1)
                done(dve.tensor_scalar(token[:], k.bank[2][:, MT:2 * MT], -float(P), float(T * P), ALU.mult, ALU.add))
                after()
                done(dve.tensor_tensor(token[:], token[:], k.bank[2][:, 0:MT], ALU.add))
                after()
                done(dve.tensor_copy(k.token_u[:], token[:]))
                done(dve.tensor_scalar(token[:], token[:], float(T * P - 1), None, ALU.min))
                after()
                done(dve.tensor_copy(k.fetch_u[:], token[:]))
                after()

            @block.scalar
            def _(act):
                act.wait_ge(s_in, 1)
                act.activation(ids[:, :, 0, :], inside, ACT.Copy, scale=ROW).then_inc(s_id, 1)

            @block.sync
            def _(sp):
                for b in range(B):
                    sp.wait_ge(s_xy, b + 1)
                    sp.dma_start(token_rows(k, b * C, C, 2), k.tiles(k.x_all[:, b * C * D:(b + 1) * C * D], C)
                                 ).then_inc(s_xs, 16)
                sp.wait_ge(s_xs, 16 * B)

            @block.gpsimd
            def _(pool):
                for b in range(B):
                    cols = slice(b * C * D, (b + 1) * C * D)
                    pool.tensor_tensor(k.tiles(k.fq_all[:, cols], C), k.tiles(k.h_all[:, cols], C),
                                       k.rep(k.gb_all[:, b * D:(b + 1) * D], C), ALU.mult).then_inc(s_gy, 1)
                    pool.wait_ge(s_gy, b + 1)
                    pool.tensor_tensor(k.x_all[:, cols], k.x_all[:, cols], k.fq_all[:, cols], ALU.add).then_inc(s_xy, 1)

            @block.tensor
            def _(pe):
                for t in range(T):
                    last = pe.transpose(k.bank[4][:, t * NE:(t + 1) * NE], k.logits_t[:, t * P:(t + 1) * P],
                                        k.ident[0:NE, 0:NE])
                last.then_inc(s_lg, 1)
                pe.wait_ge(s_oh, 1)
                pe.matmul(k.bank[0][:, 0:T * NE], k.cst[:, C_BEFORE:C_BEFORE + P], flat(oh[:]), start=True, stop=True)
                pe.matmul(k.bank[1][:, 0:T * NE], k.cst[:, C_ONES:C_ONES + P], flat(oh[:]),
                          start=True, stop=True).then_inc(s_pr, 1)
                pe.wait_ge(s_id, 2)
                for t in range(T):
                    if t % PT == 0:
                        pe.wait_ge(s_pm, t // PT + 1)
                    last = pe.matmul(k.bank[2][:, 0:2 * MT], perm[:, t, :], ids[:, t].rearrange("p i j -> p (i j)"),
                                     start=(t == 0), stop=(t == T - 1))
                last.then_inc(s_tk, 1)


R3 = 3
RG = 3 * R3
BEHIND = 6


def run_experts(nc, k):
    with ExitStack() as ctx:
        def sb(name, shape, dt=F32):
            return ctx.enter_context(nc.sbuf_tensor(name, shape, dt))
        def sem(name):
            return ctx.enter_context(nc.semaphore(name))
        xin = [k.v_all[:, i * 3 * D:(i + 1) * 3 * D] for i in range(RG)]
        xt = [sb(f"g_xt{i}", [P, P]) for i in range(R3)]
        w1c = [k.h_all[:, i * HID:(i + 1) * HID] for i in range(R3)]
        hid = [k.fq_all[:, i * HC * P:(i + 1) * HC * P] for i in range(R3)]
        gated = [sb(f"g_gated{i}", [P, D]) for i in range(R3)]
        yo = [sb(f"g_out{i}", [P, D]) for i in range(R3)]
        s_in = [sem(f"g_tile_in{i}") for i in range(RG)]
        s_st = [sem(f"g_tile_stored{i}") for i in range(R3)]
        s_t, s_xt, s_w1, s_up, s_g, s_dn, s_gt, s_yo = (
            sem("g_transposed"), sem("g_xt_ready"), sem("g_w1_ready"), sem("g_up_products"),
            sem("g_hidden_ready"), sem("g_down_products"), sem("g_gated"), sem("g_tile_out"))
        b_up = [k.bank[i] for i in range(R3)]
        b_dn = [k.bank[R3 + i] for i in range(R3)]
        b_t = k.bank[2 * R3]
        HEAD = MT % RG + RG

        def staged(eng, body):
            for j in range(HEAD):
                body(j, j % RG, j // RG)
            with eng.Fori(0, MT // RG - 2) as it:
                for i in range(HEAD, HEAD + RG):
                    body(it * RG + i, i % RG, it + i // RG)
            for j in range(MT - RG, MT):
                body(j, j % RG, j // RG)

        def expert_of(eng, j):
            return eng.value_load(k.expert_i[0:1, bass.ds(j, 1)], min_val=0, max_val=NE - 1)

        with nc.Block() as block:

            @block.gpsimd
            def _(pool):
                out_rows = k.out.rearrange("b l d -> (b l) d")

                def tokens(numbers, j):
                    return bass.IndirectOffsetOnAxis(ap=numbers[:, j:j + 1], axis=0)

                def gather(j):
                    wait(pool, s_yo, j - RG + 1)
                    pool.indirect_dma_start(xin[j % RG], None, k.rows_dram, tokens(k.fetch_u, j),
                                            bounds_check=T * P - 1, oob_is_err=False).then_inc(s_in[j % RG], 16)

                def scatter(j):
                    wait(pool, s_yo, j + 1)
                    pool.indirect_dma_start(out_rows, tokens(k.token_u, j), yo[j % R3][:], None,
                                            bounds_check=T * P - 1, oob_is_err=False).then_inc(s_st[j % R3], 16)

                for j in range(MT + BEHIND):
                    if j < MT:
                        gather(j)
                    if j >= BEHIND:
                        scatter(j - BEHIND)
                for i in range(R3):
                    pool.wait_ge(s_st[i], 16 * (MT // R3))

            @block.tensor
            def _(pe):
                def turn(j, v, w):
                    wait(pe, s_in[v], w * 16 + 16)
                    wait(pe, s_xt, j)
                    pe.transpose(b_t[:, 0:P], xin[v][:, 0:D], k.ident).then_inc(s_t, 1)

                def up(j, v):
                    u = v % R3
                    wait(pe, s_xt, j + 1)
                    wait(pe, s_w1, j + 1)
                    for c in range(HC):
                        last = pe.matmul(b_up[u][:, c * P:(c + 1) * P], w1c[u][:, c * P:(c + 1) * P], xt[u][:],
                                         start=True, stop=True)
                    last.then_inc(s_up, 1)

                def down(j, v):
                    u = v % R3
                    e = expert_of(pe, j)
                    wait(pe, s_g, j + 1)
                    wait(pe, s_gt, j - R3 + 1)
                    for c in range(HC):
                        last = pe.matmul(b_dn[u][:, 0:D], hid[u][:, c * P:(c + 1) * P],
                                         k.w2_all[:, bass.ds(e * HID + c * D, D)], start=(c == 0), stop=(c == HC - 1))
                    last.then_inc(s_dn, 1)

                def body(j, v, w):
                    up(j, v)
                    if not (isinstance(j, int) and j == MT - 1):
                        turn(j + 1, (v + 1) % RG, w + (v + 1) // RG)
                    if not (isinstance(j, int) and j == 0):
                        down(j - 1, (v - 1) % RG)

                turn(0, 0, 0)
                pe.wait_ge(k.s_w, 16 * 2 * NE)
                staged(pe, body)
                down(MT - 1, (MT - 1) % RG)

            @block.vector
            def _(dve):
                def out(j, v, w):
                    u = v % R3
                    wait(dve, s_dn, j + 1)
                    dve.tensor_tensor(gated[u][:], b_dn[u][:, 0:D], xin[v][:, D:2 * D], ALU.mult).then_inc(s_gt, 1)
                    wait(dve, s_gt, j + 1)
                    wait(dve, s_st[u], (w * (RG // R3) + v // R3) * 16)
                    dve.tensor_tensor(yo[u][:], gated[u][:], xin[v][:, 2 * D:3 * D], ALU.add).then_inc(s_yo, 1)

                def weights(j, v):
                    e = expert_of(dve, j)
                    wait(dve, s_up, j - R3 + 1)
                    dve.tensor_copy(w1c[v % R3], k.w1_all[:, bass.ds(e * HID, HID)]).then_inc(s_w1, 1)

                def body(j, v, w):
                    wait(dve, s_t, j + 1)
                    dve.tensor_scalar(xt[v % R3][:], b_t[:, 0:P], k.lnw[:, 2:3], k.lnw[:, 3:4], ALU.mult, ALU.add
                                      ).then_inc(s_xt, 1)
                    if not (isinstance(j, int) and j == MT - 1):
                        weights(j + 1, (v + 1) % RG)
                    if not (isinstance(j, int) and j < 2):
                        out(j - 2, (v - 2) % RG, w - (v < 2))

                dve.wait_ge(k.s_w, 16 * 2 * NE)
                weights(0, 0)
                staged(dve, body)
                for j in (MT - 2, MT - 1):
                    out(j, j % RG, j // RG)

            @block.scalar
            def _(act):
                def body(j, v, w):
                    wait(act, s_up, j + 1)
                    act.activation(hid[v % R3], b_up[v % R3][:], ACT.Gelu_apprx_tanh).then_inc(s_g, 1)

                staged(act, body)


_INS = ['L0_attn_x', 'L0_attn_Wqkv', 'L0_attn_bqkv', 'L0_attn_Wout', 'L0_attn_bout', 'L0_attn_gamma', 'L0_attn_beta',
        'L0_ffn_ln1_w', 'L0_ffn_ln1_b', 'L0_ffn_w_qkv', 'L0_ffn_w_proj', 'L0_ffn_ln2_w', 'L0_ffn_ln2_b',
        'L0_ffn_gate_w', 'L0_ffn_gate_b', 'L0_ffn_w1', 'L0_ffn_w2', 'L0_c', 'L0_wmod']


def constants():
    import numpy as np
    c = np.zeros((P, C_ALL), np.float32)
    p = np.arange(P)[:, None]
    m = np.arange(P)[None, :]
    pos = np.arange(H)[None, :]
    c[:, C_ID:C_ID + P] = p == m
    c[:, C_CAUSAL:C_CAUSAL + P] = p <= m
    slot_position = 2 * GH * (p % S // GH) + GH * (p // 64) + p % S % GH
    c[:, C_HMASK:C_HMASK + H] = slot_position == pos
    c[:, C_BEFORE:C_BEFORE + P] = p < m
    c[:, C_ONES:C_ONES + P] = 1.0
    c[:, C_STARTS:C_STARTS + MT] = P * np.arange(MT)
    c[:, C_INDEX:C_INDEX + P] = m
    c[:, C_FIRST:C_FIRST + NE] = NE - np.arange(NE)
    c[:, C_LEFT:C_LEFT + T] = T - np.arange(T)
    c[:, C_ROW:C_ROW + 1] = p
    return c


def kernel(**inputs):
    import numpy as _np
    import concourse.bacc as _bacc
    from concourse import mybir as _mybir
    from concourse.bass_utils import run_bass_kernel_spmd as _run

    nc = _bacc.Bacc("TRN2", target_bir_lowering=False, num_devices=1)
    arrays, args = {}, []
    for name, a in [(n, inputs[n]) for n in _INS] + [("consts", constants())]:
        a = _np.ascontiguousarray(a)
        arrays[f"in_{name}_dram"] = a
        args.append(nc.dram_tensor(f"in_{name}_dram", a.shape, _mybir.dt.from_np(a.dtype), kind="ExternalInput").ap())
    out = nc.dram_tensor("out_0_dram", (B, L, D), F32, kind="ExternalOutput").ap()
    adaln_kernel(nc, *args, out)
    r = _run(nc, [arrays], core_ids=[0])
    return r.results[0]["out_0_dram"]
```
